# Optimizing a Trainium2 kernel written in Bass

```python
import numpy as np
import jax
import jax.numpy as jnp

def _softmax(x, axis=-1):
    return jax.nn.softmax(x, axis=axis)

def _gelu(x):
    return jax.nn.gelu(x, approximate=True)

def _silu(x):
    return jax.nn.silu(x)

def _sigmoid(x):
    return jax.nn.sigmoid(x)

def _layernorm(x, axis=-1, eps=1e-05):
    m = jnp.mean(x, axis=axis, keepdims=True)
    v = jnp.var(x, axis=axis, keepdims=True)
    return (x - m) / jnp.sqrt(v + eps)

def _scatter_add(tgt, idx, src, axis=0):
    return tgt.at[idx].add(src)

def _segment_sum(src, seg, n):
    return jax.ops.segment_sum(src, seg, n)
kernel_name = 'mk_xattn_ffn_d4_seqx_r8_77b4ba'

def setup_inputs(seed: int=0):
    np.random.seed(seed)
    _w = jnp.asarray

    def _rec_inputs():
        import jax
        import jax.numpy as jnp
        _rk = jax.random.key(seed)
        x = 7.22e-05 + 1 * jax.random.normal(jax.random.fold_in(_rk, 1), (16, 64, 512), jnp.float32)
        _lenS = 64 - jax.random.randint(jax.random.fold_in(_rk, 7), (16,), 0, max(1, 64 // 4) + 1, jnp.int32)
        _lenS2 = 64 - jax.random.randint(jax.random.fold_in(_rk, 8), (16,), 0, max(1, 64 // 4) + 1, jnp.int32)
        _ctx_4096P = jax.random.normal(jax.random.fold_in(_rk, 11), (16, 16, 512), jnp.float32)
        _ctx_4096c = jax.random.dirichlet(jax.random.fold_in(_rk, 511), 0.3 * jnp.ones((16,), jnp.float32), (16, 64))
        _ctx_4096t = jnp.einsum('bsk,bkd->bsd', _ctx_4096c, _ctx_4096P)
        _ctx_4096t = _ctx_4096t * jax.lax.rsqrt(jnp.mean(jnp.square(_ctx_4096t)) + 1e-12) * 0.953939
        ctx_4096 = 4.13588e-05 + 0.999923 * (_ctx_4096t + 0.3 * jax.random.normal(jax.random.fold_in(_rk, 611), (16, 64, 512), jnp.float32))
        _validS = jnp.arange(64)[None, :] < _lenS[:, None]
        _validS2 = jnp.arange(64)[None, :] < _lenS2[:, None]
        _causal = jnp.tril(jnp.ones((64, 64), dtype=bool))
        mask_1x1xSxS2_ff0 = jnp.where(jnp.ones((1, 1, 64, 64), dtype=bool), 0.0, -1000000000.0).astype(jnp.float32)
        return (x, ctx_4096, mask_1x1xSxS2_ff0)
    x, ctx_4096, mask_1x1xSxS2_ff0 = _rec_inputs()

    def _L0_xattn_setup():
        import jax, jax.numpy as jnp
        import numpy as np
        HEADS = 8
        WINDOW = 16

        def _pointwise(W, b, t):
            return jnp.einsum('oc,bct->bot', W, t) + b[None, :, None]
        key = jax.random.key(seed)
        ks = jax.random.split(key, 10)
        B, C, T = (4, 64, 512)
        s = 0.02
        return {'x': jax.random.normal(ks[0], (B, C, T), jnp.float32), 'cond': jax.random.normal(ks[1], (B, C, T), jnp.float32), 'Wq': jax.random.normal(ks[2], (C, C), jnp.float32) * s, 'bq': jnp.zeros((C,), jnp.float32), 'Wk': jax.random.normal(ks[3], (C, C), jnp.float32) * s, 'bk': jnp.zeros((C,), jnp.float32), 'Wv': jax.random.normal(ks[4], (C, C), jnp.float32) * s, 'bv': jnp.zeros((C,), jnp.float32), 'Wo': jax.random.normal(ks[5], (C, C), jnp.float32) * s, 'bo': jnp.zeros((C,), jnp.float32)}
    _L0_xattn_all = _L0_xattn_setup()
    _L0_xattn_in = {k: v for k, v in _L0_xattn_all.items() if k in ('Wq', 'bq', 'Wk', 'bk', 'Wv', 'bv', 'Wo', 'bo')}
    del _L0_xattn_all

    def _L0_ffn_setup():
        import jax, jax.numpy as jnp
        import numpy as np
        ALPHA = 32
        R = 16
        SCALING = ALPHA / R
        key = jax.random.key(seed)
        k1, k2, k3, k4 = jax.random.split(key, 4)
        B_, S, D = (4, 256, 512)
        H, r, O = (8, R, 512)
        x = jax.random.normal(k1, (B_, S, D), dtype=jnp.float32)
        A = jax.random.normal(k2, (H, r, D), dtype=jnp.float32) * 0.02
        Bm = jax.random.normal(k3, (H, O, r), dtype=jnp.float32) * 0.02
        Wr = jax.random.normal(k4, (H, D), dtype=jnp.float32) * 0.02
        br = jnp.zeros((H,), dtype=jnp.float32)
        return {'x': x, 'A': A, 'B': Bm, 'Wr': Wr, 'br': br}
    _L0_ffn_all = _L0_ffn_setup()
    _L0_ffn_in = {k: v for k, v in _L0_ffn_all.items() if k in ('A', 'B', 'Wr', 'br')}
    del _L0_ffn_all

    def _L1_xattn_setup():
        import jax, jax.numpy as jnp
        import numpy as np
        B, Q, D = (8, 64, 512)
        CTX = 512
        H, KV, HD = (16, 4, 96)
        G = H // KV
        key = jax.random.key(seed)
        ks = jax.random.split(key, 6)
        s = 0.02
        return {'latents': jax.random.normal(ks[0], (B, Q, D), jnp.float32), 'context': jax.random.normal(ks[1], (B, CTX, D), jnp.float32), 'Wq': jax.random.normal(ks[2], (H * HD, D), jnp.float32) * s, 'Wk': jax.random.normal(ks[3], (KV * HD, D), jnp.float32) * s, 'Wv': jax.random.normal(ks[4], (KV * HD, D), jnp.float32) * s, 'Wo': jax.random.normal(ks[5], (D, H * HD), jnp.float32) * s}
    _L1_xattn_all = _L1_xattn_setup()
    _L1_xattn_in = {k: v for k, v in _L1_xattn_all.items() if k in ('Wq', 'Wk', 'Wv', 'Wo')}
    del _L1_xattn_all

    def _L1_ffn_setup():
        import jax, jax.numpy as jnp
        import numpy as np
        LORA_R = 16
        SCALE = 16.0 / np.sqrt(16.0)
        NUM_EXPERTS = 4
        TOP_K = 2
        IN_F = 512
        OUT_F = 512
        key = jax.random.key(seed)
        k_x, k_a, k_b, k_r = jax.random.split(key, 4)
        x = jax.random.normal(k_x, (2, 256, IN_F), dtype=jnp.float32)
        A = jax.random.normal(k_a, (NUM_EXPERTS, LORA_R, IN_F), dtype=jnp.float32) * (1.0 / np.sqrt(IN_F))
        B = jax.random.normal(k_b, (NUM_EXPERTS, OUT_F, LORA_R), dtype=jnp.float32) * 0.02
        Wr = jax.random.normal(k_r, (NUM_EXPERTS, IN_F), dtype=jnp.float32) * 0.02
        return {'x': x, 'A': A, 'B': B, 'Wr': Wr}
    _L1_ffn_all = _L1_ffn_setup()
    _L1_ffn_in = {k: v for k, v in _L1_ffn_all.items() if k in ('A', 'B', 'Wr')}
    del _L1_ffn_all

    def _L2_xattn_setup():
        import jax, jax.numpy as jnp
        import numpy as np
        NUM_HEADS = 32
        NUM_KV_HEADS = 8
        HEAD_DIM = 128
        HIDDEN = 512
        EPS = 1e-05

        def rmsnorm(x, w, eps=EPS):
            xf = x.astype(jnp.float32)
            var = jnp.mean(xf * xf, axis=-1, keepdims=True)
            return w * (xf * jax.lax.rsqrt(var + eps)).astype(x.dtype)
        key = jax.random.key(seed)
        ks = jax.random.split(key, 10)
        B, Q, KV = (1, 128, 6404)
        s = 1.0 / np.sqrt(HIDDEN)
        return {'hidden_states': jax.random.normal(ks[0], (B, Q, HIDDEN), jnp.float32), 'cross_attention_states': jax.random.normal(ks[1], (B, KV, HIDDEN), jnp.float32), 'attention_mask': jnp.zeros((B, 1, Q, KV), jnp.float32), 'q_proj_w': jax.random.normal(ks[2], (NUM_HEADS * HEAD_DIM, HIDDEN), jnp.float32) * s, 'k_proj_w': jax.random.normal(ks[3], (NUM_KV_HEADS * HEAD_DIM, HIDDEN), jnp.float32) * s, 'v_proj_w': jax.random.normal(ks[4], (NUM_KV_HEADS * HEAD_DIM, HIDDEN), jnp.float32) * s, 'o_proj_w': jax.random.normal(ks[5], (HIDDEN, NUM_HEADS * HEAD_DIM), jnp.float32) * s, 'q_norm_w': jnp.ones((HEAD_DIM,), jnp.float32), 'k_norm_w': jnp.ones((HEAD_DIM,), jnp.float32)}
    _L2_xattn_all = _L2_xattn_setup()
    _L2_xattn_in = {k: v for k, v in _L2_xattn_all.items() if k in ('q_proj_w', 'k_proj_w', 'v_proj_w', 'o_proj_w', 'q_norm_w', 'k_norm_w')}
    del _L2_xattn_all

    def _L2_ffn_setup():
        import jax, jax.numpy as jnp
        import numpy as np

        def sparsemax(z):
            E = z.shape[-1]
            z_sorted = -jnp.sort(-z, axis=-1)
            z_cum = jnp.cumsum(z_sorted, axis=-1)
            k = jnp.arange(1, E + 1, dtype=z.dtype)
            support = 1.0 + k * z_sorted > z_cum
            k_z = jnp.sum(support, axis=-1, keepdims=True)
            tau_sum = jnp.take_along_axis(z_cum, k_z.astype(jnp.int32) - 1, axis=-1)
            tau = (tau_sum - 1.0) / k_z.astype(z.dtype)
            return jnp.maximum(z - tau, 0.0)
        key = jax.random.key(seed)
        ks = jax.random.split(key, 6)
        B, S, D_IN, D_OUT, E, R = (8, 256, 512, 512, 8, 16)
        x = jax.random.normal(ks[0], (B, S, D_IN), dtype=jnp.float32)
        W_base = jax.random.normal(ks[1], (D_OUT, D_IN), dtype=jnp.float32) * D_IN ** (-0.5)
        b_base = jax.random.normal(ks[2], (D_OUT,), dtype=jnp.float32) * 0.01
        W_router = jax.random.normal(ks[3], (E, D_IN), dtype=jnp.float32) * D_IN ** (-0.5)
        b_router = jnp.zeros((E,), dtype=jnp.float32)
        lora_A = jax.random.normal(ks[4], (E, D_IN, R), dtype=jnp.float32) * D_IN ** (-0.5)
        lora_B = jnp.zeros((E, R, D_OUT), dtype=jnp.float32)
        return {'x': x, 'W_base': W_base, 'b_base': b_base, 'W_router': W_router, 'b_router': b_router, 'lora_A': lora_A, 'lora_B': lora_B}
    _L2_ffn_all = _L2_ffn_setup()
    _L2_ffn_in = {k: v for k, v in _L2_ffn_all.items() if k in ('W_base', 'b_base', 'W_router', 'b_router', 'lora_A', 'lora_B')}
    del _L2_ffn_all

    def _L3_xattn_setup():
        import jax, jax.numpy as jnp
        import numpy as np
        HEADS = 32
        KV_HEADS = 8
        HEAD_DIM = 128
        EPS = 1e-06

        def rms_norm(x, w):
            var = jnp.mean(jnp.square(x.astype(jnp.float32)), axis=-1, keepdims=True)
            return (x.astype(jnp.float32) * jax.lax.rsqrt(var + EPS)).astype(x.dtype) * w
        key = jax.random.key(seed)
        ks = jax.random.split(key, 6)
        bsz, n_lat, seq, hidden = (8, 64, 512, 512)
        return {'latents': jax.random.normal(ks[0], (bsz, n_lat, hidden), jnp.float32), 'context': jax.random.normal(ks[1], (bsz, seq, hidden), jnp.float32), 'Wq': jax.random.normal(ks[2], (hidden, HEADS * HEAD_DIM), jnp.float32) * 0.02, 'Wk': jax.random.normal(ks[3], (hidden, KV_HEADS * HEAD_DIM), jnp.float32) * 0.02, 'Wv': jax.random.normal(ks[4], (hidden, KV_HEADS * HEAD_DIM), jnp.float32) * 0.02, 'Wo': jax.random.normal(ks[5], (HEADS * HEAD_DIM, hidden), jnp.float32) * 0.02, 'q_norm_w': jnp.ones((HEAD_DIM,), jnp.float32), 'k_norm_w': jnp.ones((HEAD_DIM,), jnp.float32)}
    _L3_xattn_all = _L3_xattn_setup()
    _L3_xattn_in = {k: v for k, v in _L3_xattn_all.items() if k in ('Wq', 'Wk', 'Wv', 'Wo', 'q_norm_w', 'k_norm_w')}
    del _L3_xattn_all

    def _L3_ffn_setup():
        import jax, jax.numpy as jnp
        import numpy as np
        GROUP_SIZE = 64
        OUT_FEATURES = 512
        IN_FEATURES = 512
        NUM_GROUPS = IN_FEATURES // GROUP_SIZE

        def _dequantize_4bit(packed, scales, zeros):
            low = (packed & 15).astype(jnp.float32)
            high = (packed >> 4 & 15).astype(jnp.float32)
            g = packed.shape[0]
            unpacked = jnp.stack([low, high], axis=-1).reshape(g, GROUP_SIZE)
            deq = unpacked * scales[:, None] + zeros[:, None]
            return deq.reshape(OUT_FEATURES, IN_FEATURES)
        key = jax.random.key(seed)
        k1, k2, k3, k4, k5 = jax.random.split(key, 5)
        x = jax.random.normal(k1, (4, 256, IN_FEATURES), dtype=jnp.float32)
        weight_packed = jax.random.randint(k2, (OUT_FEATURES * NUM_GROUPS, GROUP_SIZE // 2), 0, 32, dtype=jnp.int32)
        weight_scales = jax.random.uniform(k3, (OUT_FEATURES * NUM_GROUPS,), dtype=jnp.float32) * 0.01 + 0.0001
        weight_zeros = jax.random.normal(k4, (OUT_FEATURES * NUM_GROUPS,), dtype=jnp.float32) * 0.05
        bias = jax.random.normal(k5, (OUT_FEATURES,), dtype=jnp.float32) * 0.02
        return {'x': x, 'weight_packed': weight_packed, 'weight_scales': weight_scales, 'weight_zeros': weight_zeros, 'bias': bias}
    _L3_ffn_all = _L3_ffn_setup()
    _L3_ffn_in = {k: v for k, v in _L3_ffn_all.items() if k in ('weight_packed', 'weight_scales', 'weight_zeros', 'bias')}
    del _L3_ffn_all
    return {'x': x, 'ctx_4096': ctx_4096, 'mask_1x1xSxS2_ff0': mask_1x1xSxS2_ff0, 'L0_xattn_Wq': _L0_xattn_in['Wq'], 'L0_xattn_bq': _L0_xattn_in['bq'], 'L0_xattn_Wk': _L0_xattn_in['Wk'], 'L0_xattn_bk': _L0_xattn_in['bk'], 'L0_xattn_Wv': _L0_xattn_in['Wv'], 'L0_xattn_bv': _L0_xattn_in['bv'], 'L0_xattn_Wo': _L0_xattn_in['Wo'], 'L0_xattn_bo': _L0_xattn_in['bo'], 'L0_ffn_A': _L0_ffn_in['A'], 'L0_ffn_B': _L0_ffn_in['B'], 'L0_ffn_Wr': _L0_ffn_in['Wr'], 'L0_ffn_br': _L0_ffn_in['br'], 'L1_xattn_Wq': _L1_xattn_in['Wq'], 'L1_xattn_Wk': _L1_xattn_in['Wk'], 'L1_xattn_Wv': _L1_xattn_in['Wv'], 'L1_xattn_Wo': _L1_xattn_in['Wo'], 'L1_ffn_A': _L1_ffn_in['A'], 'L1_ffn_B': _L1_ffn_in['B'], 'L1_ffn_Wr': _L1_ffn_in['Wr'], 'L2_xattn_q_proj_w': _L2_xattn_in['q_proj_w'], 'L2_xattn_k_proj_w': _L2_xattn_in['k_proj_w'], 'L2_xattn_v_proj_w': _L2_xattn_in['v_proj_w'], 'L2_xattn_o_proj_w': _L2_xattn_in['o_proj_w'], 'L2_xattn_q_norm_w': _L2_xattn_in['q_norm_w'], 'L2_xattn_k_norm_w': _L2_xattn_in['k_norm_w'], 'L2_ffn_W_base': _L2_ffn_in['W_base'], 'L2_ffn_b_base': _L2_ffn_in['b_base'], 'L2_ffn_W_router': _L2_ffn_in['W_router'], 'L2_ffn_b_router': _L2_ffn_in['b_router'], 'L2_ffn_lora_A': _L2_ffn_in['lora_A'], 'L2_ffn_lora_B': _L2_ffn_in['lora_B'], 'L3_xattn_Wq': _L3_xattn_in['Wq'], 'L3_xattn_Wk': _L3_xattn_in['Wk'], 'L3_xattn_Wv': _L3_xattn_in['Wv'], 'L3_xattn_Wo': _L3_xattn_in['Wo'], 'L3_xattn_q_norm_w': _L3_xattn_in['q_norm_w'], 'L3_xattn_k_norm_w': _L3_xattn_in['k_norm_w'], 'L3_ffn_weight_packed': _L3_ffn_in['weight_packed'], 'L3_ffn_weight_scales': _L3_ffn_in['weight_scales'], 'L3_ffn_weight_zeros': _L3_ffn_in['weight_zeros'], 'L3_ffn_bias': _L3_ffn_in['bias']}

def reference(x, ctx_4096, mask_1x1xSxS2_ff0, L0_xattn_Wq, L0_xattn_bq, L0_xattn_Wk, L0_xattn_bk, L0_xattn_Wv, L0_xattn_bv, L0_xattn_Wo, L0_xattn_bo, L0_ffn_A, L0_ffn_B, L0_ffn_Wr, L0_ffn_br, L1_xattn_Wq, L1_xattn_Wk, L1_xattn_Wv, L1_xattn_Wo, L1_ffn_A, L1_ffn_B, L1_ffn_Wr, L2_xattn_q_proj_w, L2_xattn_k_proj_w, L2_xattn_v_proj_w, L2_xattn_o_proj_w, L2_xattn_q_norm_w, L2_xattn_k_norm_w, L2_ffn_W_base, L2_ffn_b_base, L2_ffn_W_router, L2_ffn_b_router, L2_ffn_lora_A, L2_ffn_lora_B, L3_xattn_Wq, L3_xattn_Wk, L3_xattn_Wv, L3_xattn_Wo, L3_xattn_q_norm_w, L3_xattn_k_norm_w, L3_ffn_weight_packed, L3_ffn_weight_scales, L3_ffn_weight_zeros, L3_ffn_bias):
    import jax
    import jax.numpy as jnp

    def _L0_xattn_ref(x, cond, Wq, bq, Wk, bk, Wv, bv, Wo, bo):
        import jax, jax.numpy as jnp
        import numpy as np
        HEADS = 8
        WINDOW = 16

        def _pointwise(W, b, t):
            return jnp.einsum('oc,bct->bot', W, t) + b[None, :, None]
        B, C, T = x.shape
        H, W = (HEADS, WINDOW)
        hd = C // H
        scale = hd ** (-0.5)
        pad_left = W // 2
        pad_right = W - pad_left - 1
        q = _pointwise(Wq, bq, x)
        k = _pointwise(Wk, bk, cond)
        v = _pointwise(Wv, bv, cond)
        k = jnp.pad(k, ((0, 0), (0, 0), (pad_left, pad_right)))
        v = jnp.pad(v, ((0, 0), (0, 0), (pad_left, pad_right)))
        idx = jnp.arange(T)[:, None] + jnp.arange(W)[None, :]
        k_win = k[:, :, idx].reshape(B, H, hd, T, W)
        v_win = v[:, :, idx].reshape(B, H, hd, T, W)
        qh = q.reshape(B, H, hd, T)
        dots = jnp.einsum('bhdt,bhdtw->bhtw', qh, k_win) * scale
        attn = jax.nn.softmax(dots, axis=-1)
        out = jnp.einsum('bhtw,bhdtw->bhdt', attn, v_win)
        out = out.reshape(B, C, T)
        return _pointwise(Wo, bo, out)

    def _L0_ffn_ref(x, A, B, Wr, br):
        import jax, jax.numpy as jnp
        import numpy as np
        ALPHA = 32
        R = 16
        SCALING = ALPHA / R
        H = A.shape[0]
        router_logits = jnp.einsum('bsd,hd->bsh', x, Wr) + br
        scores = H * jax.nn.softmax(router_logits, axis=-1)
        low = jnp.einsum('bsd,hrd->bshr', x, A)
        out = jnp.einsum('bshr,hor,bsh->bso', low, B, scores)
        return SCALING * out

    def _L1_xattn_ref(latents, context, Wq, Wk, Wv, Wo):
        import jax, jax.numpy as jnp
        import numpy as np
        B, Q, D = (8, 64, 512)
        CTX = 512
        H, KV, HD = (16, 4, 96)
        G = H // KV
        b, q_len, _ = latents.shape
        hidden = jnp.concatenate([context, latents], axis=1)
        s_len = hidden.shape[1]
        q = (latents @ Wq.T).reshape(b, q_len, H, HD)
        k = (hidden @ Wk.T).reshape(b, s_len, KV, HD)
        v = (hidden @ Wv.T).reshape(b, s_len, KV, HD)
        q = q.transpose(0, 2, 1, 3).reshape(b, KV, G, q_len, HD)
        k = k.transpose(0, 2, 1, 3)
        v = v.transpose(0, 2, 1, 3)
        scale = 1.0 / jnp.sqrt(jnp.asarray(HD, q.dtype))
        scores = jnp.einsum('bkgqd,bksd->bkgqs', q, k) * scale
        attn = jax.nn.softmax(scores.astype(jnp.float32), axis=-1).astype(q.dtype)
        out = jnp.einsum('bkgqs,bksd->bkgqd', attn, v)
        out = out.reshape(b, H, q_len, HD).transpose(0, 2, 1, 3).reshape(b, q_len, H * HD)
        return out @ Wo.T

    def _L1_ffn_ref(x, A, B, Wr):
        import jax, jax.numpy as jnp
        import numpy as np
        LORA_R = 16
        SCALE = 16.0 / np.sqrt(16.0)
        NUM_EXPERTS = 4
        TOP_K = 2
        IN_F = 512
        OUT_F = 512
        orig_shape = x.shape
        flat = x.reshape(-1, orig_shape[-1])
        logits = flat @ Wr.T
        topk_vals, topk_idx = jax.lax.top_k(logits, TOP_K)
        T = flat.shape[0]
        neg_inf = jnp.finfo(logits.dtype).min
        sparse = jnp.full_like(logits, neg_inf)
        rows = jnp.arange(T)[:, None]
        sparse = sparse.at[rows, topk_idx].set(topk_vals)
        gates = jax.nn.softmax(sparse, axis=-1)
        mid = jnp.einsum('tf,erf->ter', flat, A)
        all_deltas = jnp.einsum('ter,eor->teo', mid, B) * SCALE
        delta = jnp.sum(gates[:, :, None] * all_deltas, axis=1)
        return delta.reshape(*orig_shape[:-1], -1)

    def _L2_xattn_ref(hidden_states, cross_attention_states, attention_mask, q_proj_w, k_proj_w, v_proj_w, o_proj_w, q_norm_w, k_norm_w):
        import jax, jax.numpy as jnp
        import numpy as np
        NUM_HEADS = 32
        NUM_KV_HEADS = 8
        HEAD_DIM = 128
        HIDDEN = 512
        EPS = 1e-05

        def rmsnorm(x, w, eps=EPS):
            xf = x.astype(jnp.float32)
            var = jnp.mean(xf * xf, axis=-1, keepdims=True)
            return w * (xf * jax.lax.rsqrt(var + eps)).astype(x.dtype)
        B, Q, _ = hidden_states.shape
        KV = cross_attention_states.shape[1]
        n_rep = NUM_HEADS // NUM_KV_HEADS
        q = (hidden_states @ q_proj_w.T).reshape(B, Q, NUM_HEADS, HEAD_DIM).transpose(0, 2, 1, 3)
        k = (cross_attention_states @ k_proj_w.T).reshape(B, KV, NUM_KV_HEADS, HEAD_DIM).transpose(0, 2, 1, 3)
        v = (cross_attention_states @ v_proj_w.T).reshape(B, KV, NUM_KV_HEADS, HEAD_DIM).transpose(0, 2, 1, 3)
        q = rmsnorm(q, q_norm_w)
        k = jnp.repeat(k, n_rep, axis=1)
        v = jnp.repeat(v, n_rep, axis=1)
        k = rmsnorm(k, k_norm_w)
        scale = 1.0 / np.sqrt(HEAD_DIM)
        scores = jnp.einsum('bhqd,bhkd->bhqk', q, k) * scale + attention_mask
        attn = jax.nn.softmax(scores.astype(jnp.float32), axis=-1).astype(q.dtype)
        out = jnp.einsum('bhqk,bhkd->bhqd', attn, v)
        out = out.transpose(0, 2, 1, 3).reshape(B, Q, NUM_HEADS * HEAD_DIM)
        return out @ o_proj_w.T

    def _L2_ffn_ref(x, W_base, b_base, W_router, b_router, lora_A, lora_B):
        import jax, jax.numpy as jnp
        import numpy as np

        def sparsemax(z):
            E = z.shape[-1]
            z_sorted = -jnp.sort(-z, axis=-1)
            z_cum = jnp.cumsum(z_sorted, axis=-1)
            k = jnp.arange(1, E + 1, dtype=z.dtype)
            support = 1.0 + k * z_sorted > z_cum
            k_z = jnp.sum(support, axis=-1, keepdims=True)
            tau_sum = jnp.take_along_axis(z_cum, k_z.astype(jnp.int32) - 1, axis=-1)
            tau = (tau_sum - 1.0) / k_z.astype(z.dtype)
            return jnp.maximum(z - tau, 0.0)
        base_out = jnp.einsum('bsd,od->bso', x, W_base) + b_base
        logits = jnp.einsum('bsd,ed->bse', x, W_router) + b_router
        weights = sparsemax(logits)
        h = jnp.einsum('bsd,edr->bser', x, lora_A)
        expert_out = jnp.einsum('bser,bse,ero->bso', h, weights, lora_B)
        return base_out + expert_out

    def _L3_xattn_ref(latents, context, Wq, Wk, Wv, Wo, q_norm_w, k_norm_w):
        import jax, jax.numpy as jnp
        import numpy as np
        HEADS = 32
        KV_HEADS = 8
        HEAD_DIM = 128
        EPS = 1e-06

        def rms_norm(x, w):
            var = jnp.mean(jnp.square(x.astype(jnp.float32)), axis=-1, keepdims=True)
            return (x.astype(jnp.float32) * jax.lax.rsqrt(var + EPS)).astype(x.dtype) * w
        bsz, q_len, hidden = latents.shape
        kv = jnp.concatenate([context, latents], axis=1)
        kv_len = kv.shape[1]
        groups = HEADS // KV_HEADS
        q = (latents @ Wq).reshape(bsz, q_len, HEADS, HEAD_DIM).transpose(0, 2, 1, 3)
        k = (kv @ Wk).reshape(bsz, kv_len, KV_HEADS, HEAD_DIM).transpose(0, 2, 1, 3)
        v = (kv @ Wv).reshape(bsz, kv_len, KV_HEADS, HEAD_DIM).transpose(0, 2, 1, 3)
        q = rms_norm(q, q_norm_w)
        k = rms_norm(k, k_norm_w)
        qg = q.reshape(bsz, KV_HEADS, groups, q_len, HEAD_DIM)
        scale = 1.0 / np.sqrt(HEAD_DIM)
        scores = jnp.einsum('bhgqd,bhkd->bhgqk', qg, k) * scale
        probs = jax.nn.softmax(scores.astype(jnp.float32), axis=-1).astype(q.dtype)
        out = jnp.einsum('bhgqk,bhkd->bhgqd', probs, v)
        out = out.reshape(bsz, HEADS, q_len, HEAD_DIM).transpose(0, 2, 1, 3)
        out = out.reshape(bsz, q_len, HEADS * HEAD_DIM)
        return out @ Wo

    def _L3_ffn_ref(x, weight_packed, weight_scales, weight_zeros, bias):
        import jax, jax.numpy as jnp
        import numpy as np
        GROUP_SIZE = 64
        OUT_FEATURES = 512
        IN_FEATURES = 512
        NUM_GROUPS = IN_FEATURES // GROUP_SIZE

        def _dequantize_4bit(packed, scales, zeros):
            low = (packed & 15).astype(jnp.float32)
            high = (packed >> 4 & 15).astype(jnp.float32)
            g = packed.shape[0]
            unpacked = jnp.stack([low, high], axis=-1).reshape(g, GROUP_SIZE)
            deq = unpacked * scales[:, None] + zeros[:, None]
            return deq.reshape(OUT_FEATURES, IN_FEATURES)
        weight = _dequantize_4bit(weight_packed, weight_scales, weight_zeros)
        out = jnp.einsum('bsi,oi->bso', x, weight) + bias
        return out
    x = x + _L0_xattn_ref(_layernorm(x, axis=-1), ctx_4096, L0_xattn_Wq, L0_xattn_bq, L0_xattn_Wk, L0_xattn_bk, L0_xattn_Wv, L0_xattn_bv, L0_xattn_Wo, L0_xattn_bo)
    x = x + _L0_ffn_ref(_layernorm(x, axis=-1), L0_ffn_A, L0_ffn_B, L0_ffn_Wr, L0_ffn_br)
    x = x + _L1_xattn_ref(_layernorm(x, axis=-1), ctx_4096, L1_xattn_Wq, L1_xattn_Wk, L1_xattn_Wv, L1_xattn_Wo)
    x = x + _L1_ffn_ref(_layernorm(x, axis=-1), L1_ffn_A, L1_ffn_B, L1_ffn_Wr)
    x = x + _L2_xattn_ref(_layernorm(x, axis=-1), ctx_4096, mask_1x1xSxS2_ff0, L2_xattn_q_proj_w, L2_xattn_k_proj_w, L2_xattn_v_proj_w, L2_xattn_o_proj_w, L2_xattn_q_norm_w, L2_xattn_k_norm_w)
    x = x + _L2_ffn_ref(_layernorm(x, axis=-1), L2_ffn_W_base, L2_ffn_b_base, L2_ffn_W_router, L2_ffn_b_router, L2_ffn_lora_A, L2_ffn_lora_B)
    x = x + _L3_xattn_ref(_layernorm(x, axis=-1), ctx_4096, L3_xattn_Wq, L3_xattn_Wk, L3_xattn_Wv, L3_xattn_Wo, L3_xattn_q_norm_w, L3_xattn_k_norm_w)
    x = x + _L3_ffn_ref(_layernorm(x, axis=-1), L3_ffn_weight_packed, L3_ffn_weight_scales, L3_ffn_weight_zeros, L3_ffn_bias)
    return x

_drawn_inputs = setup_inputs


def setup_inputs(seed=0):
    import zlib

    import numpy as np

    out = dict(_drawn_inputs(seed))
    spreads = {'L0_xattn_bq': (0.0, 0.8),
     'L0_xattn_bk': (0.0, 0.8),
     'L0_xattn_bv': (0.0, 0.8),
     'L0_xattn_bo': (0.0, 0.1),
     'L0_ffn_br': (0.0, 0.1),
     'L2_xattn_q_norm_w': (1.0, 0.2),
     'L2_xattn_k_norm_w': (1.0, 0.2),
     'L2_ffn_b_router': (0.0, 0.541),
     'L2_ffn_lora_B': (0.0, 0.1),
     'L3_xattn_q_norm_w': (1.0, 0.6),
     'L3_xattn_k_norm_w': (1.0, 0.6)}
    factors = {'L0_xattn_Wq': 8.0,
     'L0_xattn_Wk': 8.0,
     'L0_xattn_Wv': 5.195,
     'L0_xattn_Wo': 4.188,
     'L1_xattn_Wq': 5.941,
     'L1_xattn_Wk': 4.257,
     'L2_ffn_b_base': 8.0,
     'L3_ffn_bias': 7.42}
    for name, (base, spread) in spreads.items():
        noise = np.random.default_rng([zlib.crc32(name.encode()), seed]).standard_normal(out[name].shape)
        drawn = base * np.exp(spread * noise) if base else spread * noise
        out[name] = jnp.asarray(drawn.astype(out[name].dtype))
    for name, factor in factors.items():
        out[name] = (out[name] * factor).astype(out[name].dtype)
    return out
```

```python
from contextlib import ExitStack

import numpy as np

import concourse.bass as bass
from concourse import mybir

ALU = mybir.AluOpType
ACT = mybir.ActivationFunctionType
AX = mybir.AxisListType
F32 = mybir.dt.float32
F32R = mybir.dt.float32r
I32 = mybir.dt.int32

P = 128
D = 512
KD = D // P
B, S = 16, 64
T = B * S // P
HG = 4
NB = 2
W0 = 16
H0 = 8
PAD0 = W0 // 2
KW = D + W0
LNEPS = 1e-5
START = 4
QC = 4 * P + 2 * P
CHUNKS = 6
STG = 1024


class Attention:

    def __init__(self, groups, d, tiles, norm_eps, masked, slot0, n0, c0):
        self.groups, self.d, self.tiles, self.norm_eps, self.masked = groups, d, tiles, norm_eps, masked
        self.slot0, self.n0, self.c0 = slot0, n0, c0
        self.keys = S * tiles
        self.scale = float(d) ** -0.5
        self.steps = groups * T
        self.end = n0 + self.steps
        self.cols = HG * d + 2 * d


class Experts:

    def __init__(self, experts, rank, dense, slot, c0):
        self.e, self.r, self.dense, self.slot, self.c0 = experts, rank, dense, slot, c0
        self.er = experts * rank
        self.cols = self.er + experts


def build(nc, a):
    L1 = Attention(4, 96, 2, None, False, 1, START, 8)
    L2 = Attention(8, 128, 1, 1e-5, True, 0, L1.end, L1.c0 + CHUNKS * 4 + 4)
    L3 = Attention(8, 128, 2, 1e-6, False, 1, L2.end, L2.c0 + CHUNKS * 8 + 4)
    F0 = Experts(8, 16, False, 0, 0)
    F1 = Experts(4, 16, False, 1, L1.c0 + CHUNKS * 4)
    F2 = Experts(8, 16, True, 0, L2.c0 + CHUNKS * 8)
    CTX_C0 = 4
    NORM0 = L1.steps

    with ExitStack() as ctx:
        used = nc.sbuf_usable_end - nc.sbuf_bytes_remaining

        def at(name, shape, dt, offset):
            n = int(np.prod(shape[1:])) * 4
            return nc.alloc_sbuf_tensor_at(name, shape, dt, offset=offset), offset + (n + 31) // 32 * 32

        base = (used + 31) // 32 * 32
        X, o = at("x", [P, T, D], F32, base)
        HTh, o_e = at("hT_hi", [P, KD, B, S, 2], F32R, o)
        HTl, o = at("hT_lo", [P, KD, B, S, 2], F32R, o_e)
        w_at = o
        WQh = [None, None]; WQl = [None, None]; WOh = [None, None]; WOl = [None, None]
        for s in range(2):
            WQh[s], o = at(f"wqkv_hi{s}", [P, KD, QC], F32R, o)
            WQl[s], o = at(f"wqkv_lo{s}", [P, KD, QC], F32R, o)
            WOh[s], o = at(f"wo_hi{s}", [P, HG, D], F32R, o)
            WOl[s], o = at(f"wo_lo{s}", [P, HG, D], F32R, o)
        w_end = o
        stage = [None, None]
        for s in range(2):
            stage[s], o = at(f"stage{s}", [P, STG], F32, o)
        ident, o = at("ident", [P, P], F32, o)
        mask, o = at("mask", [P, S], F32, o)
        knorm, o = at("knorm", [P, 4], F32, o)
        kw, o = at("kw", [P, 2], F32, o)
        mhalf, o = at("mhalf", [P, 8], F32, o)
        st, o = at("ln_stats", [P, T, 6], F32, o)
        mv, o = at("ln_mean_var", [P, T, 2], F32, o)
        ve, o = at("ln_var_eps", [P, T], F32, o)
        rstd, o = at("ln_rstd", [P, T], F32, o)
        work = o
        qkh = [None, None]; vh = [None] * 4; vl = [None] * 4
        sq, o = at("squares", [P, QC], F32, work)
        ss, o = at("sumsq", [P, 8], F32, o)
        ms, o = at("meansq", [P, 8], F32, o)
        rs, o = at("rnorm", [P, 8], F32, o)
        for s in range(2):
            qkh[s], o = at(f"qk_hat{s}", [P, QC], F32, o)
        qT, o = at("qT", [P, HG * P], F32, o)
        kT, o = at("kT", [P, 2 * P], F32, o)
        for s in range(4):
            vh[s], o = at(f"v_hi{s}", [P, 2 * P], F32R, o)
            vl[s], o = at(f"v_lo{s}", [P, 2 * P], F32R, o)
        sc, o = at("scores", [P, 4 * P], F32, o)
        smx, o = at("score_max", [P, 4], F32, o)
        ssum, o = at("score_sum", [P, 4], F32, o)
        srec, o = at("score_rec", [P, 4], F32, o)
        pTh, o = at("pT_hi", [P, 4 * P], F32R, o)
        pTl, o = at("pT_lo", [P, 4 * P], F32R, o)
        oTh, o = at("oT_hi", [P, 4 * P], F32R, o)
        oTl, o = at("oT_lo", [P, 4 * P], F32R, o)
        assert o <= nc.sbuf_usable_end, o - nc.sbuf_usable_end
        xn = [None, None]
        for s in range(2):
            xn[s], o = at(f"xn{s}", [P, D], F32, work if s == 0 else o)
        lr, o = at("low_logits", [P, T, 136], F32, o)
        gated, o = at("gated", [P, T, P], F32, o)
        gT, o = at("gatedT", [P, T, P], F32, o)
        Bf, o = at("expert_out", [P, D], F32, o)
        bias, o = at("bias_rows", [P, D], F32, o)
        rb, o = at("router_bias", [P, 8], F32, o)
        z, o = at("z", [P, T, 8], F32, o)
        z2, o = at("z2", [P, T, 8], F32, o)
        z3, o = at("z3", [P, T, 8], F32, o)
        zr, o = at("zr", [P, T], F32, o)
        zs, o = at("zs", [P, T], F32, o)
        zt, o = at("zt", [P, T], F32, o)
        pair, o = at("pairs", [P, T, 8, 8], F32, o)
        pair2, o = at("pairs2", [P, T, 4, 4], F32, o)
        tri, o = at("tri", [P, 16], F32, o)
        gates, o = at("gates", [P, T, 8], F32, o)
        assert o <= nc.sbuf_usable_end
        packed, o = at("packed", [P, 4, 256], I32, w_at)
        low4, o = at("low4", [P, 4, 256], I32, o)
        high4, o = at("high4", [P, 4, 256], I32, o)
        wdq, o = at("w_dequant", [P, 4, 8, 32, 2], F32, o)
        wsc, o = at("w_scales", [P, 4, 8], F32, o)
        wze, o = at("w_zeros", [P, 4, 8], F32, o)
        dots, o = at("dots", [P, W0, D], F32, w_at)
        ctxn, _ = at("ctxn", [P, T, D], F32, w_at)
        K0, o = at("k_padded", [P, T, KW], F32, o)
        V0, o = at("v_padded", [P, T, KW], F32, o)
        E0, o = at("head_sum", [P, T, P], F32, o)
        ETr, o = at("head_spread", [P, T, P], F32R, o)
        w0, o = at("w_l0", [P, 4, P], F32, o)
        b0, o = at("b_l0", [P, 4], F32, o)
        assert o <= w_end
        q0, o = at("q_l0", [P, T, D], F32, work + 4096)
        prod = [None] * 4
        for s in range(4):
            prod[s], o = at(f"prod{s}", [P, D], F32, o)
        psumd = [None, None]
        mx0, o = at("max_l0", [P, D], F32, o)
        sum0, o = at("sum_l0", [P, D], F32, o)
        assert o <= nc.sbuf_usable_end
        ETs, _ = at("head_spread_in", [P, T, P], F32, work + 4096 + 4 * D * T)
        o = work + 4096
        for s in range(2):
            psumd[s], o = at(f"prod_pair{s}", [P, D], F32, o)
        rech, o = at("rec_hi", [P, D], F32R, o)
        recl, o = at("rec_lo", [P, D], F32R, o)
        rspread, o = at("rec_spread", [P, D], F32, o)
        o0, o = at("o_l0", [P, D], F32, o)
        eh = HTh.ap().rearrange("p k b j s -> p (k b j s)").rearrange("p (w t) -> p w t", w=W0)
        el = HTl.ap().rearrange("p k b j s -> p (k b j s)").rearrange("p (w t) -> p w t", w=W0)

        ps = {}
        for name in ("q", "kv", "qT", "kT", "s", "pT", "oT", "y"):
            ps[name] = ctx.enter_context(nc.psum_tensor("ps_" + name, [P, 512], F32))

        sems = {}

        def sem(name):
            if name not in sems:
                sems[name] = ctx.enter_context(nc.semaphore(name))
            return sems[name]

        STEP = {
            "pe": ["kv_mm", "q_mm", "qkT_mm", "s_mm", "pT_mm", "av_mm", "y_mm"],
            "act": ["v_hi", "qT_ev", "exp", "pT_hi", "oT_hi", "squared"],
            "dve": ["v_lo", "hat", "hat_k", "kT_ev", "smax", "ssub", "ssum", "srec", "prob", "pT_lo", "oT_lo", "x_add", "sumsq", "meansq"],
            "pool": ["rnorm"],
        }
        block = ctx.enter_context(nc.Block())

        def prime(eng, who):
            for name in STEP[who]:
                eng.sem_inc(sem(name), START)

        def tile_of(H, k, t, s):
            return H[:, k, 2 * t:2 * t + 2, :, s].rearrange("p b j -> p (b j)")

        def row(t3, i):
            return t3[:, bass.ds(i, 1), :].rearrange("p a b -> p (a b)")

        @block.sync
        def _(sp):
            sp.dma_start(X[:, :, :], a["x"].rearrange("(t p) d -> p t d", p=P)).then_inc(sem("x_in"), 16)
            sp.dma_start(ident[:, :], a["ident"]).then_inc(sem("small_in"), 16)
            sp.dma_start(mask[0:S, :], a["mask"]).then_inc(sem("small_in"), 16)
            sp.dma_start(mask[S:P, :], a["mask"]).then_inc(sem("small_in"), 16)
            sp.dma_start(knorm[:, :], a["knorm"]).then_inc(sem("small_in"), 16)
            sp.dma_start(w0[:, :, :], a["w0"]).then_inc(sem("small_in"), 16)
            sp.dma_start(b0[:, :], a["b0"]).then_inc(sem("small_in"), 16)
            sp.dma_start(ctxn[:, :, :], a["ctx"].rearrange("(t p) d -> p t d", p=P)).then_inc(sem("ctx_in"), 16)
            sp.dma_start(E0[:, :, :], a["head_sum"]).then_inc(sem("e_in"), 16)
            sp.dma_start(ETs[:, :, :], a["head_spread"]).then_inc(sem("e_in"), 16)

            def load(c, k, src):
                if not isinstance(k, int) or k >= 2:
                    sp.wait_ge(sem("w_lo"), k - 1)
                rows, n = src.shape[0], src.shape[1]
                sp.dma_start(stage[c % 2][0:rows, 0:n], src).then_inc(sem(f"stage{c % 2}"), 16)

            def load_experts(f, src):
                for c in range(KD):
                    load(c, f.c0 + c, src[c])

            def load_group(l, g, name):
                for c in range(KD):
                    load(c, l.c0 + g * CHUNKS + c, a[name + "_qkv"][bass.ds(g, 1), c].rearrange("o p n -> (o p) n"))
                for c in range(2):
                    load(c, l.c0 + g * CHUNKS + KD + c,
                         a[name + "_o"][bass.ds(g, 1), c].rearrange("o p n -> (o p) n"))

            load_experts(F0, a["f0_ar"])
            sp.wait_ge(sem("x_l0"), T)
            sp.dma_start(Bf[:, :], a["f0_b"]).then_inc(sem("ff_in"), 16)
            sp.dma_start(rb[:, :], a["f0_rb"].partition_broadcast(P)).then_inc(sem("ff_in"), 16)
            for c in range(KD):
                load(c, CTX_C0 + c, a["ctxT"][c])
            with sp.Fori(0, L1.groups) as g:
                load_group(L1, g, "l1")
            load_experts(F1, a["f1_ar"])
            sp.wait_ge(sem("x_add"), L1.end)
            sp.dma_start(Bf[0:F1.er, :], a["f1_b"]).then_inc(sem("ff_in"), 16)
            sp.dma_start(tri[:, :], a["tri"].partition_broadcast(P)).then_inc(sem("ff_in"), 16)
            with sp.Fori(0, L2.groups) as g:
                load_group(L2, g, "l2")
            load_experts(F2, a["f2_ar"])
            sp.wait_ge(sem("x_add"), L2.end)
            sp.dma_start(Bf[:, :], a["f2_b"]).then_inc(sem("ff_in"), 16)
            sp.dma_start(rb[:, :], a["f2_rb"].partition_broadcast(P)).then_inc(sem("ff_in"), 16)
            sp.dma_start(bias[:, :], a["f2_bias"].partition_broadcast(P)).then_inc(sem("ff_in"), 16)
            with sp.Fori(0, L3.groups) as g:
                load_group(L3, g, "l3")
            sp.wait_ge(sem("x_add"), L3.end)
            sp.dma_start(bias[:, :], a["f3_bias"].partition_broadcast(P)).then_inc(sem("ff_in"), 16)
            sp.dma_start(packed[:, :, :], a["packed"].rearrange("(t p) c -> p t c", p=P)).then_inc(sem("pk_in"), 16)
            sp.dma_start(wsc[:, :, :], a["scales"].rearrange("(t p) g -> p t g", p=P)).then_inc(sem("pk_in"), 16)
            sp.dma_start(wze[:, :, :], a["zeros"].rearrange("(t p) g -> p t g", p=P)).then_inc(sem("pk_in"), 16)
            for t in range(T):
                sp.wait_ge(sem("dense_add"), T + t + 1)
                sp.dma_start(a["out"][t * P:(t + 1) * P, :], X[:, t, :]).then_inc(sem("out"), 16)
            sp.wait_ge(sem("out"), 16 * T)

        @block.tensor
        def _(pe):
            prime(pe, "pe")
            pe.sem_inc(sem("dot_mm"), 4)
            pe.sem_inc(sem("pairsum_mm"), 2)

            def passes(out, groups):
                n = len(groups)
                for k, (sh, sl, mh, ml) in enumerate(groups):
                    pe.matmul(out, sh, mh, start=(k == 0), stop=False)
                    pe.matmul(out, sh, ml, start=False, stop=False)
                    last = pe.matmul(out, sl, mh, start=False, stop=(k == n - 1))
                return last

            def norm_transposes(phase):
                for t in range(T):
                    pe.wait_ge(sem("ln_xn"), phase * T + t + 1)
                    if t >= 2:
                        pe.wait_ge(sem("ln_lo"), (phase - 1) * T + t - 1)
                    bank = ps["q" if t % 2 == 0 else "kv"]
                    for k in range(KD):
                        last = pe.transpose(bank[:, k * P:(k + 1) * P], xn[t % 2][:, k * P:(k + 1) * P], ident[:, :])
                    last.then_inc(sem("ln_T"), 1)

            def windowed_attention():
                pe.wait_ge(sem("small_in"), 96)
                pe.wait_ge(sem("ctx_in"), 16)
                for t in range(T):
                    pe.wait_ge(sem("ln_xn"), t + 1)
                    if t >= 2:
                        pe.wait_ge(sem("l0_ev"), 3 * (t - 1))
                    for j, (src, even, odd) in enumerate(((xn[t % 2][:, :], "q", "qT"), (ctxn[:, t, :], "kv", "kT"),
                                                          (ctxn[:, t, :], "s", "pT"))):
                        pe.matmul(ps[odd if t % 2 else even][:, :], w0[:, j, :], src,
                                  start=True, stop=True).then_inc(sem("l0_mm"), 1)
                pe.wait_ge(sem("e_in"), 32)
                with pe.Fori(0, W0 // 2) as i:
                    for h in range(2):
                        bank = ps[("y", "oT")[h]]
                        pe.wait_ge(sem("dots_ev"), i * 2 + h + 1)
                        for t in range(T):
                            j = i * 16 + h * 8 + t
                            pe.wait_ge(sem("prod"), j + 1)
                            pe.matmul(bank[:, :], E0[:, t, :], prod[t % 4][:, :],
                                      start=(t == 0), stop=(t == T - 1)).then_inc(sem("dot_mm"), 1)
                pe.wait_ge(sem("e_lo"), W0)
                pe.wait_ge(sem("dots_ev"), W0 + 2)
                pe.wait_ge(sem("et_cast"), 1)
                banks = ("q", "kv", "qT", "kT")
                for t in range(T):
                    obank = ps[("s", "pT")[t % 2]]

                    def spread(i, u):
                        j = t * W0 + i * 4 + u
                        pe.wait_ge(sem("pv"), j + 1)
                        pe.matmul(ps[banks[u]][:, :], ETr[:, t, :], row(eh, i * 4 + u), start=True, stop=False)
                        pe.matmul(ps[banks[u]][:, :], ETr[:, t, :], row(el, i * 4 + u), start=False,
                                  stop=True).then_inc(sem("spread_mm"), 1)

                    def pairsum(k, slot, first=False, last=False):
                        pe.wait_ge(sem("pair"), k + 3)
                        pe.matmul(obank[:, :], ident[:, :], psumd[slot][:, :], start=first, stop=last,
                                  skip_group_check=True).then_inc(sem("pairsum_mm"), 1)

                    if t >= 2:
                        pe.wait_ge(sem("o_l0"), t - 1)
                    k0 = t * W0 // 2
                    for u in range(4):
                        spread(0, u)
                    pairsum(k0, 0, first=True)
                    with pe.Fori(1, W0 // 4) as i:
                        spread(i, 0)
                        spread(i, 1)
                        pairsum(i * 2 + (k0 - 1), 1)
                        spread(i, 2)
                        spread(i, 3)
                        pairsum(i * 2 + k0, 0)
                    if t == 0:
                        pe.wait_ge(sem("rec_lo"), 1)
                    if t >= 1:
                        pe.wait_ge(sem("o_l0"), t)
                        pe.wait_ge(sem("rspread_ev"), t)
                    pe.matmul(ps["y"][:, :], ETr[:, t, :], rech[:, :], start=True, stop=False)
                    pe.matmul(ps["y"][:, :], ETr[:, t, :], recl[:, :], start=False, stop=True).then_inc(sem("rspread_mm"), 1)
                    pairsum(k0 + 7, 1, last=True)
                    pe.wait_ge(sem("o_l0"), t + 1)
                    if t >= 1:
                        pe.wait_ge(sem("x_l0"), t)
                    pe.matmul(ps["oT"][:, :], w0[:, 3, :], o0[:, :], start=True, stop=True).then_inc(sem("y_l0"), 1)

            def experts(f, phase, index):
                xf = index * T
                for t in range(T):
                    pe.wait_ge(sem("ln_lo"), phase * T + t + 1 - T)
                    if f is None:
                        if t == 0:
                            pe.wait_ge(sem("wdq_lo"), KD)
                        wh, wl, cols = WQh[1], WQl[1], 0
                    else:
                        if t == 0:
                            pe.wait_ge(sem("w_lo"), f.c0 + KD)
                        wh, wl, cols = WQh[f.slot], WQl[f.slot], f.cols
                    off = D if f is None or f.dense else 0
                    st_h = [tile_of(HTh, k, t, 1) for k in range(KD)]
                    st_l = [tile_of(HTl, k, t, 1) for k in range(KD)]
                    if cols:
                        if t >= 2:
                            pe.wait_ge(sem("lr_ev"), index * T + t - 1)
                        passes(ps[("s", "pT")[t % 2]][:, 0:cols],
                               [(st_h[k], st_l[k], wh[:, k, off:off + cols], wl[:, k, off:off + cols])
                                for k in range(KD)]).then_inc(sem("lr_mm"), 1)
                    if off:
                        n = (0 if f is not None else T)
                        if t >= 2:
                            pe.wait_ge(sem("dense_add"), n + t - 1)
                        passes(ps[("oT", "y")[t % 2]][:, :],
                               [(st_h[k], st_l[k], wh[:, k, 0:D], wl[:, k, 0:D])
                                for k in range(KD)]).then_inc(sem("dense_mm"), 1)
                if f is None:
                    return
                pe.wait_ge(sem("gated"), index + 1)
                for t in range(T):
                    last = pe.transpose(ps[("qT", "kT")[t // 4]][0:f.er, t % 4 * P:t % 4 * P + P],
                                        gated[:, t, 0:f.er], ident[:, :])
                    if t % 4 == 3:
                        last.then_inc(sem("gT_mm"), 1)
                pe.wait_ge(sem("ff_in"), FF_IN[index])
                if f.dense:
                    pe.wait_ge(sem("dense_add"), T)
                for t in range(T):
                    pe.wait_ge(sem("gT_ev"), 2 * index + 1 + t // 4)
                    if t >= 2:
                        pe.wait_ge(sem("x_ff"), xf + t - 1)
                    pe.matmul(ps[("oT", "y")[t % 2]][:, :], gT[0:f.er, t, :], Bf[0:f.er, :],
                              start=True, stop=True).then_inc(sem("ff_mm"), 1)

            def attention(l, phase):
                d, cols = l.d, l.cols

                def project(n, t, slot, g):
                    if t == 0:
                        pe.wait_ge(sem("w_lo"), g * CHUNKS + (l.c0 + KD))
                    pe.wait_ge(sem("ln_lo"), (phase - 1) * T + t + 1)
                    pe.wait_ge(sem("v_lo"), n)
                    pe.wait_ge(sem("hat_k"), n)
                    for j in range(l.tiles):
                        if l.tiles == 2:
                            st_ = lambda H, k: H[:, k, 2 * t + j, :, :].rearrange("p j s -> p (j s)")
                        else:
                            st_ = lambda H, k: tile_of(H, k, t, 0)
                        last = passes(ps["kv"][:, j * 2 * d:(j + 1) * 2 * d],
                                      [(st_(HTh, k), st_(HTl, k), WQh[slot][:, k, HG * d:cols],
                                        WQl[slot][:, k, HG * d:cols]) for k in range(KD)])
                    last.then_inc(sem("kv_mm"), 1)
                    pe.wait_ge(sem("hat"), n)
                    passes(ps["q"][:, 0:HG * d],
                           [(tile_of(HTh, k, t, 1), tile_of(HTl, k, t, 1),
                             WQh[slot][:, k, 0:HG * d], WQl[slot][:, k, 0:HG * d])
                            for k in range(KD)]).then_inc(sem("q_mm"), 1)

                def transpose_qk(n):
                    pe.wait_ge(sem("hat"), n + 1)
                    pe.wait_ge(sem("qT_ev"), n)
                    pe.wait_ge(sem("kT_ev"), n)
                    hat = qkh_of(n)
                    for h in range(HG):
                        pe.transpose(ps["qT"][0:d, h * P:(h + 1) * P], hat[:, h * d:(h + 1) * d], ident[:, :])
                    for j in range(l.tiles):
                        last = pe.transpose(ps["kT"][0:d, j * P:(j + 1) * P],
                                            hat[:, (HG + j) * d:(HG + j + 1) * d], ident[:, :])
                    last.then_inc(sem("qkT_mm"), 1)

                def scores(n):
                    pe.wait_ge(sem("qT_ev"), n + 1)
                    pe.wait_ge(sem("kT_ev"), n + 1)
                    pe.wait_ge(sem("ssub"), n)
                    
                    for hp in range(2):
                        for b in range(NB):
                            c = (hp * NB + b) * l.keys
                            last = pe.matmul(ps["s"][:, c:c + l.keys], qT[0:d, (b * 2 + hp) * P:(b * 2 + hp + 1) * P],
                                             kT[0:d, b * l.keys:(b + 1) * l.keys], start=True, stop=True)
                    last.then_inc(sem("s_mm"), 1)

                def transpose_p(n):
                    pe.wait_ge(sem("prob"), n + 1)
                    pe.wait_ge(sem("pT_lo"), n)
                    if l.tiles == 2:
                        for b in range(NB):
                            for hp in range(2):
                                c = (hp * NB + b) * P
                                last = pe.transpose(ps["pT"][:, (b * 2 + hp) * P:(b * 2 + hp + 1) * P],
                                                    sc[:, c:c + P], ident[:, :])
                    else:
                        for hp in range(2):
                            last = pe.transpose(ps["pT"][:, hp * P:(hp + 1) * P], sc[:, hp * P:(hp + 1) * P],
                                                ident[:, :])
                    last.then_inc(sem("pT_mm"), 1)

                def values(n, v):
                    pe.wait_ge(sem("pT_lo"), n + 1)
                    pe.wait_ge(sem("v_lo"), n + 1)
                    pe.wait_ge(sem("oT_lo"), n)
                    if l.tiles == 2:
                        for b in range(NB):
                            c = slice(b * 2 * P, (b + 1) * 2 * P)
                            last = passes(ps["oT"][0:d, c], [(vh[v][:, b * d:(b + 1) * d], vl[v][:, b * d:(b + 1) * d],
                                                              pTh[:, c], pTl[:, c])])
                    else:
                        last = passes(ps["oT"][0:d, :], [(vh[v][:, 0:d], vl[v][:, 0:d], pTh[:, :], pTl[:, :])])
                    last.then_inc(sem("av_mm"), 1)

                def project_out(n, t, slot, g):
                    if t == 0:
                        pe.wait_ge(sem("w_lo"), g * CHUNKS + (l.c0 + CHUNKS))
                    pe.wait_ge(sem("oT_lo"), n + 1)
                    pe.wait_ge(sem("x_add"), n)
                    passes(ps["y"][:, :], [(oTh[0:d, h * P:(h + 1) * P], oTl[0:d, h * P:(h + 1) * P], WOh[slot][0:d, h, :], WOl[slot][0:d, h, :])
                                           for h in range(HG)]).then_inc(sem("y_mm"), 1)

                slots = [(l.slot0 + h) % 2 for h in range(2)]
                n0 = l.n0
                pe.wait_ge(sem("ln_lo"), phase * T)
                qkh_of = lambda n: qkh[parity[0]]
                parity = [0]
                project(n0, 0, slots[0], 0)
                project(n0 + 1, 1, slots[0], 0)
                transpose_qk(n0)
                scores(n0)
                last_i = l.groups // 2 - 1
                with pe.Fori(0, l.groups // 2) as i:
                    for s in range(2 * T):
                        n = i * (2 * T) + (n0 + s)

                        def ahead2():
                            u = (s + 2) % (2 * T)
                            project(n + 2, u % T, slots[u // T], i * 2 + (s + 2) // T)

                        if s >= 2 * T - 2:
                            with pe.If(i < last_i):
                                ahead2()
                        else:
                            ahead2()
                        parity[0] = (s + 1) % 2
                        if s == 2 * T - 1:
                            with pe.If(i < last_i):
                                transpose_qk(n + 1)
                        else:
                            transpose_qk(n + 1)
                        transpose_p(n)
                        if s == 0:
                            with pe.If(i > 0):
                                project_out(n - 1, T - 1, slots[1], 0)
                        else:
                            project_out(n - 1, (s - 1) % T, slots[(s - 1) // T], i * 2 + (s - 1) // T)
                        if s == 2 * T - 1:
                            with pe.If(i < last_i):
                                scores(n + 1)
                        else:
                            scores(n + 1)
                        values(n, s % 4)
                project_out(l.end - 1, T - 1, slots[1], 0)

            windowed_attention()
            norm_transposes(1)
            experts(F0, 1, 0)
            norm_transposes(2)
            attention(L1, 2)
            norm_transposes(3)
            experts(F1, 3, 1)
            norm_transposes(4)
            attention(L2, 4)
            norm_transposes(5)
            experts(F2, 5, 2)
            norm_transposes(6)
            attention(L3, 6)
            for k in range(KD):
                pe.wait_ge(sem("wdq"), 1)
                bank = ps[("qT", "kT", "s", "pT")[k]]
                wk = wdq[:, :, :, :, :].rearrange("p t g j e -> p t (g j e)")
                for o_ in range(4):
                    last = pe.transpose(bank[:, o_ * P:(o_ + 1) * P], wk[:, o_, k * P:(k + 1) * P], ident[:, :])
                last.then_inc(sem("wdq_T"), 1)
            norm_transposes(7)
            experts(None, 7, 3)

        @block.scalar
        def _(act):
            prime(act, "act")
            act.sem_inc(sem("dots_ev"), 2)

            def copy(out, in_):
                return act.activation(out, in_, ACT.Copy)

            def cut_hi(c, k, out, rows, n, src_view=None):
                if isinstance(k, int):
                    act.wait_ge(sem(f"stage{c % 2}"), 16 * (k // 2 + 1))
                else:
                    act.wait_ge(sem(f"stage{c % 2}"), k)
                src = stage[c % 2][0:rows, 0:n]
                if src_view:
                    src = src_view(src)
                copy(out, src).then_inc(sem("w_hi"), 1)

            def cut_experts(f):
                n = f.cols + (D if f.dense else 0)
                for c in range(KD):
                    cut_hi(c, f.c0 + c, WQh[f.slot][:, c, 0:n], P, n)

            def cut_chunk(l, c, slot, g=None):
                if g is None:
                    k = l.c0 + c
                else:
                    k = g * (8 * CHUNKS) + 16 * ((l.c0 + c) // 2 + 1)
                if c < KD:
                    cut_hi(c, k, WQh[slot][:, c, 0:l.cols], P, l.cols)
                else:
                    cut_hi(c, k, WOh[slot][0:l.d, 2 * (c - KD):2 * (c - KD) + 2, :].rearrange("p h n -> p (h n)"),
                           l.d, STG)

            def norm_hi(phase):
                for t in range(T):
                    act.wait_ge(sem("ln_T"), (phase - 1) * T + t + 1)
                    bank = ps["q" if t % 2 == 0 else "kv"]
                    copy(HTh[:, :, 2 * t:2 * t + 2, :, 1], bank[:, :].rearrange("p (k b j) -> p k b j", k=KD, b=NB))\
                        .then_inc(sem("ln_hi"), 1)

            def windowed_attention():
                act.wait_ge(sem("e_in"), 32)
                copy(ETr[:, :, :], ETs[:, :, :]).then_inc(sem("et_cast"), 1)
                for t in range(T):
                    for j, (out, even, odd) in enumerate(((q0[:, t, :], "q", "qT"), (K0[:, t, PAD0:PAD0 + D], "kv", "kT"),
                                                          (V0[:, t, PAD0:PAD0 + D], "s", "pT"))):
                        act.wait_ge(sem("l0_mm"), 3 * t + j + 1)
                        act.activation(out, ps[odd if t % 2 else even][:, :], ACT.Identity, bias=b0[:, j:j + 1])\
                            .then_inc(sem("l0_ev"), 1)
                with act.Fori(0, W0 // 2) as i:
                    for h in range(2):
                        act.wait_ge(sem("dot_mm"), i * 16 + (h * 8 + 8 + 4))
                        copy(row(dots, i * 2 + h), ps[("y", "oT")[h]][:, :]).then_inc(sem("dots_ev"), 1)
                with act.Fori(0, W0) as w:
                    act.wait_ge(sem("e_sub"), w + 1)
                    act.activation(row(dots, w), row(dots, w), ACT.Exp, scale=float(S // H0) ** -0.5)\
                        .then_inc(sem("e_exp"), 1)
                    act.wait_ge(sem("e_exp"), w + 1)
                    copy(row(eh, w), row(dots, w)).then_inc(sem("e_hi"), 1)
                act.wait_ge(sem("rec"), 1)
                copy(rech[:, :], mx0[:, :]).then_inc(sem("rec_hi"), 1)
                for t in range(T):
                    act.wait_ge(sem("rspread_mm"), t + 1)
                    if t >= 1:
                        act.wait_ge(sem("o_l0"), t)
                    copy(rspread[:, :], ps["y"][:, :]).then_inc(sem("rspread_ev"), 1)

            def experts(f, index):
                for t in range(T):
                    act.wait_ge(sem("lr_mm"), index * T + t + 1)
                    copy(lr[:, t, 0:f.cols], ps[("s", "pT")[t % 2]][:, 0:f.cols]).then_inc(sem("lr_ev"), 1)
                if index < 2:
                    act.wait_ge(sem("gate_in"), index + 1)
                    act.activation(z2[:, :, 0:f.e], z[:, :, 0:f.e], ACT.Exp).then_inc(sem("gate_exp"), 1)
                for h in range(2):
                    act.wait_ge(sem("gT_mm"), 2 * index + h + 1)
                    copy(gT[0:f.er, 4 * h:4 * h + 4, :].rearrange("p t n -> p (t n)"),
                         ps[("qT", "kT")[h]][0:f.er, :]).then_inc(sem("gT_ev"), 1)

            def attention(l, f):
                d = l.d

                def v_and_squares(n, v):
                    act.wait_ge(sem("kv_mm"), n + 1)
                    act.wait_ge(sem("av_mm"), n - 3)
                    kv = ps["kv"][:, 0:l.tiles * 2 * d].rearrange("p (j c) -> p j c", j=l.tiles)
                    if l.norm_eps is not None:
                        act.wait_ge(sem("sumsq"), n - NORM0)
                        act.activation(sq[:, HG * d:(HG + l.tiles) * d].rearrange("p (j c) -> p j c", j=l.tiles),
                                       kv[:, :, 0:d], ACT.Square)
                    copy(vh[v][:, 0:l.tiles * d].rearrange("p (j c) -> p j c", j=l.tiles), kv[:, :, d:2 * d])\
                        .then_inc(sem("v_hi"), 1)
                    if l.norm_eps is not None:
                        act.wait_ge(sem("q_mm"), n + 1)
                        act.activation(sq[:, 0:HG * d], ps["q"][:, 0:HG * d], ACT.Square).then_inc(sem("squared"), 1)

                def qT_out(n):
                    act.wait_ge(sem("qkT_mm"), n + 1)
                    act.wait_ge(sem("s_mm"), n)
                    copy(qT[0:d, :].rearrange("p (b h q) -> p h b q", b=NB, h=HG),
                         ps["qT"][0:d, :].rearrange("p (h b q) -> p h b q", h=HG, b=NB)).then_inc(sem("qT_ev"), 1)

                def exps(n):
                    act.wait_ge(sem("ssub"), n + 1)
                    act.activation(sc[:, 0:4 * l.keys], sc[:, 0:4 * l.keys], ACT.Exp,
                                   scale=1.0 if l.masked else l.scale).then_inc(sem("exp"), 1)

                def pT_out(n):
                    act.wait_ge(sem("pT_mm"), n + 1)
                    act.wait_ge(sem("av_mm"), n)
                    if l.tiles == 2:
                        copy(pTh[:, :], ps["pT"][:, :]).then_inc(sem("pT_hi"), 1)
                    else:
                        for b in range(NB):
                            last = copy(pTh[b * S:(b + 1) * S, b * 2 * P:(b + 1) * 2 * P],
                                        block_of(b))
                        last.then_inc(sem("pT_hi"), 1)

                def block_of(b):
                    return ps["pT"][b * S:(b + 1) * S, 0:2 * P]

                by_head = lambda v: v[0:d, :].rearrange("p (h b q) -> p b h q", h=HG, b=NB)
                from_batch = lambda v: v[0:d, :].rearrange("p (b h q) -> p b h q", b=NB, h=HG)

                def oT_out(n):
                    act.wait_ge(sem("av_mm"), n + 1)
                    act.wait_ge(sem("y_mm"), n)
                    copy(by_head(oTh), from_batch(ps["oT"])).then_inc(sem("oT_hi"), 1)

                slots = [(l.slot0 + h) % 2 for h in range(2)]
                n0 = l.n0
                v_and_squares(n0, 0)
                v_and_squares(n0 + 1, 1)
                qT_out(n0)
                last_i = l.groups // 2 - 1
                with act.Fori(0, l.groups // 2) as i:
                    for s in range(2 * T):
                        n = i * (2 * T) + (n0 + s)
                        if s == 0:
                            with act.If(i > 0):
                                oT_out(n - 1)
                        else:
                            oT_out(n - 1)
                        exps(n)
                        if s >= 2 * T - 2:
                            with act.If(i < last_i):
                                v_and_squares(n + 2, (s + 2) % 4)
                        else:
                            v_and_squares(n + 2, (s + 2) % 4)
                        if s == 2 * T - 1:
                            with act.If(i < last_i):
                                qT_out(n + 1)
                        else:
                            qT_out(n + 1)
                        pT_out(n)
                        c = s % T - 1
                        if 0 <= c < CHUNKS:
                            slot = slots[(s // T + 1) % 2]
                            if s < T:
                                act.wait_ge(sem("y_mm"), n - 1)
                                cut_chunk(l, c, slot, i * 2 + 1)
                            else:
                                with act.If(i < last_i):
                                    act.wait_ge(sem("y_mm"), n - 1)
                                    cut_chunk(l, c, slot, i * 2 + 2)
                oT_out(l.end - 1)
                if f is not None:
                    act.wait_ge(sem("y_mm"), l.end - T)
                    cut_experts(f)

            windowed_attention()
            act.wait_ge(sem("x_l0"), T)
            cut_experts(F0)
            norm_hi(1)
            for c in range(KD):
                cut_hi(c, CTX_C0 + c, HTh[:, c, :, :, 0], P, STG, lambda v: v.rearrange("p (b j) -> p b j", b=B))
            experts(F0, 0)
            for c in range(CHUNKS):
                cut_chunk(L1, c, L1.slot0)
            norm_hi(2)
            attention(L1, F1)
            norm_hi(3)
            for c in range(CHUNKS):
                cut_chunk(L2, c, L2.slot0)
            experts(F1, 1)
            norm_hi(4)
            attention(L2, F2)
            norm_hi(5)
            for c in range(CHUNKS):
                cut_chunk(L3, c, L3.slot0)
            experts(F2, 2)
            norm_hi(6)
            attention(L3, None)
            for k in range(KD):
                act.wait_ge(sem("wdq_T"), k + 1)
                copy(WQh[1][:, k, 0:D], ps[("qT", "kT", "s", "pT")[k]][:, :]).then_inc(sem("wdq_hi"), 1)
            norm_hi(7)

        @block.gpsimd
        def _(pool):
            prime(pool, "pool")
            pool.sem_inc(sem("pair"), 2)
            pool.memset(mhalf[:, :], -0.5).then_inc(sem("mhalf"), 1)
            pool.wait_ge(sem("mhalf"), 1)

            def sub(out, in0, in1):
                return pool.tensor_tensor(out, in0, in1, ALU.subtract)

            def cut_lo(c, k, out, hi, rows, n, src_view=None):
                pool.wait_ge(sem("w_hi"), k + 1)
                src = stage[c % 2][0:rows, 0:n]
                if src_view:
                    src = src_view(src)
                sub(out, src, hi.bitcast(F32)).then_inc(sem("w_lo"), 1)

            def cut_experts(f):
                n = f.cols + (D if f.dense else 0)
                for c in range(KD):
                    cut_lo(c, f.c0 + c, WQl[f.slot][:, c, 0:n], WQh[f.slot][:, c, 0:n], P, n)

            def cut_chunk(l, c, slot, g=0):
                k = g * CHUNKS + (l.c0 + c)
                if c < KD:
                    cut_lo(c, k, WQl[slot][:, c, 0:l.cols], WQh[slot][:, c, 0:l.cols], P, l.cols)
                else:
                    v = [w[slot][0:l.d, 2 * (c - KD):2 * (c - KD) + 2, :].rearrange("p h n -> p (h n)")
                         for w in (WOl, WOh)]
                    cut_lo(c, k, v[0], v[1], l.d, STG)

            def norm_rstd(phase):
                pool.wait_ge(sem("ln_mv"), (phase + 1) * T)
                if phase:
                    pool.wait_ge(sem("ln_xn"), phase * T)
                pool.tensor_scalar(ve[:, :], mv[:, :, 1], LNEPS, None, ALU.add).then_inc(sem("ln_ve"), 1)
                pool.wait_ge(sem("ln_ve"), phase + 1)
                pool.tensor_tensor(rstd[:, :], ve[:, :], mhalf[:, 0:T], ALU.pow).then_inc(sem("ln_rstd"), 1)

            def attention(l):
                def norms(n):
                    k = HG + l.tiles
                    m = n - NORM0
                    pool.wait_ge(sem("meansq"), m + 1)
                    pool.wait_ge(sem("hat"), n)
                    pool.tensor_tensor(rs[:, 0:k], ms[:, 0:k], mhalf[:, 0:k], ALU.pow).then_inc(sem("rnorm"), 1)

                slots = [(l.slot0 + h) % 2 for h in range(2)]
                if l.norm_eps is not None:
                    norms(l.n0)
                    norms(l.n0 + 1)
                last_i = l.groups // 2 - 1
                with pool.Fori(0, l.groups // 2) as i:
                    for s in range(2 * T):
                        n = i * (2 * T) + (l.n0 + s)
                        if l.norm_eps is not None:
                            if s >= 2 * T - 2:
                                with pool.If(i < last_i):
                                    norms(n + 2)
                            else:
                                norms(n + 2)
                        c = s % T - 1
                        if 0 <= c < CHUNKS:
                            slot = slots[(s // T + 1) % 2]
                            if s < T:
                                cut_chunk(l, c, slot, i * 2 + 1)
                            else:
                                with pool.If(i < last_i):
                                    cut_chunk(l, c, slot, i * 2 + 2)

            def add_bias(index, phase, ff_in):
                pool.wait_ge(sem("ff_in"), ff_in)
                for t in range(T):
                    pool.wait_ge(sem("ln_xn"), phase * T + t + 1)
                    pool.tensor_tensor(X[:, t, :], X[:, t, :], bias[:, :], ALU.add).then_inc(sem("bias_add"), 1)

            norm_rstd(0)
            with pool.Fori(1, W0) as w:
                pool.wait_ge(sem("e_exp"), w + 1)
                pool.wait_ge(sem("e_sum"), w)
                pool.tensor_tensor(sum0[:, :], sum0[:, :], row(dots, w), ALU.add).then_inc(sem("e_sum"), 1)
            with pool.Fori(0, T * W0 // 4) as i:
                for h in range(2):
                    k = i * 2 + h
                    pool.wait_ge(sem("pv"), k * 2 + 6)
                    pool.wait_ge(sem("pairsum_mm"), k + 1)
                    pool.tensor_tensor(psumd[h][:, :], prod[2 * h][:, :], prod[2 * h + 1][:, :], ALU.add)\
                        .then_inc(sem("pair"), 1)
            cut_experts(F0)
            norm_rstd(1)
            for c in range(KD):
                v = lambda x: x.rearrange("p (b j) -> p b j", b=B)
                cut_lo(c, CTX_C0 + c, HTl[:, c, :, :, 0], HTh[:, c, :, :, 0], P, STG, v)
            for c in range(CHUNKS):
                cut_chunk(L1, c, L1.slot0)
            norm_rstd(2)
            attention(L1)
            cut_experts(F1)
            norm_rstd(3)
            for c in range(CHUNKS):
                cut_chunk(L2, c, L2.slot0)
            norm_rstd(4)
            attention(L2)
            cut_experts(F2)
            norm_rstd(5)
            add_bias(2, 5, FF_IN[2])
            for c in range(CHUNKS):
                cut_chunk(L3, c, L3.slot0)
            norm_rstd(6)
            attention(L3)
            norm_rstd(7)
            add_bias(3, 7, FF_IN[3])

        @block.vector
        def _(dve):
            prime(dve, "dve")
            dve.sem_inc(sem("pv"), 4)
            links = [0]

            def link(ins):
                links[0] += 1
                ins.then_inc(sem("dve_link"), 1)
                dve.wait_ge(sem("dve_link"), links[0])

            def sub(out, in0, in1):
                return dve.tensor_tensor(out, in0, in1, ALU.subtract)

            def norm_stats(phase, ready):
                for t in range(T):
                    ready(t)
                    dve.bn_stats(st[:, t, :], X[:, t, :]).then_inc(sem("ln_st"), 1)
                for t in range(T):
                    dve.wait_ge(sem("ln_st"), phase * T + t + 1)
                    dve.bn_aggr(mv[:, t, :], st[:, t, :]).then_inc(sem("ln_mv"), 1)

            def norm_tile(phase, t, used):
                if t == 0:
                    dve.wait_ge(sem("ln_rstd"), phase + 1)
                    dve.wait_ge(sem("ln_mv"), (phase + 1) * T)
                used(t)
                dve.tensor_scalar(xn[t % 2][:, :], X[:, t, :], mv[:, t, 0:1], rstd[:, t:t + 1],
                                  ALU.subtract, ALU.mult).then_inc(sem("ln_xn"), 1)

            def norm(phase, ready):
                norm_stats(phase, ready)

                def used(t):
                    if t >= 2:
                        dve.wait_ge(sem("ln_T"), (phase - 1) * T + t - 1)

                for t in range(2):
                    norm_tile(phase, t, used)
                for t in range(T):
                    dve.wait_ge(sem("ln_hi"), (phase - 1) * T + t + 1)
                    bank = ps["q" if t % 2 == 0 else "kv"]
                    sub(HTl[:, :, 2 * t:2 * t + 2, :, 1], bank[:, :].rearrange("p (k b j) -> p k b j", k=KD, b=NB),
                        HTh[:, :, 2 * t:2 * t + 2, :, 1].bitcast(F32)).then_inc(sem("ln_lo"), 1)
                    if t + 2 < T:
                        norm_tile(phase, t + 2, used)

            def windowed_attention():
                for pad in (K0, V0):
                    dve.memset(pad[:, :, 0:PAD0], 0.0)
                    dve.memset(pad[:, :, PAD0 + D:KW], 0.0).then_inc(sem("pads"), 1)
                norm_stats(0, lambda t: dve.wait_ge(sem("x_in"), 16))

                def used(t):
                    if t >= 2:
                        dve.wait_ge(sem("l0_mm"), 3 * (t - 2) + 1)

                for t in range(T):
                    norm_tile(0, t, used)
                dve.wait_ge(sem("pads"), 2)
                dve.wait_ge(sem("l0_ev"), 3 * T)
                dve.wait_ge(sem("et_cast"), 1)
                with dve.Fori(0, W0 // 2) as i:
                    for h in range(2):
                        for t in range(T):
                            j = i * 16 + (h * 8 + t)
                            dve.wait_ge(sem("dot_mm"), j + 1)
                            dve.tensor_tensor(prod[t % 4][:, :], q0[:, t, :], K0[:, t, bass.ds(i * 2 + h, D)],
                                              ALU.mult).then_inc(sem("prod"), 1)
                dve.wait_ge(sem("dots_ev"), W0 + 2)
                link(dve.tensor_copy(mx0[:, :], dots[:, 0, :]))
                link(dve.tensor_reduce(mx0[:, :], dots[:, :, :].rearrange("p w t -> p t w"), AX.X, ALU.max))
                sub(dots[:, 0, :], dots[:, 0, :], mx0[:, :]).then_inc(sem("e_sub"), 1)
                sub(dots[:, 1, :], dots[:, 1, :], mx0[:, :]).then_inc(sem("e_sub"), 1)
                dve.wait_ge(sem("e_exp"), 1)
                dve.tensor_copy(sum0[:, :], dots[:, 0, :]).then_inc(sem("e_sum"), 1)
                dve.wait_ge(sem("e_hi"), 1)
                sub(el[:, 0, :], dots[:, 0, :], eh[:, 0, :].bitcast(F32)).then_inc(sem("e_lo"), 1)
                with dve.Fori(1, W0 - 1) as w:
                    sub(row(dots, w + 1), row(dots, w + 1), mx0[:, :]).then_inc(sem("e_sub"), 1)
                    dve.wait_ge(sem("e_hi"), w + 1)
                    sub(row(el, w), row(dots, w), row(eh, w).bitcast(F32)).then_inc(sem("e_lo"), 1)
                dve.wait_ge(sem("e_hi"), W0)
                sub(el[:, W0 - 1, :], dots[:, W0 - 1, :], eh[:, W0 - 1, :].bitcast(F32)).then_inc(sem("e_lo"), 1)
                dve.wait_ge(sem("e_sum"), W0)
                dve.reciprocal(mx0[:, :], sum0[:, :]).then_inc(sem("rec"), 1)
                dve.wait_ge(sem("rec_hi"), 1)
                sub(recl[:, :], mx0[:, :], rech[:, :].bitcast(F32)).then_inc(sem("rec_lo"), 1)
                banks = ("q", "kv", "qT", "kT")
                for t in range(T):
                    with dve.Fori(0, W0 // 4) as i:
                        for u in range(4):
                            j = i * 4 + (t * W0 + u)
                            dve.wait_ge(sem("spread_mm"), j + 1)
                            dve.wait_ge(sem("pair"), (i * 2 + (t * W0 // 2 + u // 2)) + 1)
                            dve.tensor_tensor(prod[u][:, :], ps[banks[u]][:, :], V0[:, t, bass.ds(i * 4 + u, D)],
                                              ALU.mult).then_inc(sem("pv"), 1)
                    dve.wait_ge(sem("pairsum_mm"), (t + 1) * W0 // 2 + 2)
                    dve.wait_ge(sem("rspread_ev"), t + 1)
                    if t >= 1:
                        dve.wait_ge(sem("y_l0"), t)
                    dve.tensor_tensor(o0[:, :], ps[("s", "pT")[t % 2]][:, :], rspread[:, :], ALU.mult)\
                        .then_inc(sem("o_l0"), 1)
                    dve.wait_ge(sem("y_l0"), t + 1)
                    dve.scalar_tensor_tensor(X[:, t, :], ps["oT"][:, :], b0[:, 3:4], X[:, t, :], ALU.add, ALU.add)\
                        .then_inc(sem("x_l0"), 1)

            def expand(v, shape):
                return v.to_broadcast(shape)

            def experts(f, index):
                e = f.e
                if f.dense:
                    for t in range(T):
                        dve.wait_ge(sem("dense_mm"), t + 1)
                        dve.wait_ge(sem("bias_add"), t + 1)
                        dve.tensor_tensor(X[:, t, :], X[:, t, :], ps[("oT", "y")[t % 2]][:, :], ALU.add)\
                            .then_inc(sem("dense_add"), 1)
                dve.wait_ge(sem("lr_ev"), (index + 1) * T)
                dve.wait_ge(sem("ff_in"), FF_IN[index])
                logits = lr[:, :, f.er:f.er + e]
                over_e = lambda v: v[:, :].unsqueeze(2).to_broadcast([P, T, e])
                zv, ev = z[:, :, 0:e], z2[:, :, 0:e]
                as_j = lambda v: v.unsqueeze(2).to_broadcast([P, T, e, e])
                as_e = lambda v: v.unsqueeze(3).to_broadcast([P, T, e, e])
                if index == 0:
                    link(dve.tensor_tensor(zv, logits, rb[:, 0:e].unsqueeze(1).to_broadcast([P, T, e]), ALU.add))
                    link(dve.tensor_reduce(zr[:, :], zv, AX.X, ALU.max))
                    sub(zv, zv, over_e(zr)).then_inc(sem("gate_in"), 1)
                    dve.wait_ge(sem("gate_exp"), 1)
                    link(dve.tensor_reduce(zs[:, :], ev, AX.X, ALU.add))
                    link(dve.reciprocal(zt[:, :], zs[:, :]))
                    link(dve.scalar_tensor_tensor(gates[:, :, 0:e], ev, e * 32.0 / 16.0, over_e(zt), ALU.mult, ALU.mult))
                elif index == 1:
                    link(dve.tensor_reduce(zr[:, :], logits, AX.X, ALU.max))
                    sub(zv, logits, over_e(zr)).then_inc(sem("gate_in"), 1)
                    pv = pair[:, :, 0:e, 0:e]
                    dve.tensor_tensor(pv, as_j(logits), as_e(logits), ALU.is_gt)
                    link(dve.tensor_tensor(pair2[:, :, :, :], as_j(logits), as_e(logits), ALU.is_equal))
                    link(dve.tensor_tensor(pair2[:, :, :, :], pair2[:, :, :, :],
                                           tri[:, :].rearrange("p (a b) -> p a b", a=e).unsqueeze(1).to_broadcast([P, T, e, e]),
                                           ALU.mult))
                    link(dve.tensor_tensor(pv, pv, pair2[:, :, :, :], ALU.add))
                    link(dve.tensor_reduce(z3[:, :, 0:e], pv, AX.X, ALU.add))
                    dve.wait_ge(sem("gate_exp"), 2)
                    link(dve.scalar_tensor_tensor(ev, z3[:, :, 0:e], 1.5, ev, ALU.is_lt, ALU.mult))
                    link(dve.tensor_reduce(zs[:, :], ev, AX.X, ALU.add))
                    link(dve.reciprocal(zt[:, :], zs[:, :]))
                    link(dve.scalar_tensor_tensor(gates[:, :, 0:e], ev, 4.0, over_e(zt), ALU.mult, ALU.mult))
                else:
                    link(dve.tensor_tensor(zv, logits, rb[:, 0:e].unsqueeze(1).to_broadcast([P, T, e]), ALU.add))
                    link(dve.tensor_tensor(pair[:, :, :, :], as_j(zv), as_e(zv), ALU.subtract))
                    link(dve.tensor_scalar(pair[:, :, :, :], pair[:, :, :, :], 0.0, None, ALU.max))
                    link(dve.tensor_reduce(z3[:, :, :], pair[:, :, :, :], AX.X, ALU.add))
                    link(dve.tensor_scalar(z3[:, :, :], z3[:, :, :], 1.0, None, ALU.is_lt))
                    dve.tensor_reduce(zr[:, :], z3[:, :, :], AX.X, ALU.add)
                    link(dve.tensor_tensor(z2[:, :, :], z3[:, :, :], zv, ALU.mult))
                    link(dve.tensor_reduce(zs[:, :], z2[:, :, :], AX.X, ALU.add))
                    link(dve.reciprocal(zt[:, :], zr[:, :]))
                    link(dve.scalar_tensor_tensor(zs[:, :], zs[:, :], -1.0, zt[:, :], ALU.add, ALU.mult))
                    link(dve.tensor_tensor(z2[:, :, :], zv, over_e(zs), ALU.subtract))
                    link(dve.tensor_scalar(gates[:, :, :], z2[:, :, :], 0.0, None, ALU.max))
                for h in range(2):
                    tt = slice(4 * h, 4 * h + 4)
                    last = dve.tensor_tensor(gated[:, tt, 0:f.er].rearrange("p t (e r) -> p t e r", e=e),
                                             lr[:, tt, 0:f.er].rearrange("p t (e r) -> p t e r", e=e),
                                             gates[:, tt, 0:e].unsqueeze(3).to_broadcast([P, 4, e, f.r]), ALU.mult)
                last.then_inc(sem("gated"), 1)
                for t in range(T):
                    dve.wait_ge(sem("ff_mm"), index * T + t + 1)
                    dve.wait_ge(sem("dense_add"), T if f.dense else 0) if f.dense else None
                    dve.tensor_tensor(X[:, t, :], X[:, t, :], ps[("oT", "y")[t % 2]][:, :], ALU.add)\
                        .then_inc(sem("x_ff"), 1)

            def attention(l, norm_w):
                d, keys = l.d, l.keys
                nq = HG + l.tiles

                def v_rest(n, v):
                    dve.wait_ge(sem("v_hi"), n + 1)
                    kv = ps["kv"][:, 0:l.tiles * 2 * d].rearrange("p (j c) -> p j c", j=l.tiles)
                    sub(vl[v][:, 0:l.tiles * d].rearrange("p (j c) -> p j c", j=l.tiles), kv[:, :, d:2 * d],
                        vh[v][:, 0:l.tiles * d].rearrange("p (j c) -> p j c", j=l.tiles).bitcast(F32))\
                        .then_inc(sem("v_lo"), 1)

                def sum_squares(n):
                    if l.norm_eps is None:
                        return
                    m = n - NORM0
                    dve.wait_ge(sem("squared"), m + 1)
                    dve.tensor_reduce(ss[:, 0:nq], sq[:, 0:nq * d].rearrange("p (h c) -> p h c", h=nq), AX.X, ALU.add)\
                        .then_inc(sem("sumsq"), 1)
                    dve.wait_ge(sem("sumsq"), m + 1)
                    dve.wait_ge(sem("rnorm"), m)
                    dve.tensor_scalar(ms[:, 0:nq], ss[:, 0:nq], 1.0 / d, l.norm_eps, ALU.mult, ALU.add)\
                        .then_inc(sem("meansq"), 1)

                def hats(n, p):
                    dve.wait_ge(sem("kv_mm"), n + 1)
                    dve.wait_ge(sem("q_mm"), n + 1)
                    dve.wait_ge(sem("qkT_mm"), n - 1)
                    kv = ps["kv"][:, 0:l.tiles * 2 * d].rearrange("p (j c) -> p j c", j=l.tiles)[:, :, 0:d]
                    k_out = qkh[p][:, HG * d:nq * d].rearrange("p (j c) -> p j c", j=l.tiles)
                    if l.norm_eps is None:
                        dve.tensor_copy(k_out, kv).then_inc(sem("hat_k"), 1)
                        dve.tensor_copy(qkh[p][:, 0:HG * d], ps["q"][:, 0:HG * d]).then_inc(sem("hat"), 1)
                    else:
                        dve.wait_ge(sem("rnorm"), n - NORM0 + 1)
                        dve.tensor_tensor(k_out, kv, rs[:, HG:nq].unsqueeze(2).to_broadcast([P, l.tiles, d]), ALU.mult)\
                            .then_inc(sem("hat_k"), 1)
                        dve.tensor_tensor(qkh[p][:, 0:HG * d].rearrange("p (h c) -> p h c", h=HG),
                                          ps["q"][:, 0:HG * d].rearrange("p (h c) -> p h c", h=HG),
                                          rs[:, 0:HG].unsqueeze(2).to_broadcast([P, HG, d]), ALU.mult)\
                            .then_inc(sem("hat"), 1)

                def kT_out(n):
                    dve.wait_ge(sem("qkT_mm"), n + 1)
                    dve.wait_ge(sem("s_mm"), n)
                    src = ps["kT"][0:d, 0:l.tiles * P]
                    if norm_w is None:
                        dve.tensor_copy(kT[0:d, 0:l.tiles * P], src).then_inc(sem("kT_ev"), 1)
                    else:
                        dve.tensor_scalar(kT[0:d, 0:l.tiles * P], src, norm_w, None, ALU.mult).then_inc(sem("kT_ev"), 1)

                s3 = sc[:, 0:4 * keys].rearrange("p (g k) -> p g k", g=4)
                p3 = ps["s"][:, 0:4 * keys].rearrange("p (g k) -> p g k", g=4)
                over_k = lambda v: v[:, :].unsqueeze(2).to_broadcast([P, 4, keys])

                def score_rest(n):
                    dve.wait_ge(sem("s_mm"), n + 1)
                    dve.wait_ge(sem("pT_mm"), n)
                    if l.masked:
                        dve.scalar_tensor_tensor(s3, p3, l.scale, mask[:, :].unsqueeze(1).to_broadcast([P, 4, keys]),
                                                 ALU.mult, ALU.add).then_inc(sem("masked"), 1)
                        dve.wait_ge(sem("masked"), n - l.n0 + 1)
                        src = s3
                    else:
                        src = p3
                    dve.tensor_reduce(smx[:, :], src, AX.X, ALU.max).then_inc(sem("smax"), 1)
                    dve.wait_ge(sem("smax"), n + 1)
                    sub(s3, src, over_k(smx)).then_inc(sem("ssub"), 1)

                def probs(n):
                    dve.wait_ge(sem("exp"), n + 1)
                    dve.tensor_reduce(ssum[:, :], s3, AX.X, ALU.add).then_inc(sem("ssum"), 1)
                    dve.wait_ge(sem("ssum"), n + 1)
                    dve.reciprocal(srec[:, :], ssum[:, :]).then_inc(sem("srec"), 1)
                    dve.wait_ge(sem("srec"), n + 1)
                    dve.tensor_tensor(s3, s3, over_k(srec), ALU.mult).then_inc(sem("prob"), 1)

                def pT_rest(n):
                    dve.wait_ge(sem("pT_hi"), n + 1)
                    if l.tiles == 2:
                        sub(pTl[:, :], ps["pT"][:, :], pTh[:, :].bitcast(F32)).then_inc(sem("pT_lo"), 1)
                    else:
                        for b in range(NB):
                            c = slice(b * 2 * P, (b + 1) * 2 * P)
                            r = slice(b * S, (b + 1) * S)
                            last = sub(pTl[r, c], ps["pT"][r, 0:2 * P], pTh[r, c].bitcast(F32))
                        last.then_inc(sem("pT_lo"), 1)

                by_head = lambda v: v[0:d, :].rearrange("p (h b q) -> p b h q", h=HG, b=NB)
                from_batch = lambda v: v[0:d, :].rearrange("p (b h q) -> p b h q", b=NB, h=HG)

                def oT_rest(n):
                    dve.wait_ge(sem("oT_hi"), n + 1)
                    sub(by_head(oTl), from_batch(ps["oT"]), by_head(oTh).bitcast(F32)).then_inc(sem("oT_lo"), 1)

                def x_update(n, t):
                    dve.wait_ge(sem("y_mm"), n + 1)
                    dve.tensor_tensor(X[:, t, :], X[:, t, :], ps["y"][:, :], ALU.add).then_inc(sem("x_add"), 1)

                n0 = l.n0
                if l.tiles == 1:
                    for v in (pTh, pTl):
                        for b in range(NB):
                            dve.memset(v[b * S:(b + 1) * S, (1 - b) * 2 * P:(2 - b) * 2 * P].bitcast(F32), 0.0)
                for k in range(2):
                    v_rest(n0 + k, k)
                    sum_squares(n0 + k)
                    hats(n0 + k, k)
                kT_out(n0)
                last_i = l.groups // 2 - 1
                with dve.Fori(0, l.groups // 2) as i:
                    for s in range(2 * T):
                        n = i * (2 * T) + (n0 + s)
                        score_rest(n)
                        if s == 0:
                            with dve.If(i > 0):
                                oT_rest(n - 1)
                        else:
                            oT_rest(n - 1)
                        probs(n)
                        if s >= 2 * T - 2:
                            with dve.If(i < last_i):
                                v_rest(n + 2, (s + 2) % 4)
                                sum_squares(n + 2)
                        else:
                            v_rest(n + 2, (s + 2) % 4)
                            sum_squares(n + 2)
                        if s == 2 * T - 1:
                            with dve.If(i < last_i):
                                kT_out(n + 1)
                        else:
                            kT_out(n + 1)
                        pT_rest(n)
                        if s >= 2 * T - 2:
                            with dve.If(i < last_i):
                                hats(n + 2, s % 2)
                        else:
                            hats(n + 2, s % 2)
                        if s == 0:
                            with dve.If(i > 0):
                                x_update(n - 1, T - 1)
                        else:
                            x_update(n - 1, (s - 1) % T)
                oT_rest(l.end - 1)
                x_update(l.end - 1, T - 1)

            def ready(name, first):
                return lambda t: dve.wait_ge(sem(name), first + t + 1)

            dve.wait_ge(sem("small_in"), 96)
            for j in range(2):
                dve.tensor_tensor(kw[:, j:j + 1], knorm[:, 2 * j:2 * j + 1], knorm[:, 2 * j + 1:2 * j + 2], ALU.mult)\
                    .then_inc(sem("kw"), 1)
            dve.wait_ge(sem("kw"), 2)
            windowed_attention()
            norm(1, ready("x_l0", 0))
            experts(F0, 0)
            norm(2, ready("x_ff", 0))
            attention(L1, None)
            norm(3, ready("x_add", L1.end - T))
            experts(F1, 1)
            norm(4, ready("x_ff", T))
            attention(L2, kw[:, 0:1])
            norm(5, ready("x_add", L2.end - T))
            experts(F2, 2)
            norm(6, ready("x_ff", 2 * T))
            attention(L3, kw[:, 1:2])
            dve.wait_ge(sem("pk_in"), 48)
            dve.tensor_scalar(low4[:, :, :], packed[:, :, :], 15, None, ALU.bitwise_and)
            link(dve.tensor_scalar(high4[:, :, :], packed[:, :, :], 4, 15, ALU.logical_shift_right, ALU.bitwise_and))
            for t in range(4):
                for j, nib in enumerate((low4, high4)):
                    shape = [P, 8, 32]
                    dve.tensor_tensor(wdq[:, t, :, :, j], nib[:, t, :].rearrange("p (g c) -> p g c", g=8),
                                      wsc[:, t, :].unsqueeze(2).to_broadcast(shape), ALU.mult).then_inc(sem("wdq_mul"), 1)
            for t in range(4):
                for j in range(2):
                    dve.wait_ge(sem("wdq_mul"), 2 * t + j + 1)
                    last = dve.tensor_tensor(wdq[:, t, :, :, j], wdq[:, t, :, :, j],
                                             wze[:, t, :].unsqueeze(2).to_broadcast([P, 8, 32]), ALU.add)
            last.then_inc(sem("wdq"), 1)
            for k in range(KD):
                dve.wait_ge(sem("wdq_hi"), k + 1)
                sub(WQl[1][:, k, 0:D], ps[("qT", "kT", "s", "pT")[k]][:, :], WQh[1][:, k, 0:D].bitcast(F32))\
                    .then_inc(sem("wdq_lo"), 1)
            norm(7, ready("x_add", L3.end - T))
            for t in range(T):
                dve.wait_ge(sem("dense_mm"), T + t + 1)
                dve.wait_ge(sem("bias_add"), T + t + 1)
                dve.tensor_tensor(X[:, t, :], X[:, t, :], ps[("oT", "y")[t % 2]][:, :], ALU.add)\
                    .then_inc(sem("dense_add"), 1)


FF_IN = [32, 64, 112, 128]


def kernel(**inputs):
    import concourse.bacc as bacc
    from concourse.bass_utils import run_bass_kernel_spmd

    v = {k: np.asarray(x) for k, x in inputs.items()}
    f32 = np.float32

    def pair_rows(w):
        out = np.zeros((P, P), w.dtype)
        out[:S, :S] = w.T
        out[S:, S:] = w.T
        return out

    def group_qkv(wq, wk, wv, groups, d):
        q = wq.reshape(KD, P, groups, HG * d).transpose(2, 0, 1, 3)
        k = wk.reshape(KD, P, groups, d).transpose(2, 0, 1, 3)
        w = wv.reshape(KD, P, groups, d).transpose(2, 0, 1, 3)
        return np.ascontiguousarray(np.concatenate([q, k, w], -1))

    def group_out(wo, groups, d):
        return np.ascontiguousarray(wo.reshape(groups, 2, 2, d, D).transpose(0, 1, 3, 2, 4).reshape(groups, 2, d, 2 * D))

    def rows(w):
        return np.ascontiguousarray(w.T.reshape(KD, P, -1))

    ranks = lambda w: w.reshape(-1, D)
    c = np.arange(P)
    head = np.zeros((P, T, P), f32)
    for t in range(T):
        head[c, t, t * 16 + c // 8] = 1.0
    arrays = {
        "x": v["x"].reshape(B * S, D),
        "ctx": v["ctx_4096"].reshape(B * S, D),
        "ctxT": np.ascontiguousarray(v["ctx_4096"].reshape(B * S, D).T.reshape(KD, P, B * S)),
        "mask": v["mask_1x1xSxS2_ff0"].reshape(S, S),
        "ident": np.eye(P, dtype=f32),
        "tri": np.tril(np.ones((4, 4), f32), -1).reshape(16),
        "head_sum": head,
        "head_spread": np.ascontiguousarray(head.transpose(2, 1, 0)),
        "w0": np.ascontiguousarray(np.stack([pair_rows(v["L0_xattn_W" + n]) for n in "qkvo"], 1)),
        "b0": np.ascontiguousarray(np.stack([np.tile(v["L0_xattn_b" + n], 2) for n in "qkvo"], 1)),
        "knorm": np.ascontiguousarray(np.stack([v["L2_xattn_q_norm_w"], v["L2_xattn_k_norm_w"],
                                                v["L3_xattn_q_norm_w"], v["L3_xattn_k_norm_w"]], 1)),
        "f0_ar": rows(np.concatenate([ranks(v["L0_ffn_A"]), v["L0_ffn_Wr"]], 0)),
        "f0_b": np.ascontiguousarray(v["L0_ffn_B"].transpose(0, 2, 1).reshape(P, D)),
        "f0_rb": v["L0_ffn_br"],
        "f1_ar": rows(np.concatenate([ranks(v["L1_ffn_A"]), v["L1_ffn_Wr"]], 0)),
        "f1_b": np.ascontiguousarray(v["L1_ffn_B"].transpose(0, 2, 1).reshape(64, D)),
        "f2_ar": rows(np.concatenate([v["L2_ffn_W_base"], ranks(v["L2_ffn_lora_A"].transpose(0, 2, 1)),
                                      v["L2_ffn_W_router"]], 0)),
        "f2_b": v["L2_ffn_lora_B"].reshape(P, D),
        "f2_rb": v["L2_ffn_b_router"],
        "f2_bias": v["L2_ffn_b_base"],
        "l1_qkv": group_qkv(v["L1_xattn_Wq"].T, v["L1_xattn_Wk"].T, v["L1_xattn_Wv"].T, 4, 96),
        "l1_o": group_out(v["L1_xattn_Wo"].T, 4, 96),
        "l2_qkv": group_qkv(v["L2_xattn_q_proj_w"].T, v["L2_xattn_k_proj_w"].T, v["L2_xattn_v_proj_w"].T, 8, 128),
        "l2_o": group_out(v["L2_xattn_o_proj_w"].T, 8, 128),
        "l3_qkv": group_qkv(v["L3_xattn_Wq"], v["L3_xattn_Wk"], v["L3_xattn_Wv"], 8, 128),
        "l3_o": group_out(v["L3_xattn_Wo"], 8, 128),
        "packed": v["L3_ffn_weight_packed"].reshape(D, 256),
        "scales": v["L3_ffn_weight_scales"].reshape(D, 8),
        "zeros": v["L3_ffn_weight_zeros"].reshape(D, 8),
        "f3_bias": v["L3_ffn_bias"],
    }
    nc = bacc.Bacc("TRN2", target_bir_lowering=False, num_devices=1)
    feeds, aps = {}, {}
    for name, x in arrays.items():
        x = np.ascontiguousarray(x)
        feeds["in_" + name] = x
        aps[name] = nc.dram_tensor("in_" + name, x.shape, mybir.dt.from_np(x.dtype), kind="ExternalInput").ap()
    aps["out"] = nc.dram_tensor("out_x", (B * S, D), F32, kind="ExternalOutput").ap()
    build(nc, aps)
    r = run_bass_kernel_spmd(nc, [feeds], core_ids=[0])
    return r.results[0]["out_x"].reshape(B, S, D)
```

```python
from contextlib import ExitStack

import numpy as np

import concourse.bass as bass
from concourse import mybir

ALU = mybir.AluOpType
ACT = mybir.ActivationFunctionType
AX = mybir.AxisListType
F32 = mybir.dt.float32
F32R = mybir.dt.float32r
I32 = mybir.dt.int32

P = 128
D = 512
KD = D // P
B, S = 16, 64
T = B * S // P
HG = 4
NB = 2
W0 = 16
H0 = 8
PAD0 = W0 // 2
KW = D + W0
LNEPS = 1e-5
START = 4
QC = 4 * P + 2 * P
CHUNKS = 6
STG = 1024


class Attention:

    def __init__(self, groups, d, tiles, norm_eps, masked, slot0, n0, c0):
        self.groups, self.d, self.tiles, self.norm_eps, self.masked = groups, d, tiles, norm_eps, masked
        self.slot0, self.n0, self.c0 = slot0, n0, c0
        self.keys = S * tiles
        self.scale = float(d) ** -0.5
        self.steps = groups * T
        self.end = n0 + self.steps
        self.cols = HG * d + 2 * d


class Experts:

    def __init__(self, experts, rank, dense, slot, c0):
        self.e, self.r, self.dense, self.slot, self.c0 = experts, rank, dense, slot, c0
        self.er = experts * rank
        self.cols = self.er + experts


def build(nc, a):
    L1 = Attention(4, 96, 2, None, False, 1, START, 8)
    L2 = Attention(8, 128, 1, 1e-5, True, 0, L1.end, L1.c0 + CHUNKS * 4 + 4)
    L3 = Attention(8, 128, 2, 1e-6, False, 1, L2.end, L2.c0 + CHUNKS * 8 + 4)
    F0 = Experts(8, 16, False, 0, 0)
    F1 = Experts(4, 16, False, 1, L1.c0 + CHUNKS * 4)
    F2 = Experts(8, 16, True, 0, L2.c0 + CHUNKS * 8)
    CTX_C0 = 4
    SMALL = 16 * 10
    SUMS = 6
    SUM_AT = (7, 9, 13, 15, 16 + 1, 16 + 5)
    NORM0 = L1.steps

    with ExitStack() as ctx:
        used = nc.sbuf_usable_end - nc.sbuf_bytes_remaining

        def at(name, shape, dt, offset):
            n = int(np.prod(shape[1:])) * 4
            return nc.alloc_sbuf_tensor_at(name, shape, dt, offset=offset), offset + (n + 31) // 32 * 32

        base = (used + 31) // 32 * 32
        X, o = at("x", [P, T, D], F32, base)
        HT_at = o
        HTh, o_e = at("hT_hi", [P, KD, B, S, 2], F32R, o)
        HTl, o = at("hT_lo", [P, KD, B, S, 2], F32R, o_e)
        w_at = o
        WQh = [None, None]; WQl = [None, None]; WOh = [None, None]; WOl = [None, None]
        for s in range(2):
            WQh[s], o = at(f"wqkv_hi{s}", [P, KD, QC], F32R, o)
            WQl[s], o = at(f"wqkv_lo{s}", [P, KD, QC], F32R, o)
            wo_at = o
            WOh[s], o = at(f"wo_hi{s}", [P, HG, D], F32R, o)
            WOl[s], o = at(f"wo_lo{s}", [P, HG, D], F32R, o)
        w_end = o
        stage = [None, None]
        for s in range(2):
            stage[s], o = at(f"stage{s}", [P, STG], F32, o)
        ident, o = at("ident", [P, P], F32, o)
        ident_r, o = at("ident_r", [P, P], F32R, o)
        mask, o = at("mask", [P, S], F32, o)
        knorm, o = at("knorm", [P, 4], F32, o)
        kw, o = at("kw", [P, 2], F32, o)
        mhalf, o = at("mhalf", [P, 8], F32, o)
        st, o = at("ln_stats", [P, T, 6], F32, o)
        mv, o = at("ln_mean_var", [P, T, 2], F32, o)
        ve, o = at("ln_var_eps", [P, T], F32, o)
        rstd, o = at("ln_rstd", [P, T], F32, o)
        mneg, o = at("ln_minus_mean", [P, T], F32, o)
        shift, o = at("ln_shift", [P, T], F32, o)
        rb = [None, None]
        for s in range(2):
            rb[s], o = at(f"router_bias{s}", [P, 8], F32, o)
        tri, o = at("tri", [P, 16], F32, o)
        xn = [None, None]
        for s in range(2):
            xn[s], o = at(f"xn{s}", [P, D], F32, o)
        bias, o = at("bias_rows", [P, D], F32, o)
        bias_at = o
        o += 256
        work = o
        qkh = [None, None]; vh = [None] * 4; vl = [None] * 4
        sq, o = at("squares", [P, QC], F32, work)
        ss, o = at("sumsq", [P, 8], F32, o)
        ms, o = at("meansq", [P, 8], F32, o)
        rs, o = at("rnorm", [P, 8], F32, o)
        for s in range(2):
            qkh[s], o = at(f"qk_hat{s}", [P, QC], F32, o)
        qT, o = at("qT", [P, HG * P], F32, o)
        kT, o = at("kT", [P, 2 * P], F32, o)
        for s in range(4):
            vh[s], o = at(f"v_hi{s}", [P, 2 * P], F32R, o)
            vl[s], o = at(f"v_lo{s}", [P, 2 * P], F32R, o)
        sc, o = at("scores", [P, 4 * P], F32, o)
        smx, o = at("score_max", [P, 4], F32, o)
        ssum, o = at("score_sum", [P, 4], F32, o)
        srec, o = at("score_rec", [P, 4], F32, o)
        pTh, o = at("pT_hi", [P, 4 * P], F32R, o)
        pTl, o = at("pT_lo", [P, 4 * P], F32R, o)
        oTh, o = at("oT_hi", [P, 4 * P], F32R, o)
        oTl, o = at("oT_lo", [P, 4 * P], F32R, o)
        assert o <= nc.sbuf_usable_end, o - nc.sbuf_usable_end
        lr, o = at("low_logits", [P, T, 136], F32, work)
        gated, o = at("gated", [P, T, P], F32, o)
        gT, o = at("gatedT", [P, T, P], F32, o)
        Bf, o = at("expert_out", [P, D], F32, o)
        z, o = at("z", [P, T, 8], F32, o)
        z2, o = at("z2", [P, T, 8], F32, o)
        z3, o = at("z3", [P, T, 8], F32, o)
        zr, o = at("zr", [P, T], F32, o)
        zs, o = at("zs", [P, T], F32, o)
        zt, o = at("zt", [P, T], F32, o)
        pair, o = at("pairs", [P, T, 8, 8], F32, o)
        pair2, o = at("pairs2", [P, T, 4, 4], F32, o)
        gates, o = at("gates", [P, T, 8], F32, o)
        assert o <= nc.sbuf_usable_end
        packed, o = at("packed", [P, 4, 256], I32, wo_at)
        low4, o = at("low4", [P, 4, 256], I32, o)
        wdq, o = at("w_dequant", [P, 4, 8, 32, 2], F32, o)
        assert o <= w_end
        wsc, o = at("w_scales", [P, 4, 8], F32, bias_at)
        wze, o = at("w_zeros", [P, 4, 8], F32, o)
        dots, o = at("dots", [P, W0 + 1, D], F32, w_at)
        ctxn, _ = at("ctxn", [P, T, D], F32, w_at)
        K0, o = at("k_padded", [P, T, KW], F32, o)
        V0, o = at("v_padded", [P, T, KW], F32, o)
        E0, o = at("head_sum", [P, T, P], F32, o)
        ETr, o = at("head_spread", [P, T, P], F32R, o)
        w0, o = at("w_l0", [P, 4, P], F32, o)
        b0, o = at("b_l0", [P, 4], F32, o)
        assert o <= w_end
        q0, o = at("q_l0", [P, T, D], F32, work)
        mx0, o = at("max_l0", [P, D], F32, o)
        prod = [None] * 8
        for s in range(4):
            prod[s], o = at(f"prod{s}", [P, D], F32, o)
        assert o <= nc.sbuf_usable_end
        E0r, o = at("head_sum_r", [P, T, P], F32R, HT_at)
        ETs, o = at("head_spread_in", [P, T, P], F32, o)
        proh = [None] * 4; prol = [None] * 4
        for s in range(4):
            proh[s], o = at(f"prod_hi{s}", [P, D], F32R, o)
            prol[s], o = at(f"prod_lo{s}", [P, D], F32R, o)
        for s in range(4, 8):
            prod[s], o = at(f"prod{s}", [P, D], F32, o)
        assert o <= w_at
        qk_prod = [prod[s] for s in (0, 4, 1, 5, 2, 6, 3, 7)]
        o = work
        psumd = [None] * 4; rspread = [None, None]
        for s in range(4):
            psumd[s], o = at(f"prod_pair{s}", [P, D], F32, o)
        rec, o = at("rec_l0", [P, D], F32, o)
        rech, o = at("rec_hi", [P, D], F32R, o)
        recl, o = at("rec_lo", [P, D], F32R, o)
        o = w_at + 4 * (W0 + 1) * D
        pv_prod = [prod[s] for s in range(4)] + [None] * 4
        for s in range(4, 8):
            pv_prod[s], o = at(f"pv_prod{s}", [P, D], F32, o)
        for s in range(2):
            rspread[s], o = at(f"rec_spread{s}", [P, D], F32, o)
        o0, o = at("o_l0", [P, D], F32, o)
        spread_of = [None, None]
        for s in range(2):
            spread_of[s], o = at(f"head_spread_of{s}", [P, P], F32R, o)
        assert o <= w_at + 4 * (W0 + 1) * D + 4 * T * KW
        eh = HTh.ap().rearrange("p k b j s -> p (k b j s)").rearrange("p (w t) -> p w t", w=W0)
        el = HTl.ap().rearrange("p k b j s -> p (k b j s)").rearrange("p (w t) -> p w t", w=W0)

        ps = {}
        for name in ("q", "kv", "qT", "kT", "s", "pT", "oT", "y"):
            ps[name] = ctx.enter_context(nc.psum_tensor("ps_" + name, [P, 512], F32))

        sems = {}

        def sem(name):
            if name not in sems:
                sems[name] = ctx.enter_context(nc.semaphore(name))
            return sems[name]

        STEP = {
            "pe": ["kv_mm", "q_mm", "qkT_mm", "s_mm", "pT_mm", "av_mm", "y_mm"],
            "act": ["v_hi", "qT_ev", "exp", "pT_hi", "oT_hi", "squared"],
            "dve": ["v_lo", "hat", "hat_k", "kT_ev", "smax", "ssub", "ssum", "srec", "prob", "pT_lo", "oT_lo", "x_add", "sumsq", "meansq"],
            "pool": ["rnorm"],
        }
        block = ctx.enter_context(nc.Block())

        def prime(eng, who):
            for name in STEP[who]:
                eng.sem_inc(sem(name), START)

        def tile_of(H, k, t, s):
            return H[:, k, 2 * t:2 * t + 2, :, s].rearrange("p b j -> p (b j)")

        def row(t3, i):
            return t3[:, bass.ds(i, 1), :].rearrange("p a b -> p (a b)")

        def norm_bank(phase, t):
            return ps[(("s", "pT"), ("q", "kv"))[phase % 2][t % 2]]

        @block.sync
        def _(sp):
            sp.dma_start(w0[:, :, :], a["w0"]).then_inc(sem("w0_in"), 16)
            sp.dma_start(b0[:, :], a["b0"]).then_inc(sem("b0_in"), 16)
            for h in range(T // 2):
                sp.dma_start(ctxn[:, 2 * h:2 * h + 2, :], a["ctx"][2 * h * P:2 * (h + 1) * P, :].rearrange("(t p) d -> p t d", p=P))\
                    .then_inc(sem(f"ctx_in{h}"), 16)
            sp.dma_start(E0[:, :, :], a["head_sum"]).then_inc(sem("e_in"), 16)
            sp.dma_start(ETs[:, :, :], a["head_spread"]).then_inc(sem("e_in"), 16)
            sp.dma_start(ident[:, :], a["ident"]).then_inc(sem("small_in"), 16)
            sp.dma_start(mask[0:S, :], a["mask"]).then_inc(sem("small_in"), 16)
            sp.dma_start(mask[S:P, :], a["mask"]).then_inc(sem("small_in"), 16)
            sp.dma_start(knorm[:, :], a["knorm"]).then_inc(sem("small_in"), 16)
            sp.dma_start(rb[0][:, :], a["f0_rb"].partition_broadcast(P)).then_inc(sem("small_in"), 16)
            sp.dma_start(rb[1][:, :], a["f2_rb"].partition_broadcast(P)).then_inc(sem("small_in"), 16)
            sp.dma_start(tri[:, :], a["tri"].partition_broadcast(P)).then_inc(sem("small_in"), 16)
            sp.dma_start(bias[:, :], a["f2_bias"].partition_broadcast(P)).then_inc(sem("small_in"), 16)
            sp.dma_start(wsc[:, :, :], a["scales"].rearrange("(t p) g -> p t g", p=P)).then_inc(sem("small_in"), 16)
            sp.dma_start(wze[:, :, :], a["zeros"].rearrange("(t p) g -> p t g", p=P)).then_inc(sem("small_in"), 16)

            def load(c, k, src):
                if not isinstance(k, int) or k >= 2:
                    sp.wait_ge(sem("w_lo"), k - 1)
                rows, n = src.shape[0], src.shape[1]
                sp.dma_start(stage[c % 2][0:rows, 0:n], src).then_inc(sem(f"stage{c % 2}"), 16)

            def load_experts(f, src):
                for c in range(KD):
                    load(c, f.c0 + c, src[c])

            def load_group(l, g, name):
                for c in range(KD):
                    load(c, l.c0 + g * CHUNKS + c, a[name + "_qkv"][bass.ds(g, 1), c].rearrange("o p n -> (o p) n"))
                for c in range(2):
                    load(c, l.c0 + g * CHUNKS + KD + c,
                         a[name + "_o"][bass.ds(g, 1), c].rearrange("o p n -> (o p) n"))

            load_experts(F0, a["f0_ar"])
            for c in range(2):
                load(c, CTX_C0 + c, a["ctxT"][c])
            sp.wait_ge(sem("x_l0"), T + 1)
            sp.dma_start(Bf[:, :], a["f0_b"]).then_inc(sem("ff_in"), 16)
            for c in range(2, KD):
                load(c, CTX_C0 + c, a["ctxT"][c])
            with sp.Fori(0, L1.groups) as g:
                load_group(L1, g, "l1")
            load_experts(F1, a["f1_ar"])
            sp.wait_ge(sem("x_add"), L1.end)
            sp.dma_start(Bf[0:F1.er, :], a["f1_b"]).then_inc(sem("ff_in"), 16)
            with sp.Fori(0, L2.groups) as g:
                load_group(L2, g, "l2")
            load_experts(F2, a["f2_ar"])
            sp.wait_ge(sem("x_add"), L2.end)
            sp.dma_start(Bf[:, :], a["f2_b"]).then_inc(sem("ff_in"), 16)
            with sp.Fori(0, L3.groups) as g:
                load_group(L3, g, "l3")
            sp.wait_ge(sem("bias_add"), T)
            sp.dma_start(bias[:, :], a["f3_bias"].partition_broadcast(P)).then_inc(sem("bias_in"), 16)
            sp.wait_ge(sem("y_mm"), L3.end - T)
            sp.dma_start(packed[:, :, :], a["packed"].rearrange("(t p) c -> p t c", p=P)).then_inc(sem("pk_in"), 16)
            for t in range(T):
                sp.wait_ge(sem("dense_add"), T + t + 1)
                sp.dma_start(a["out"][t * P:(t + 1) * P, :], X[:, t, :]).then_inc(sem("out"), 16)
            sp.wait_ge(sem("out"), 16 * T)

        @block.tensor
        def _(pe):
            prime(pe, "pe")
            pe.sem_inc(sem("even_mm"), 4)
            pe.sem_inc(sem("odd_mm"), 4)
            pe.sem_inc(sem("spread_mm"), 2 * W0)
            pe.sem_inc(sem("windowsum_mm"), 3)
            pe.sem_inc(sem("y_l0"), 1)

            def passes(out, groups):
                n = len(groups)
                for k, (sh, sl, mh, ml) in enumerate(groups):
                    pe.matmul(out, sh, mh, start=(k == 0), stop=False)
                    pe.matmul(out, sh, ml, start=False, stop=False)
                    last = pe.matmul(out, sl, mh, start=False, stop=(k == n - 1))
                return last

            def norm_T(phase, t):
                pe.wait_ge(sem("ln_xn"), phase * T + t + 1)
                if t >= 2:
                    pe.wait_ge(sem("ln_lo"), (phase - 1) * T + t - 1)
                bank = norm_bank(phase, t)
                for k in range(KD):
                    last = pe.transpose(bank[:, k * P:(k + 1) * P], xn[t % 2][:, k * P:(k + 1) * P], ident[:, :])
                last.then_inc(sem("ln_T"), 1)

            def windowed_attention():
                banks = ("q", "kv", "s", "qT", "kT", "pT")
                pe.wait_ge(sem("w0_in"), 16)
                for m in range(3 * T):
                    t = m // 2 if m < 2 * T else m - 2 * T
                    if m >= 6:
                        if m % 2 == 0 or m - 6 >= 2 * T:
                            pe.wait_ge(sem("l0_ev"), (m - 6) // 2 + 1 if m - 6 < 2 * T else m - 5 - T)
                        else:
                            pe.wait_ge(sem("v_ev"), (m - 6) // 2 + 1)
                    if m < 2 * T:
                        if m % 4 == 0:
                            pe.wait_ge(sem(f"ctx_in{t // 2}"), 16)
                        j, moving = 1 + m % 2, ctxn[:, t, :]
                    else:
                        pe.wait_ge(sem("ln_xn"), t + 1)
                        j, moving = 0, xn[t % 2][:, :]
                    pe.matmul(ps[banks[m % 6]][:, :], w0[:, j, :], moving, start=True, stop=True).then_inc(sem("l0_mm"), 1)

                def even(w, h, m):
                    pe.wait_ge(sem("prod"), w * T + (2 * m + 1))
                    if m == 0:
                        pe.wait_ge(sem("dots_ev"), w + 1)
                    pe.matmul(ps[("y", "oT")[h]][:, :], E0[:, 2 * m, :], qk_prod[2 * m][:, :],
                              start=(m == 0), stop=False, skip_group_check=True).then_inc(sem("even_mm"), 1)

                def odd(w, h, m):
                    bank = ps[("y", "oT")[h]]
                    pe.wait_ge(sem("prod_lo"), w * (T // 2) + (m + 1) + 4)
                    pe.matmul(bank[:, :], E0r[:, 2 * m + 1, :], proh[m][:, :], start=False, stop=False, skip_group_check=True)
                    pe.matmul(bank[:, :], E0r[:, 2 * m + 1, :], prol[m][:, :], start=False,
                              stop=(m == T // 2 - 1), skip_group_check=True).then_inc(sem("odd_mm"), 1)

                pe.wait_ge(sem("e_in"), 32)
                pe.wait_ge(sem("e_cast"), 1)
                with pe.Fori(0, W0 // 2) as i:
                    for h in range(2):
                        w = i * 2 + h
                        for m in range(T // 2):
                            even(w, h, m)
                            if m >= 2:
                                odd(w, h, m - 2)
                            elif h == 1:
                                odd(w - 1, 0, m + 2)
                            else:
                                with pe.If(i > 0):
                                    odd(w - 1, 1, m + 2)
                for m in range(2, T // 2):
                    odd(W0 - 1, 1, m)
                pe.wait_ge(sem("dots_ev"), W0 + 2)
                banks = ("q", "kv", "qT", "kT")

                def spread(t, h, u):
                    j = t * W0 + u
                    pe.wait_ge(sem("pv"), j + 1)
                    pe.matmul(ps[banks[u % 4]][:, :], spread_of[h][:, :], eh[:, u, :], start=True, stop=False)
                    pe.matmul(ps[banks[u % 4]][:, :], spread_of[h][:, :], el[:, u, :], start=False,
                              stop=True).then_inc(sem("spread_mm"), 1)

                def windowsum(t, h, k):
                    if k == 0:
                        pe.wait_ge(sem("o_l0"), t + 1)
                    if k % 3 == 2:
                        pe.wait_ge(sem("quad"), t * 2 + (k // 3 + 1))
                    else:
                        pe.wait_ge(sem("pair"), t * (W0 // 2) + (k // 3 * 4 + k % 3 + 5))
                    pe.matmul(ps[("s", "pT")[h]][:, :], ident[:, :], psumd[k % 3][:, :], start=(k == 0),
                              stop=(k == SUMS - 1), skip_group_check=True).then_inc(sem("windowsum_mm"), 1)

                def weight_sum():
                    for w in range(W0):
                        pe.wait_ge(sem(("e_lo", "e_lo_odd")[w % 2]), w // 2 + 1)
                        for part, last in ((eh, False), (el, w == W0 - 1)):
                            ins = pe.matmul(ps["oT"][:, :], ident_r[:, :], part[:, w, :],
                                            start=(w == 0 and part is eh), stop=last)
                    ins.then_inc(sem("e_sum"), 1)

                def rec_spread(t, h):
                    pe.wait_ge(sem("rec_lo"), 1)
                    pe.wait_ge(sem("rspread_ev"), t + 1)
                    pe.matmul(ps["y"][:, :], spread_of[h][:, :], rech[:, :], start=True, stop=False)
                    pe.matmul(ps["y"][:, :], spread_of[h][:, :], recl[:, :], start=False, stop=True)\
                        .then_inc(sem("rspread_mm"), 1)

                def out(t):
                    pe.wait_ge(sem("o_l0"), t + 3)
                    pe.wait_ge(sem("x_l0"), t + 1)
                    pe.matmul(ps["oT"][:, :], w0[:, 3, :], o0[:, :], start=True, stop=True).then_inc(sem("y_l0"), 1)

                pe.wait_ge(sem("e_cast"), 3)
                weight_sum()
                with pe.Fori(0, T // 2) as i:
                    for h in range(2):
                        t = i * 2 + h
                        pe.wait_ge(sem("spread_of"), t + 1)
                        for u in range(W0):
                            spread(t, h, u)
                            if u in SUM_AT:
                                windowsum(t, h, SUM_AT.index(u))
                            elif u + W0 in SUM_AT and h == 1:
                                windowsum(t - 1, 0, SUM_AT.index(u + W0))
                            elif u + W0 in SUM_AT:
                                with pe.If(i > 0):
                                    windowsum(t - 1, 1, SUM_AT.index(u + W0))
                            if u == W0 - 2:
                                rec_spread(t, h)
                            if u == 11 and h == 1:
                                out(t - 1)
                            elif u == 11:
                                with pe.If(i > 0):
                                    out(t - 1)
                for k in (SUMS - 2, SUMS - 1):
                    windowsum(T - 1, 1, k)
                out(T - 1)

            def experts(f, phase, index, x_done):
                xf = index * T
                if f is None:
                    wh, wl, cols, n_dense = WQh[1], WQl[1], 0, T
                else:
                    wh, wl, cols, n_dense = WQh[f.slot], WQl[f.slot], f.cols, 0
                off = D if f is None or f.dense else 0
                products = lambda t, c: [(tile_of(HTh, k, t, 1), tile_of(HTl, k, t, 1), wh[:, k, c], wl[:, k, c])
                                         for k in range(KD)]

                def low_rank(t):
                    if cols:
                        pe.wait_ge(sem("ln_lo"), (phase - 1) * T + t + 1)
                        if t >= 2:
                            pe.wait_ge(sem("lr_ev"), index * T + t - 1)
                        passes(ps[("s", "pT")[t % 2]][:, 0:cols], products(t, slice(off, off + cols)))\
                            .then_inc(sem("lr_mm"), 1)

                def dense(t):
                    if off:
                        pe.wait_ge(sem("ln_lo"), (phase - 1) * T + t + 1)
                        if t >= 2:
                            pe.wait_ge(sem("dense_add"), n_dense + t - 1)
                        elif t == 1:
                            pe.wait_ge(sem("x_add"), x_done)
                        passes(ps[("oT", "y")[t % 2]][:, :], products(t, slice(0, D))).then_inc(sem("dense_mm"), 1)

                def gates_T(h):
                    pe.wait_ge(sem("gated"), 2 * index + h + 1)
                    for j in range(4):
                        last = pe.transpose(ps[("qT", "kT")[h]][0:f.er, j * P:j * P + P],
                                            gated[:, 4 * h + j, 0:f.er], ident[:, :])
                    last.then_inc(sem("gT_mm"), 1)

                def expand(t):
                    pe.wait_ge(sem("gT_ev"), 2 * index + 1 + t // 4)
                    if t >= 2:
                        pe.wait_ge(sem("x_ff"), xf + t - 1)
                    pe.matmul(ps[("oT", "y")[t % 2]][:, :], gT[0:f.er, t, :], Bf[0:f.er, :],
                              start=True, stop=True).then_inc(sem("ff_mm"), 1)

                if f is None:
                    pe.wait_ge(sem("wdq_lo"), KD)
                else:
                    pe.wait_ge(sem("w_lo"), f.c0 + KD)
                for t in range(3):
                    low_rank(t)
                if f is None:
                    dense(0)
                    dense(1)
                norm_T(phase, 4)
                norm_T(phase, 5)
                low_rank(3)
                for t in range(2 if f is None else 0, 4):
                    dense(t)
                for t in range(4, 6):
                    low_rank(t)
                    norm_T(phase, t + 2)
                dense(4)
                dense(5)
                if f is not None:
                    gates_T(0)
                low_rank(6)
                low_rank(7)
                dense(6)
                dense(7)
                if f is None:
                    return
                pe.wait_ge(sem("ff_in"), 16 * (index + 1))
                if f.dense:
                    pe.wait_ge(sem("dense_add"), T)
                for t in range(4):
                    expand(t)
                gates_T(1)
                for t in range(4, T):
                    expand(t)

            def attention(l, phase):
                d, cols = l.d, l.cols

                def project(n, t, slot, g):
                    if t == 0:
                        pe.wait_ge(sem("w_lo"), g * CHUNKS + (l.c0 + KD))
                    pe.wait_ge(sem("ln_lo"), (phase - 1) * T + t + 1)
                    pe.wait_ge(sem("v_lo"), n)
                    pe.wait_ge(sem("hat_k"), n)
                    for j in range(l.tiles):
                        if l.tiles == 2:
                            st_ = lambda H, k: H[:, k, 2 * t + j, :, :].rearrange("p j s -> p (j s)")
                        else:
                            st_ = lambda H, k: tile_of(H, k, t, 0)
                        last = passes(ps["kv"][:, j * 2 * d:(j + 1) * 2 * d],
                                      [(st_(HTh, k), st_(HTl, k), WQh[slot][:, k, HG * d:cols],
                                        WQl[slot][:, k, HG * d:cols]) for k in range(KD)])
                    last.then_inc(sem("kv_mm"), 1)
                    pe.wait_ge(sem("hat"), n)
                    passes(ps["q"][:, 0:HG * d],
                           [(tile_of(HTh, k, t, 1), tile_of(HTl, k, t, 1),
                             WQh[slot][:, k, 0:HG * d], WQl[slot][:, k, 0:HG * d])
                            for k in range(KD)]).then_inc(sem("q_mm"), 1)

                def transpose_qk(n):
                    pe.wait_ge(sem("hat"), n + 1)
                    pe.wait_ge(sem("qT_ev"), n)
                    pe.wait_ge(sem("kT_ev"), n)
                    hat = qkh_of(n)
                    for h in range(HG):
                        pe.transpose(ps["qT"][0:d, h * P:(h + 1) * P], hat[:, h * d:(h + 1) * d], ident[:, :])
                    for j in range(l.tiles):
                        last = pe.transpose(ps["kT"][0:d, j * P:(j + 1) * P],
                                            hat[:, (HG + j) * d:(HG + j + 1) * d], ident[:, :])
                    last.then_inc(sem("qkT_mm"), 1)

                def scores(n):
                    pe.wait_ge(sem("qT_ev"), n + 1)
                    pe.wait_ge(sem("kT_ev"), n + 1)
                    pe.wait_ge(sem("ssub"), n)
                    
                    for hp in range(2):
                        for b in range(NB):
                            c = (hp * NB + b) * l.keys
                            last = pe.matmul(ps["s"][:, c:c + l.keys], qT[0:d, (b * 2 + hp) * P:(b * 2 + hp + 1) * P],
                                             kT[0:d, b * l.keys:(b + 1) * l.keys], start=True, stop=True)
                    last.then_inc(sem("s_mm"), 1)

                def transpose_p(n):
                    pe.wait_ge(sem("prob"), n + 1)
                    pe.wait_ge(sem("pT_lo"), n)
                    if l.tiles == 2:
                        for b in range(NB):
                            for hp in range(2):
                                c = (hp * NB + b) * P
                                last = pe.transpose(ps["pT"][:, (b * 2 + hp) * P:(b * 2 + hp + 1) * P],
                                                    sc[:, c:c + P], ident[:, :])
                    else:
                        for hp in range(2):
                            last = pe.transpose(ps["pT"][:, hp * P:(hp + 1) * P], sc[:, hp * P:(hp + 1) * P],
                                                ident[:, :])
                    last.then_inc(sem("pT_mm"), 1)

                def values(n, v):
                    pe.wait_ge(sem("pT_lo"), n + 1)
                    pe.wait_ge(sem("v_lo"), n + 1)
                    pe.wait_ge(sem("oT_lo"), n)
                    if l.tiles == 2:
                        for b in range(NB):
                            c = slice(b * 2 * P, (b + 1) * 2 * P)
                            last = passes(ps["oT"][0:d, c], [(vh[v][:, b * d:(b + 1) * d], vl[v][:, b * d:(b + 1) * d],
                                                              pTh[:, c], pTl[:, c])])
                    else:
                        last = passes(ps["oT"][0:d, :], [(vh[v][:, 0:d], vl[v][:, 0:d], pTh[:, :], pTl[:, :])])
                    last.then_inc(sem("av_mm"), 1)

                def project_out(n, t, slot, g):
                    if t == 0:
                        pe.wait_ge(sem("w_lo"), g * CHUNKS + (l.c0 + CHUNKS))
                    pe.wait_ge(sem("oT_lo"), n + 1)
                    pe.wait_ge(sem("x_add"), n)
                    passes(ps["y"][:, :], [(oTh[0:d, h * P:(h + 1) * P], oTl[0:d, h * P:(h + 1) * P], WOh[slot][0:d, h, :], WOl[slot][0:d, h, :])
                                           for h in range(HG)]).then_inc(sem("y_mm"), 1)

                slots = [(l.slot0 + h) % 2 for h in range(2)]
                n0 = l.n0
                qkh_of = lambda n: qkh[parity[0]]
                parity = [0]
                for t in range(4):
                    norm_T(phase, t)
                project(n0, 0, slots[0], 0)
                norm_T(phase, 4)
                norm_T(phase, 5)
                project(n0 + 1, 1, slots[0], 0)
                norm_T(phase, 6)
                norm_T(phase, 7)
                transpose_qk(n0)
                pe.wait_ge(sem("ln_lo"), phase * T)
                scores(n0)
                last_i = l.groups // 2 - 1
                with pe.Fori(0, l.groups // 2) as i:
                    for s in range(2 * T):
                        n = i * (2 * T) + (n0 + s)

                        def ahead2():
                            u = (s + 2) % (2 * T)
                            project(n + 2, u % T, slots[u // T], i * 2 + (s + 2) // T)

                        if s >= 2 * T - 2:
                            with pe.If(i < last_i):
                                ahead2()
                            with pe.If(i > last_i - 1):
                                if s == 2 * T - 2:
                                    pe.wait_ge(sem("v_lo"), l.end)
                                    pe.wait_ge(sem("hat"), l.end)
                                for t in range(2):
                                    norm_T(phase + 1, 2 * (s - 2 * T + 2) + t)
                        else:
                            ahead2()
                        parity[0] = (s + 1) % 2
                        if s == 2 * T - 1:
                            with pe.If(i < last_i):
                                transpose_qk(n + 1)
                        else:
                            transpose_qk(n + 1)
                        transpose_p(n)
                        if s == 0:
                            with pe.If(i > 0):
                                project_out(n - 1, T - 1, slots[1], 0)
                        else:
                            project_out(n - 1, (s - 1) % T, slots[(s - 1) // T], i * 2 + (s - 1) // T)
                        if s == 2 * T - 1:
                            with pe.If(i < last_i):
                                scores(n + 1)
                        else:
                            scores(n + 1)
                        values(n, s % 4)
                project_out(l.end - 1, T - 1, slots[1], 0)

            windowed_attention()
            for t in range(4):
                norm_T(1, t)
            experts(F0, 1, 0, 0)
            attention(L1, 2)
            experts(F1, 3, 1, L1.end)
            attention(L2, 4)
            experts(F2, 5, 2, L2.end)
            attention(L3, 6)
            for k in range(KD):
                pe.wait_ge(sem("wdq"), 2)
                bank = ps[("qT", "kT", "s", "pT")[k]]
                wk = wdq[:, :, :, :, :].rearrange("p t g j e -> p t (g j e)")
                for o_ in range(4):
                    last = pe.transpose(bank[:, o_ * P:(o_ + 1) * P], wk[:, o_, k * P:(k + 1) * P], ident[:, :])
                last.then_inc(sem("wdq_T"), 1)
            experts(None, 7, 3, L3.end)

        @block.scalar
        def _(act):
            prime(act, "act")
            act.sem_inc(sem("dots_ev"), 2)
            act.sem_inc(sem("rspread_ev"), 1)
            for h in range(T // 2):
                act.dma_start(X[:, 2 * h:2 * h + 2, :], a["x"][2 * h * P:2 * (h + 1) * P, :].rearrange("(t p) d -> p t d", p=P))\
                    .then_inc(sem(f"x_in{h}"), 16)

            def copy(out, in_):
                return act.activation(out, in_, ACT.Copy)

            def cut_hi(c, k, out, rows, n, src_view=None):
                if isinstance(k, int):
                    act.wait_ge(sem(f"stage{c % 2}"), 16 * (k // 2 + 1))
                else:
                    act.wait_ge(sem(f"stage{c % 2}"), k)
                src = stage[c % 2][0:rows, 0:n]
                if src_view:
                    src = src_view(src)
                copy(out, src).then_inc(sem("w_hi"), 1)

            def cut_experts(f, only=None):
                n = f.cols + (D if f.dense else 0)
                for c in range(KD) if only is None else (only,):
                    cut_hi(c, f.c0 + c, WQh[f.slot][:, c, 0:n], P, n)

            def cut_chunk(l, c, slot, g=None):
                if g is None:
                    k = l.c0 + c
                else:
                    k = g * (8 * CHUNKS) + 16 * ((l.c0 + c) // 2 + 1)
                if c < KD:
                    cut_hi(c, k, WQh[slot][:, c, 0:l.cols], P, l.cols)
                else:
                    cut_hi(c, k, WOh[slot][0:l.d, 2 * (c - KD):2 * (c - KD) + 2, :].rearrange("p h n -> p (h n)"),
                           l.d, STG)

            def norm_x(phase, t):
                act.wait_ge(sem("ln_shift"), 2 * phase + t // 4 + 1)
                if t >= 2:
                    act.wait_ge(sem("ln_T"), (phase - 1) * T + t - 1)
                act.activation(xn[t % 2][:, :], X[:, t, :], ACT.Identity, bias=shift[:, t:t + 1],
                               scale=rstd[:, t:t + 1]).then_inc(sem("ln_xn"), 1)

            def norm_hi(phase, t):
                act.wait_ge(sem("ln_T"), (phase - 1) * T + t + 1)
                copy(HTh[:, :, 2 * t:2 * t + 2, :, 1], norm_bank(phase, t)[:, :].rearrange("p (k b j) -> p k b j", k=KD, b=NB))\
                    .then_inc(sem("ln_hi"), 1)

            def windowed_attention():
                act.wait_ge(sem("b0_in"), 16)
                for m in range(3 * T):
                    t = m // 2 if m < 2 * T else m - 2 * T
                    j = 1 + m % 2 if m < 2 * T else 0
                    if j == 2:
                        continue
                    dst = (q0[:, t, :], K0[:, t, PAD0:PAD0 + D])[j]
                    act.wait_ge(sem("l0_mm"), m + 1)
                    act.activation(dst, ps[("q", "kv", "s", "qT", "kT", "pT")[m % 6]][:, :], ACT.Identity, bias=b0[:, j:j + 1])\
                        .then_inc(sem("l0_ev"), 1)

                act.wait_ge(sem("e_in"), 32)
                copy(E0r[:, :, :], E0[:, :, :]).then_inc(sem("e_cast"), 1)

                def dots_out(w, h):
                    act.wait_ge(sem("odd_mm"), w * (T // 2) + (T // 2 + 4))
                    copy(row(dots, w + 1), ps[("y", "oT")[h]][:, :]).then_inc(sem("dots_ev"), 1)

                with act.Fori(0, W0 // 2) as i:
                    for h in range(2):
                        w = i * 2 + h
                        for m in range(T // 2):
                            act.wait_ge(sem("prod"), w * T + (2 * m + 2))
                            act.wait_ge(sem("odd_mm"), w * (T // 2) + (m + 1))
                            copy(proh[m][:, :], qk_prod[2 * m + 1][:, :]).then_inc(sem("prod_hi"), 1)
                            if m == 2 and h == 1:
                                dots_out(w - 1, 0)
                            elif m == 2:
                                with act.If(i > 0):
                                    dots_out(w - 1, 1)
                dots_out(W0 - 1, 1)
                copy(ETr[:, :, :], ETs[:, :, :]).then_inc(sem("e_cast"), 1)
                act.wait_ge(sem("small_in"), SMALL)
                copy(ident_r[:, :], ident[:, :]).then_inc(sem("e_cast"), 1)
                act.wait_ge(sem("e_cast"), 2)
                with act.Fori(0, W0 // 2) as i:
                    for h in range(2):
                        w = i * 2 + h
                        act.wait_ge(sem("e_sub"), w + 1)
                        act.activation(row(dots, w + 1), row(dots, w + 1), ACT.Exp, scale=float(S // H0) ** -0.5)\
                            .then_inc(sem("e_exp"), 1)
                    for h in range(2):
                        w = i * 2 + h
                        act.wait_ge(sem("e_exp"), w + 1)
                        copy(row(eh, w), row(dots, w + 1)).then_inc(sem("e_hi"), 1)
                with act.Fori(0, T // 2) as i:
                    for h in range(2):
                        t = i * 2 + h
                        act.wait_ge(sem("spread_mm"), t * W0 + W0)
                        copy(spread_of[h][:, :], row(ETr, t)).then_inc(sem("spread_of"), 1)
                        if h == 0:
                            act.wait_ge(sem("rec"), 1)
                            with act.If(i > T // 2 - 2):
                                cut_experts(F0)
                            with act.If(i < 1):
                                copy(rech[:, :], rec[:, :]).then_inc(sem("rec_hi"), 1)
                        act.wait_ge(sem("rspread_mm"), t + 1)
                        act.wait_ge(sem("o_l0"), t + 1)
                        copy(rspread[h][:, :], ps["y"][:, :]).then_inc(sem("rspread_ev"), 1)

            def experts(f, phase, cuts):
                index = (phase - 1) // 2

                def low_rank(t):
                    act.wait_ge(sem("lr_mm"), index * T + t + 1)
                    copy(lr[:, t, 0:f.cols], ps[("s", "pT")[t % 2]][:, 0:f.cols]).then_inc(sem("lr_ev"), 1)

                def gate_exp(h):
                    if index < 2:
                        act.wait_ge(sem("gate_in"), 2 * index + h + 1)
                        act.activation(z2[:, 4 * h:4 * h + 4, 0:f.e], z[:, 4 * h:4 * h + 4, 0:f.e], ACT.Exp)\
                            .then_inc(sem("gate_exp"), 1)

                def gates_T(h):
                    act.wait_ge(sem("gT_mm"), 2 * index + h + 1)
                    copy(gT[0:f.er, 4 * h:4 * h + 4, :].rearrange("p t n -> p (t n)"),
                         ps[("qT", "kT")[h]][0:f.er, :]).then_inc(sem("gT_ev"), 1)

                def cut_some(place):
                    for cut_one in cuts[place]:
                        cut_one()

                low_rank(0)
                low_rank(1)
                norm_x(phase, 4)
                norm_x(phase, 5)
                low_rank(2)
                norm_hi(phase, 4)
                norm_hi(phase, 5)
                low_rank(3)
                norm_x(phase, 6)
                norm_x(phase, 7)
                gate_exp(0)
                cut_some(0)
                for t in range(4, 6):
                    low_rank(t)
                    norm_hi(phase, t + 2)
                gates_T(0)
                low_rank(6)
                low_rank(7)
                gate_exp(1)
                cut_some(1)
                gates_T(1)
                cut_some(2)
                norm_x(phase + 1, 0)
                norm_x(phase + 1, 1)
                for t in range(4):
                    norm_hi(phase + 1, t)
                    norm_x(phase + 1, t + 2)
                    if t == 1:
                        cut_some(3)

            def attention(l, f, phase, cuts=()):
                d = l.d

                def v_and_squares(n, v):
                    act.wait_ge(sem("kv_mm"), n + 1)
                    act.wait_ge(sem("av_mm"), n - 3)
                    kv = ps["kv"][:, 0:l.tiles * 2 * d].rearrange("p (j c) -> p j c", j=l.tiles)
                    if l.norm_eps is not None:
                        act.wait_ge(sem("sumsq"), n - NORM0)
                        act.activation(sq[:, HG * d:(HG + l.tiles) * d].rearrange("p (j c) -> p j c", j=l.tiles),
                                       kv[:, :, 0:d], ACT.Square)
                    copy(vh[v][:, 0:l.tiles * d].rearrange("p (j c) -> p j c", j=l.tiles), kv[:, :, d:2 * d])\
                        .then_inc(sem("v_hi"), 1)
                    if l.norm_eps is not None:
                        act.wait_ge(sem("q_mm"), n + 1)
                        act.activation(sq[:, 0:HG * d], ps["q"][:, 0:HG * d], ACT.Square).then_inc(sem("squared"), 1)

                def qT_out(n):
                    act.wait_ge(sem("qkT_mm"), n + 1)
                    act.wait_ge(sem("s_mm"), n)
                    copy(qT[0:d, :].rearrange("p (b h q) -> p h b q", b=NB, h=HG),
                         ps["qT"][0:d, :].rearrange("p (h b q) -> p h b q", h=HG, b=NB)).then_inc(sem("qT_ev"), 1)

                def exps(n):
                    act.wait_ge(sem("ssub"), n + 1)
                    act.activation(sc[:, 0:4 * l.keys], sc[:, 0:4 * l.keys], ACT.Exp,
                                   scale=1.0 if l.masked else l.scale).then_inc(sem("exp"), 1)

                def pT_out(n):
                    act.wait_ge(sem("pT_mm"), n + 1)
                    act.wait_ge(sem("av_mm"), n)
                    if l.tiles == 2:
                        copy(pTh[:, :], ps["pT"][:, :]).then_inc(sem("pT_hi"), 1)
                    else:
                        for b in range(NB):
                            last = copy(pTh[b * S:(b + 1) * S, b * 2 * P:(b + 1) * 2 * P],
                                        block_of(b))
                        last.then_inc(sem("pT_hi"), 1)

                def block_of(b):
                    return ps["pT"][b * S:(b + 1) * S, 0:2 * P]

                by_head = lambda v: v[0:d, :].rearrange("p (h b q) -> p b h q", h=HG, b=NB)
                from_batch = lambda v: v[0:d, :].rearrange("p (b h q) -> p b h q", b=NB, h=HG)

                def oT_out(n):
                    act.wait_ge(sem("av_mm"), n + 1)
                    act.wait_ge(sem("y_mm"), n)
                    copy(by_head(oTh), from_batch(ps["oT"])).then_inc(sem("oT_hi"), 1)

                slots = [(l.slot0 + h) % 2 for h in range(2)]
                n0 = l.n0
                v_and_squares(n0, 0)
                norm_hi(phase, 4)
                norm_x(phase, 6)
                norm_hi(phase, 5)
                norm_x(phase, 7)
                v_and_squares(n0 + 1, 1)
                norm_hi(phase, 6)
                norm_hi(phase, 7)
                qT_out(n0)
                for cut_one in cuts:
                    cut_one()
                last_i = l.groups // 2 - 1
                with act.Fori(0, l.groups // 2) as i:
                    for s in range(2 * T):
                        n = i * (2 * T) + (n0 + s)
                        if s == 0:
                            with act.If(i > 0):
                                oT_out(n - 1)
                        else:
                            oT_out(n - 1)
                        exps(n)
                        if s >= 2 * T - 2:
                            with act.If(i < last_i):
                                v_and_squares(n + 2, (s + 2) % 4)
                            with act.If(i > last_i - 1):
                                for t in range(2):
                                    norm_hi(phase + 1, 2 * (s - 2 * T + 2) + t)
                        else:
                            v_and_squares(n + 2, (s + 2) % 4)
                        if s == 2 * T - 1:
                            with act.If(i < last_i):
                                qT_out(n + 1)
                        else:
                            qT_out(n + 1)
                        pT_out(n)
                        c = s % T - 1
                        if 0 <= c < CHUNKS:
                            slot = slots[(s // T + 1) % 2]
                            if s < T:
                                act.wait_ge(sem("y_mm"), n - 1)
                                cut_chunk(l, c, slot, i * 2 + 1)
                            else:
                                with act.If(i < last_i):
                                    act.wait_ge(sem("y_mm"), n - 1)
                                    cut_chunk(l, c, slot, i * 2 + 2)
                                if c < KD and f is not None:
                                    with act.If(i > last_i - 1):
                                        act.wait_ge(sem("y_mm"), n - 1)
                                        cut_experts(f, c)
                        if s in (2 * T - 3, 2 * T - 2):
                            with act.If(i > last_i - 1):
                                for t in range(2):
                                    norm_x(phase + 1, 2 * (s - 2 * T + 3) + t)
                oT_out(l.end - 1)

            def cuts_of(l, places):
                c, out = 0, []
                for n in places:
                    out.append([(lambda k=k: cut_chunk(l, k, l.slot0)) for k in range(c, c + n)])
                    c += n
                return out

            def cut_ctx(c):
                cut_hi(c, CTX_C0 + c, HTh[:, c, :, :, 0], P, STG, lambda v: v.rearrange("p (b j) -> p b j", b=B))

            windowed_attention()
            norm_x(1, 0)
            norm_x(1, 1)
            for t in range(4):
                norm_hi(1, t)
                if t < 2:
                    norm_x(1, t + 2)
            act.wait_ge(sem("x_l0"), T + 1)
            cuts = cuts_of(L1, (0, 0, 2, 2, 2))
            cuts[0] = [lambda: cut_ctx(0), lambda: cut_ctx(1)]
            cuts[1] = [lambda: cut_ctx(2), lambda: cut_ctx(3)]
            experts(F0, 1, cuts)
            attention(L1, F1, 2, cuts[4])
            experts(F1, 3, cuts_of(L2, (2, 2, 2, 0)))
            attention(L2, F2, 4)
            experts(F2, 5, cuts_of(L3, (2, 2, 2, 0)))
            attention(L3, None, 6)
            for k in range(KD):
                act.wait_ge(sem("wdq_T"), k + 1)
                copy(WQh[1][:, k, 0:D], ps[("qT", "kT", "s", "pT")[k]][:, :]).then_inc(sem("wdq_hi"), 1)
            norm_x(7, 4)
            norm_x(7, 5)
            for t in range(4, T):
                norm_hi(7, t)
                if t + 2 < T:
                    norm_x(7, t + 2)

        @block.gpsimd
        def _(pool):
            prime(pool, "pool")
            pool.sem_inc(sem("pair"), 4)
            pool.sem_inc(sem("prod_lo"), 4)
            pool.memset(mhalf[:, :], -0.5).then_inc(sem("mhalf"), 1)
            pool.wait_ge(sem("mhalf"), 1)

            def sub(out, in0, in1):
                return pool.tensor_tensor(out, in0, in1, ALU.subtract)

            def cut_lo(c, k, out, hi, rows, n, src_view=None):
                pool.wait_ge(sem("w_hi"), k + 1)
                src = stage[c % 2][0:rows, 0:n]
                if src_view:
                    src = src_view(src)
                sub(out, src, hi.bitcast(F32)).then_inc(sem("w_lo"), 1)

            def cut_experts(f, chunks=range(KD)):
                n = f.cols + (D if f.dense else 0)
                for c in chunks:
                    cut_lo(c, f.c0 + c, WQl[f.slot][:, c, 0:n], WQh[f.slot][:, c, 0:n], P, n)

            def cut_chunk(l, c, slot, g=0):
                k = g * CHUNKS + (l.c0 + c)
                if c < KD:
                    cut_lo(c, k, WQl[slot][:, c, 0:l.cols], WQh[slot][:, c, 0:l.cols], P, l.cols)
                else:
                    v = [w[slot][0:l.d, 2 * (c - KD):2 * (c - KD) + 2, :].rearrange("p h n -> p (h n)")
                         for w in (WOl, WOh)]
                    cut_lo(c, k, v[0], v[1], l.d, STG)

            def norm_rstd(phase, h):
                tt = slice(4 * h, 4 * h + 4)
                pool.wait_ge(sem("ln_mv"), phase * T + 4 * h + 4)
                if phase:
                    pool.wait_ge(sem("ln_xn"), (phase - 1) * T + 4 * h + 4)
                pool.tensor_scalar(ve[:, tt], mv[:, tt, 1], LNEPS, None, ALU.add).then_inc(sem("ln_ve"), 1)
                pool.tensor_scalar(mneg[:, tt], mv[:, tt, 0], -1.0, None, ALU.mult).then_inc(sem("ln_ve"), 1)
                pool.wait_ge(sem("ln_ve"), 4 * phase + 2 * h + 2)
                pool.tensor_tensor(rstd[:, tt], ve[:, tt], mhalf[:, 0:4], ALU.pow).then_inc(sem("ln_rstd"), 1)
                pool.wait_ge(sem("ln_rstd"), 2 * phase + h + 1)
                pool.tensor_tensor(shift[:, tt], mneg[:, tt], rstd[:, tt], ALU.mult).then_inc(sem("ln_shift"), 1)

            def attention(l, f, phase):
                def norms(n):
                    k = HG + l.tiles
                    m = n - NORM0
                    pool.wait_ge(sem("meansq"), m + 1)
                    pool.wait_ge(sem("hat"), n)
                    pool.tensor_tensor(rs[:, 0:k], ms[:, 0:k], mhalf[:, 0:k], ALU.pow).then_inc(sem("rnorm"), 1)

                slots = [(l.slot0 + h) % 2 for h in range(2)]
                if l.norm_eps is not None:
                    norms(l.n0)
                    norms(l.n0 + 1)
                last_i = l.groups // 2 - 1
                with pool.Fori(0, l.groups // 2) as i:
                    for s in range(2 * T):
                        n = i * (2 * T) + (l.n0 + s)
                        if l.norm_eps is not None:
                            if s >= 2 * T - 2:
                                with pool.If(i < last_i):
                                    norms(n + 2)
                            else:
                                norms(n + 2)
                        c = s % T - 1
                        if 0 <= c < CHUNKS:
                            slot = slots[(s // T + 1) % 2]
                            if s < T:
                                cut_chunk(l, c, slot, i * 2 + 1)
                            else:
                                with pool.If(i < last_i):
                                    cut_chunk(l, c, slot, i * 2 + 2)
                                if c < KD and f is not None:
                                    with pool.If(i > last_i - 1):
                                        cut_experts(f, (c,))
                        if s == 2 * T - 4:
                            with pool.If(i > last_i - 1):
                                norm_rstd(phase + 1, 0)
                norm_rstd(phase + 1, 1)

            def add_bias(phase, tiles):
                for t in tiles:
                    pool.wait_ge(sem("ln_xn"), phase * T + t + 1)
                    pool.tensor_tensor(X[:, t, :], X[:, t, :], bias[:, :], ALU.add).then_inc(sem("bias_add"), 1)

            norm_rstd(0, 0)
            norm_rstd(0, 1)
            with pool.Fori(0, W0) as w:
                for m in range(T // 2):
                    pool.wait_ge(sem("prod_hi"), w * (T // 2) + (m + 1))
                    sub(prol[m][:, :], qk_prod[2 * m + 1][:, :], proh[m][:, :].bitcast(F32)).then_inc(sem("prod_lo"), 1)
            with pool.Fori(0, W0 // 2) as i:
                pool.wait_ge(sem("e_hi"), i * 2 + 1)
                sub(row(el, i * 2), row(dots, i * 2 + 1), row(eh, i * 2).bitcast(F32)).then_inc(sem("e_lo"), 1)
            def pairs(first, end):
                with pool.Fori(first, end) as i:
                    for h in range(4):
                        k = i * 4 + h
                        pool.wait_ge(sem("pv"), k * 2 + 6)
                        pool.wait_ge(sem("windowsum_mm"), i * 3 + min(h + 1, 3))
                        pool.tensor_tensor(psumd[h][:, :], pv_prod[2 * h][:, :], pv_prod[2 * h + 1][:, :], ALU.add)\
                            .then_inc(sem("pair"), 1)
                    pool.wait_ge(sem("pair"), i * 4 + 8)
                    pool.tensor_tensor(psumd[2][:, :], psumd[2][:, :], psumd[3][:, :], ALU.add).then_inc(sem("quad"), 1)

            pairs(0, 12)
            cut_experts(F0, (0, 1))
            pairs(12, 14)
            cut_experts(F0, (2, 3))
            pairs(14, 16)
            norm_rstd(1, 0)
            norm_rstd(1, 1)

            def cut_ctx(c):
                cut_lo(c, CTX_C0 + c, HTl[:, c, :, :, 0], HTh[:, c, :, :, 0], P, STG,
                       lambda x: x.rearrange("p (b j) -> p b j", b=B))

            def cut_first(l, chunks):
                for c in chunks:
                    cut_chunk(l, c, l.slot0)

            for c in range(KD):
                cut_ctx(c)
            norm_rstd(2, 0)
            cut_first(L1, (0, 1))
            norm_rstd(2, 1)
            cut_first(L1, (2, 3, 4, 5))
            attention(L1, F1, 2)
            cut_first(L2, (0, 1, 2, 3))
            norm_rstd(4, 0)
            cut_first(L2, (4,))
            norm_rstd(4, 1)
            cut_first(L2, (5,))
            attention(L2, F2, 4)
            add_bias(5, range(4))
            cut_first(L3, (0, 1))
            add_bias(5, range(4, T))
            cut_first(L3, (2, 3))
            norm_rstd(6, 0)
            cut_first(L3, (4,))
            norm_rstd(6, 1)
            cut_first(L3, (5,))
            attention(L3, None, 6)
            pool.wait_ge(sem("bias_in"), 16)
            add_bias(7, range(T))

        @block.vector
        def _(dve):
            prime(dve, "dve")
            dve.sem_inc(sem("pv"), 4)
            dve.sem_inc(sem("o_l0"), 2)
            dve.sem_inc(sem("x_l0"), 1)
            links = [0]

            def link(ins):
                links[0] += 1
                ins.then_inc(sem("dve_link"), 1)
                dve.wait_ge(sem("dve_link"), links[0])

            def sub(out, in0, in1):
                return dve.tensor_tensor(out, in0, in1, ALU.subtract)

            def stats(t):
                dve.bn_stats(st[:, t, :], X[:, t, :]).then_inc(sem("ln_st"), 1)

            def mean_var(phase, h):
                for t in range(4 * h, 4 * h + 4):
                    dve.wait_ge(sem("ln_st"), phase * T + t + 1)
                    dve.bn_aggr(mv[:, t, :], st[:, t, :]).then_inc(sem("ln_mv"), 1)

            def norm_lo(phase, t):
                dve.wait_ge(sem("ln_hi"), (phase - 1) * T + t + 1)
                sub(HTl[:, :, 2 * t:2 * t + 2, :, 1], norm_bank(phase, t)[:, :].rearrange("p (k b j) -> p k b j", k=KD, b=NB),
                    HTh[:, :, 2 * t:2 * t + 2, :, 1].bitcast(F32)).then_inc(sem("ln_lo"), 1)

            def windowed_attention():
                for pad in (K0, V0):
                    dve.memset(pad[:, :, 0:PAD0], 0.0)
                    dve.memset(pad[:, :, PAD0 + D:KW], 0.0).then_inc(sem("pads"), 1)
                dve.memset(mx0[:, :], -3.0e38).then_inc(sem("max_l0"), 1)
                dve.wait_ge(sem("b0_in"), 16)

                def v_out(t):
                    dve.wait_ge(sem("l0_mm"), 2 * t + 2)
                    dve.tensor_scalar(V0[:, t, PAD0:PAD0 + D], ps[("q", "kv", "s", "qT", "kT", "pT")[(2 * t + 1) % 6]][:, :],
                                      b0[:, 2:3], None, ALU.add).then_inc(sem("v_ev"), 1)

                for h in range(2):
                    for t in range(4 * h, 4 * h + 4):
                        v_out(t)
                        dve.wait_ge(sem(f"x_in{t // 2}"), 16)
                        stats(t)
                    mean_var(0, h)
                for t in range(T):
                    dve.wait_ge(sem("ln_shift"), t // 4 + 1)
                    if t >= 2:
                        dve.wait_ge(sem("l0_mm"), 2 * T + t - 1)
                    dve.tensor_scalar(xn[t % 2][:, :], X[:, t, :], mv[:, t, 0:1], rstd[:, t:t + 1],
                                      ALU.subtract, ALU.mult).then_inc(sem("ln_xn"), 1)
                dve.wait_ge(sem("pads"), 2)
                dve.wait_ge(sem("l0_ev"), 2 * T)

                def running_max(w):
                    dve.wait_ge(sem("dots_ev"), w + 3)
                    dve.wait_ge(sem("max_l0"), w + 1)
                    dve.tensor_tensor(mx0[:, :], mx0[:, :], row(dots, w + 1), ALU.max).then_inc(sem("max_l0"), 1)

                with dve.Fori(0, W0 // 2) as i:
                    for h in range(2):
                        w = i * 2 + h
                        for t in range(T):
                            dve.wait_ge(sem(("even_mm", "prod_lo")[t % 2]), w * (T // 2) + (t // 2 + 1))
                            dve.tensor_tensor(qk_prod[t][:, :], q0[:, t, :], K0[:, t, bass.ds(w, D)],
                                              ALU.mult).then_inc(sem("prod"), 1)
                        if h == 1:
                            running_max(w - 1)
                        else:
                            with dve.If(i > 0):
                                running_max(w - 1)
                dve.wait_ge(sem("dots_ev"), W0 + 2)
                dve.wait_ge(sem("max_l0"), W0)
                dve.tensor_tensor(mx0[:, :], mx0[:, :], dots[:, W0, :], ALU.max).then_inc(sem("max_l0"), 1)
                dve.wait_ge(sem("max_l0"), W0 + 1)
                for w in range(W0):
                    sub(dots[:, w + 1, :], dots[:, w + 1, :], mx0[:, :]).then_inc(sem("e_sub"), 1)
                for w in range(1, W0, 2):
                    dve.wait_ge(sem("e_hi"), w + 1)
                    sub(el[:, w, :], dots[:, w + 1, :], eh[:, w, :].bitcast(F32)).then_inc(sem("e_lo_odd"), 1)
                banks = ("q", "kv", "qT", "kT")

                def weighted(t, u):
                    j = t * W0 + u
                    dve.wait_ge(sem("spread_mm"), j + (1 + 2 * W0))
                    dve.wait_ge(sem("pair"), t * (W0 // 2) + (u // 2 + 1))
                    dve.tensor_tensor(pv_prod[u % 8][:, :], ps[banks[u % 4]][:, :],
                                      V0[:, bass.ds(t, 1), u:u + D].rearrange("p a b -> p (a b)"), ALU.mult)\
                        .then_inc(sem("pv"), 1)

                def over_sum(t, h):
                    dve.wait_ge(sem("windowsum_mm"), t * SUMS + (SUMS + 3))
                    dve.wait_ge(sem("rspread_ev"), t + 2)
                    dve.wait_ge(sem("y_l0"), t + 1)
                    dve.tensor_tensor(o0[:, :], ps[("s", "pT")[h]][:, :], rspread[h][:, :], ALU.mult)\
                        .then_inc(sem("o_l0"), 1)

                def x_update(t):
                    dve.wait_ge(sem("y_l0"), t + 2)
                    dve.scalar_tensor_tensor(row(X, t), ps["oT"][:, :], b0[:, 3:4], row(X, t), ALU.add, ALU.add)\
                        .then_inc(sem("x_l0"), 1)

                def stats_l0(t):
                    dve.wait_ge(sem("x_l0"), t + 2)
                    dve.bn_stats(row(st, t), row(X, t)).then_inc(sem("ln_st"), 1)

                with dve.Fori(0, T // 2) as i:
                    for h in range(2):
                        t = i * 2 + h
                        for u in range(W0):
                            weighted(t, u)
                            for at_, step in ((7, lambda v: over_sum(v, 1 - h)), (12, x_update), (14, stats_l0)):
                                if u == at_ and h == 1:
                                    step(t - 1)
                                elif u == at_:
                                    with dve.If(i > 0):
                                        step(nc.s_assert_within(t - 1, 0, T - 1, skip_runtime_bounds_check_because="i > 0 in here"))
                            if u == 6 and h == 0:
                                with dve.If(i < 1):
                                    dve.wait_ge(sem("e_sum"), 1)
                                    dve.reciprocal(rec[:, :], ps["oT"][:, :]).then_inc(sem("rec"), 1)
                                    dve.wait_ge(sem("rec_hi"), 1)
                                    sub(recl[:, :], rec[:, :], rech[:, :].bitcast(F32)).then_inc(sem("rec_lo"), 1)
                mean_var(1, 0)
                over_sum(T - 1, 1)
                x_update(T - 1)
                stats_l0(T - 1)
                mean_var(1, 1)

            def gating(f, index, h, meanwhile=lambda: None):
                e = f.e
                tt = slice(4 * h, 4 * h + 4)
                dve.wait_ge(sem("lr_ev"), index * T + 4 * h + 4)
                if index == 0:
                    dve.wait_ge(sem("small_in"), SMALL)
                logits = lr[:, tt, f.er:f.er + e]
                over_e = lambda v: v[:, tt].unsqueeze(2).to_broadcast([P, 4, e])
                zv, ev, wv, gv = z[:, tt, 0:e], z2[:, tt, 0:e], z3[:, tt, 0:e], gates[:, tt, 0:e]
                pv, qv = pair[:, tt, 0:e, 0:e], pair2[:, tt, :, :]
                r1, s1, t1 = zr[:, tt], zs[:, tt], zt[:, tt]
                as_j = lambda v: v.unsqueeze(2).to_broadcast([P, 4, e, e])
                as_e = lambda v: v.unsqueeze(3).to_broadcast([P, 4, e, e])
                if index != 1:
                    link(dve.tensor_tensor(zv, logits, rb[index // 2][:, 0:e].unsqueeze(1).to_broadcast([P, 4, e]), ALU.add))
                if index == 0:
                    link(dve.tensor_reduce(r1, zv, AX.X, ALU.max))
                    sub(zv, zv, over_e(zr)).then_inc(sem("gate_in"), 1)
                    meanwhile()
                    dve.wait_ge(sem("gate_exp"), h + 1)
                    link(dve.tensor_reduce(s1, ev, AX.X, ALU.add))
                    link(dve.reciprocal(t1, s1))
                    link(dve.scalar_tensor_tensor(gv, ev, e * 32.0 / 16.0, over_e(zt), ALU.mult, ALU.mult))
                elif index == 1:
                    link(dve.tensor_reduce(r1, logits, AX.X, ALU.max))
                    sub(zv, logits, over_e(zr)).then_inc(sem("gate_in"), 1)
                    dve.tensor_tensor(pv, as_j(logits), as_e(logits), ALU.is_gt)
                    link(dve.tensor_tensor(qv, as_j(logits), as_e(logits), ALU.is_equal))
                    link(dve.tensor_tensor(qv, qv,
                                           tri[:, :].rearrange("p (a b) -> p a b", a=e).unsqueeze(1).to_broadcast([P, 4, e, e]),
                                           ALU.mult))
                    link(dve.tensor_tensor(pv, pv, qv, ALU.add))
                    link(dve.tensor_reduce(wv, pv, AX.X, ALU.add))
                    meanwhile()
                    dve.wait_ge(sem("gate_exp"), 2 + h + 1)
                    link(dve.scalar_tensor_tensor(ev, wv, 1.5, ev, ALU.is_lt, ALU.mult))
                    link(dve.tensor_reduce(s1, ev, AX.X, ALU.add))
                    link(dve.reciprocal(t1, s1))
                    link(dve.scalar_tensor_tensor(gv, ev, 4.0, over_e(zt), ALU.mult, ALU.mult))
                else:
                    link(dve.tensor_tensor(pv, as_j(zv), as_e(zv), ALU.subtract))
                    link(dve.tensor_scalar(pv, pv, 0.0, None, ALU.max))
                    link(dve.tensor_reduce(wv, pv, AX.X, ALU.add))
                    link(dve.tensor_scalar(wv, wv, 1.0, None, ALU.is_lt))
                    dve.tensor_reduce(r1, wv, AX.X, ALU.add)
                    link(dve.tensor_tensor(ev, wv, zv, ALU.mult))
                    link(dve.tensor_reduce(s1, ev, AX.X, ALU.add))
                    link(dve.reciprocal(t1, r1))
                    link(dve.scalar_tensor_tensor(s1, s1, -1.0, t1, ALU.add, ALU.mult))
                    link(dve.tensor_tensor(ev, zv, over_e(zs), ALU.subtract))
                    link(dve.tensor_scalar(gv, ev, 0.0, None, ALU.max))
                dve.tensor_tensor(gated[:, tt, 0:f.er].rearrange("p t (e r) -> p t e r", e=e),
                                  lr[:, tt, 0:f.er].rearrange("p t (e r) -> p t e r", e=e),
                                  gv.unsqueeze(3).to_broadcast([P, 4, e, f.r]), ALU.mult).then_inc(sem("gated"), 1)

            def dense_add(n_dense, tiles):
                for t in tiles:
                    dve.wait_ge(sem("dense_mm"), n_dense + t + 1)
                    dve.wait_ge(sem("bias_add"), n_dense + t + 1)
                    dve.tensor_tensor(X[:, t, :], X[:, t, :], ps[("oT", "y")[t % 2]][:, :], ALU.add)\
                        .then_inc(sem("dense_add"), 1)

            def experts(f, phase):
                index = (phase - 1) // 2
                dense = (lambda *tiles: dense_add(0, tiles)) if f.dense else (lambda *tiles: None)

                def x_update(t):
                    dve.wait_ge(sem("ff_mm"), index * T + t + 1)
                    dve.tensor_tensor(X[:, t, :], X[:, t, :], ps[("oT", "y")[t % 2]][:, :], ALU.add)\
                        .then_inc(sem("x_ff"), 1)

                def x_stats(t):
                    dve.wait_ge(sem("x_ff"), index * T + t + 1)
                    stats(t)

                def first_two():
                    x_update(0)
                    x_update(1)

                norm_lo(phase, 4)
                norm_lo(phase, 5)
                gating(f, index, 0)
                dense(0, 1, 2, 3)
                norm_lo(phase, 6)
                norm_lo(phase, 7)
                dense(4, 5)
                if f.dense:
                    gating(f, index, 1)
                    dense(6, 7)
                    dve.wait_ge(sem("dense_add"), T)
                    first_two()
                else:
                    gating(f, index, 1, first_two)
                x_update(2)
                x_stats(0)
                x_update(3)
                x_stats(1)
                x_stats(2)
                x_stats(3)
                mean_var(phase + 1, 0)
                x_update(4)
                x_update(5)
                x_stats(4)
                x_update(6)
                x_stats(5)
                x_update(7)
                x_stats(6)
                x_stats(7)
                mean_var(phase + 1, 1)
                for t in range(4):
                    norm_lo(phase + 1, t)

            def attention(l, norm_w, phase, dequantise=None):
                d, keys = l.d, l.keys
                nq = HG + l.tiles

                def v_rest(n, v):
                    dve.wait_ge(sem("v_hi"), n + 1)
                    kv = ps["kv"][:, 0:l.tiles * 2 * d].rearrange("p (j c) -> p j c", j=l.tiles)
                    sub(vl[v][:, 0:l.tiles * d].rearrange("p (j c) -> p j c", j=l.tiles), kv[:, :, d:2 * d],
                        vh[v][:, 0:l.tiles * d].rearrange("p (j c) -> p j c", j=l.tiles).bitcast(F32))\
                        .then_inc(sem("v_lo"), 1)

                def sum_squares(n):
                    if l.norm_eps is None:
                        return
                    m = n - NORM0
                    dve.wait_ge(sem("squared"), m + 1)
                    dve.tensor_reduce(ss[:, 0:nq], sq[:, 0:nq * d].rearrange("p (h c) -> p h c", h=nq), AX.X, ALU.add)\
                        .then_inc(sem("sumsq"), 1)
                    dve.wait_ge(sem("sumsq"), m + 1)
                    dve.wait_ge(sem("rnorm"), m)
                    dve.tensor_scalar(ms[:, 0:nq], ss[:, 0:nq], 1.0 / d, l.norm_eps, ALU.mult, ALU.add)\
                        .then_inc(sem("meansq"), 1)

                def hats(n, p):
                    dve.wait_ge(sem("kv_mm"), n + 1)
                    dve.wait_ge(sem("q_mm"), n + 1)
                    dve.wait_ge(sem("qkT_mm"), n - 1)
                    kv = ps["kv"][:, 0:l.tiles * 2 * d].rearrange("p (j c) -> p j c", j=l.tiles)[:, :, 0:d]
                    k_out = qkh[p][:, HG * d:nq * d].rearrange("p (j c) -> p j c", j=l.tiles)
                    if l.norm_eps is None:
                        dve.tensor_copy(k_out, kv).then_inc(sem("hat_k"), 1)
                        dve.tensor_copy(qkh[p][:, 0:HG * d], ps["q"][:, 0:HG * d]).then_inc(sem("hat"), 1)
                    else:
                        dve.wait_ge(sem("rnorm"), n - NORM0 + 1)
                        dve.tensor_tensor(k_out, kv, rs[:, HG:nq].unsqueeze(2).to_broadcast([P, l.tiles, d]), ALU.mult)\
                            .then_inc(sem("hat_k"), 1)
                        dve.tensor_tensor(qkh[p][:, 0:HG * d].rearrange("p (h c) -> p h c", h=HG),
                                          ps["q"][:, 0:HG * d].rearrange("p (h c) -> p h c", h=HG),
                                          rs[:, 0:HG].unsqueeze(2).to_broadcast([P, HG, d]), ALU.mult)\
                            .then_inc(sem("hat"), 1)

                def kT_out(n):
                    dve.wait_ge(sem("qkT_mm"), n + 1)
                    dve.wait_ge(sem("s_mm"), n)
                    src = ps["kT"][0:d, 0:l.tiles * P]
                    if norm_w is None:
                        dve.tensor_copy(kT[0:d, 0:l.tiles * P], src).then_inc(sem("kT_ev"), 1)
                    else:
                        dve.tensor_scalar(kT[0:d, 0:l.tiles * P], src, norm_w, None, ALU.mult).then_inc(sem("kT_ev"), 1)

                s3 = sc[:, 0:4 * keys].rearrange("p (g k) -> p g k", g=4)
                p3 = ps["s"][:, 0:4 * keys].rearrange("p (g k) -> p g k", g=4)
                over_k = lambda v: v[:, :].unsqueeze(2).to_broadcast([P, 4, keys])

                def score_rest(n):
                    dve.wait_ge(sem("s_mm"), n + 1)
                    dve.wait_ge(sem("pT_mm"), n)
                    if l.masked:
                        dve.scalar_tensor_tensor(s3, p3, l.scale, mask[:, :].unsqueeze(1).to_broadcast([P, 4, keys]),
                                                 ALU.mult, ALU.add).then_inc(sem("masked"), 1)
                        dve.wait_ge(sem("masked"), n - l.n0 + 1)
                        src = s3
                    else:
                        src = p3
                    dve.tensor_reduce(smx[:, :], src, AX.X, ALU.max).then_inc(sem("smax"), 1)
                    dve.wait_ge(sem("smax"), n + 1)
                    sub(s3, src, over_k(smx)).then_inc(sem("ssub"), 1)

                def probs(n):
                    dve.wait_ge(sem("exp"), n + 1)
                    dve.tensor_reduce(ssum[:, :], s3, AX.X, ALU.add).then_inc(sem("ssum"), 1)
                    dve.wait_ge(sem("ssum"), n + 1)
                    dve.reciprocal(srec[:, :], ssum[:, :]).then_inc(sem("srec"), 1)
                    dve.wait_ge(sem("srec"), n + 1)
                    dve.tensor_tensor(s3, s3, over_k(srec), ALU.mult).then_inc(sem("prob"), 1)

                def pT_rest(n):
                    dve.wait_ge(sem("pT_hi"), n + 1)
                    if l.tiles == 2:
                        sub(pTl[:, :], ps["pT"][:, :], pTh[:, :].bitcast(F32)).then_inc(sem("pT_lo"), 1)
                    else:
                        for b in range(NB):
                            c = slice(b * 2 * P, (b + 1) * 2 * P)
                            r = slice(b * S, (b + 1) * S)
                            last = sub(pTl[r, c], ps["pT"][r, 0:2 * P], pTh[r, c].bitcast(F32))
                        last.then_inc(sem("pT_lo"), 1)

                by_head = lambda v: v[0:d, :].rearrange("p (h b q) -> p b h q", h=HG, b=NB)
                from_batch = lambda v: v[0:d, :].rearrange("p (b h q) -> p b h q", b=NB, h=HG)

                def oT_rest(n):
                    dve.wait_ge(sem("oT_hi"), n + 1)
                    sub(by_head(oTl), from_batch(ps["oT"]), by_head(oTh).bitcast(F32)).then_inc(sem("oT_lo"), 1)

                def x_update(n, t):
                    dve.wait_ge(sem("y_mm"), n + 1)
                    dve.tensor_tensor(X[:, t, :], X[:, t, :], ps["y"][:, :], ALU.add).then_inc(sem("x_add"), 1)

                n0 = l.n0
                if l.tiles == 1:
                    for v in (pTh, pTl):
                        for b in range(NB):
                            dve.memset(v[b * S:(b + 1) * S, (1 - b) * 2 * P:(2 - b) * 2 * P].bitcast(F32), 0.0)
                for k in range(2):
                    v_rest(n0 + k, k)
                    sum_squares(n0 + k)
                    hats(n0 + k, k)
                    norm_lo(phase, 4 + 2 * k)
                    norm_lo(phase, 5 + 2 * k)
                kT_out(n0)
                last_i = l.groups // 2 - 1
                with dve.Fori(0, l.groups // 2) as i:
                    for s in range(2 * T):
                        n = i * (2 * T) + (n0 + s)
                        score_rest(n)
                        if s == 0:
                            with dve.If(i > 0):
                                oT_rest(n - 1)
                        else:
                            oT_rest(n - 1)
                        probs(n)
                        if s >= 2 * T - 2:
                            with dve.If(i < last_i):
                                v_rest(n + 2, (s + 2) % 4)
                                sum_squares(n + 2)
                        else:
                            v_rest(n + 2, (s + 2) % 4)
                            sum_squares(n + 2)
                        if s == 2 * T - 1:
                            with dve.If(i < last_i):
                                kT_out(n + 1)
                        else:
                            kT_out(n + 1)
                        pT_rest(n)
                        if s >= 2 * T - 2:
                            with dve.If(i < last_i):
                                hats(n + 2, s % 2)
                            with dve.If(i > last_i - 1):
                                for t in range(2):
                                    norm_lo(phase + 1, 2 * (s - 2 * T + 2) + t)
                        else:
                            hats(n + 2, s % 2)
                        if s == 0:
                            with dve.If(i > 0):
                                x_update(n - 1, T - 1)
                        else:
                            x_update(n - 1, (s - 1) % T)
                        if s > T:
                            with dve.If(i > last_i - 1):
                                dve.wait_ge(sem("x_add"), n0 + (l.groups - 2) * T + s)
                                stats(s - 1 - T)
                                if s == 2 * T - 4:
                                    mean_var(phase + 1, 0)
                                if dequantise and s >= T + 2:
                                    dequantise(s - T - 2)
                oT_rest(l.end - 1)
                x_update(l.end - 1, T - 1)
                dve.wait_ge(sem("x_add"), l.end)
                stats(T - 1)
                mean_var(phase + 1, 1)

            def dequantise(step):
                shape = [P, 4, 8, 32]
                if step == 0:
                    dve.wait_ge(sem("pk_in"), 16)
                    dve.tensor_scalar(low4[:, :, :], packed[:, :, :], 15, None, ALU.bitwise_and).then_inc(sem("nibbles"), 1)
                elif step == 1:
                    dve.tensor_scalar(packed[:, :, :], packed[:, :, :], 4, 15, ALU.logical_shift_right, ALU.bitwise_and)\
                        .then_inc(sem("nibbles"), 1)
                elif step < 4:
                    nib = (low4, packed)[step - 2]
                    dve.wait_ge(sem("nibbles"), step - 1)
                    dve.tensor_tensor(wdq[:, :, :, :, step - 2], nib[:, :, :].rearrange("p t (g c) -> p t g c", g=8),
                                      wsc[:, :, :].unsqueeze(3).to_broadcast(shape), ALU.mult).then_inc(sem("wdq_mul"), 1)
                else:
                    dve.wait_ge(sem("wdq_mul"), step - 3)
                    w = wdq[:, :, :, :, step - 4]
                    dve.tensor_tensor(w, w, wze[:, :, :].unsqueeze(3).to_broadcast(shape), ALU.add).then_inc(sem("wdq"), 1)

            windowed_attention()
            for t in range(4):
                norm_lo(1, t)
            experts(F0, 1)
            attention(L1, None, 2)
            experts(F1, 3)
            for j in range(2):
                dve.tensor_tensor(kw[:, j:j + 1], knorm[:, 2 * j:2 * j + 1], knorm[:, 2 * j + 1:2 * j + 2], ALU.mult)\
                    .then_inc(sem("kw"), 1)
            dve.wait_ge(sem("kw"), 2)
            attention(L2, kw[:, 0:1], 4)
            experts(F2, 5)
            attention(L3, kw[:, 1:2], 6, dequantise)
            for k in range(KD):
                dve.wait_ge(sem("wdq_hi"), k + 1)
                sub(WQl[1][:, k, 0:D], ps[("qT", "kT", "s", "pT")[k]][:, :], WQh[1][:, k, 0:D].bitcast(F32))\
                    .then_inc(sem("wdq_lo"), 1)
            dense_add(T, (0, 1))
            norm_lo(7, 4)
            norm_lo(7, 5)
            dense_add(T, (2, 3))
            norm_lo(7, 6)
            norm_lo(7, 7)
            dense_add(T, range(4, T))


def kernel(**inputs):
    import concourse.bacc as bacc
    from concourse.bass_utils import run_bass_kernel_spmd

    v = {k: np.asarray(x) for k, x in inputs.items()}
    f32 = np.float32

    def pair_rows(w):
        out = np.zeros((P, P), w.dtype)
        out[:S, :S] = w.T
        out[S:, S:] = w.T
        return out

    def group_qkv(wq, wk, wv, groups, d):
        q = wq.reshape(KD, P, groups, HG * d).transpose(2, 0, 1, 3)
        k = wk.reshape(KD, P, groups, d).transpose(2, 0, 1, 3)
        w = wv.reshape(KD, P, groups, d).transpose(2, 0, 1, 3)
        return np.ascontiguousarray(np.concatenate([q, k, w], -1))

    def group_out(wo, groups, d):
        return np.ascontiguousarray(wo.reshape(groups, 2, 2, d, D).transpose(0, 1, 3, 2, 4).reshape(groups, 2, d, 2 * D))

    def rows(w):
        return np.ascontiguousarray(w.T.reshape(KD, P, -1))

    ranks = lambda w: w.reshape(-1, D)
    c = np.arange(P)
    head = np.zeros((P, T, P), f32)
    for t in range(T):
        head[c, t, t * 16 + c // 8] = 1.0
    arrays = {
        "x": v["x"].reshape(B * S, D),
        "ctx": v["ctx_4096"].reshape(B * S, D),
        "ctxT": np.ascontiguousarray(v["ctx_4096"].reshape(B * S, D).T.reshape(KD, P, B * S)),
        "mask": v["mask_1x1xSxS2_ff0"].reshape(S, S),
        "ident": np.eye(P, dtype=f32),
        "tri": np.tril(np.ones((4, 4), f32), -1).reshape(16),
        "head_sum": head,
        "head_spread": np.ascontiguousarray(head.transpose(2, 1, 0)),
        "w0": np.ascontiguousarray(np.stack([pair_rows(v["L0_xattn_W" + n]) for n in "qkvo"], 1)),
        "b0": np.ascontiguousarray(np.stack([np.tile(v["L0_xattn_b" + n], 2) for n in "qkvo"], 1)),
        "knorm": np.ascontiguousarray(np.stack([v["L2_xattn_q_norm_w"], v["L2_xattn_k_norm_w"],
                                                v["L3_xattn_q_norm_w"], v["L3_xattn_k_norm_w"]], 1)),
        "f0_ar": rows(np.concatenate([ranks(v["L0_ffn_A"]), v["L0_ffn_Wr"]], 0)),
        "f0_b": np.ascontiguousarray(v["L0_ffn_B"].transpose(0, 2, 1).reshape(P, D)),
        "f0_rb": v["L0_ffn_br"],
        "f1_ar": rows(np.concatenate([ranks(v["L1_ffn_A"]), v["L1_ffn_Wr"]], 0)),
        "f1_b": np.ascontiguousarray(v["L1_ffn_B"].transpose(0, 2, 1).reshape(64, D)),
        "f2_ar": rows(np.concatenate([v["L2_ffn_W_base"], ranks(v["L2_ffn_lora_A"].transpose(0, 2, 1)),
                                      v["L2_ffn_W_router"]], 0)),
        "f2_b": v["L2_ffn_lora_B"].reshape(P, D),
        "f2_rb": v["L2_ffn_b_router"],
        "f2_bias": v["L2_ffn_b_base"],
        "l1_qkv": group_qkv(v["L1_xattn_Wq"].T, v["L1_xattn_Wk"].T, v["L1_xattn_Wv"].T, 4, 96),
        "l1_o": group_out(v["L1_xattn_Wo"].T, 4, 96),
        "l2_qkv": group_qkv(v["L2_xattn_q_proj_w"].T, v["L2_xattn_k_proj_w"].T, v["L2_xattn_v_proj_w"].T, 8, 128),
        "l2_o": group_out(v["L2_xattn_o_proj_w"].T, 8, 128),
        "l3_qkv": group_qkv(v["L3_xattn_Wq"], v["L3_xattn_Wk"], v["L3_xattn_Wv"], 8, 128),
        "l3_o": group_out(v["L3_xattn_Wo"], 8, 128),
        "packed": v["L3_ffn_weight_packed"].reshape(D, 256),
        "scales": v["L3_ffn_weight_scales"].reshape(D, 8),
        "zeros": v["L3_ffn_weight_zeros"].reshape(D, 8),
        "f3_bias": v["L3_ffn_bias"],
    }
    nc = bacc.Bacc("TRN2", target_bir_lowering=False, num_devices=1)
    feeds, aps = {}, {}
    for name, x in arrays.items():
        x = np.ascontiguousarray(x)
        feeds["in_" + name] = x
        aps[name] = nc.dram_tensor("in_" + name, x.shape, mybir.dt.from_np(x.dtype), kind="ExternalInput").ap()
    aps["out"] = nc.dram_tensor("out_x", (B * S, D), F32, kind="ExternalOutput").ap()
    build(nc, aps)
    r = run_bass_kernel_spmd(nc, [feeds], core_ids=[0])
    return r.results[0]["out_x"].reshape(B, S, D)
```

```python
from contextlib import ExitStack

import numpy as np

import concourse.bass as bass
from concourse import mybir

ALU = mybir.AluOpType
ACT = mybir.ActivationFunctionType
AX = mybir.AxisListType
F32 = mybir.dt.float32
F32R = mybir.dt.float32r
I32 = mybir.dt.int32

P = 128
D = 512
KD = D // P
B, S = 16, 64
T = B * S // P
HG = 4
NB = 2
W0 = 16
H0 = 8
PAD0 = W0 // 2
KW = D + W0
LNEPS = 1e-5
START = 4
QC = 4 * P + 2 * P
CHUNKS = 6
STG = 1024


class Attention:

    def __init__(self, groups, d, tiles, norm_eps, masked, slot0, n0, c0):
        self.groups, self.d, self.tiles, self.norm_eps, self.masked = groups, d, tiles, norm_eps, masked
        self.slot0, self.n0, self.c0 = slot0, n0, c0
        self.keys = S * tiles
        self.scale = float(d) ** -0.5
        self.steps = groups * T
        self.end = n0 + self.steps
        self.cols = HG * d + 2 * d


class Experts:

    def __init__(self, experts, rank, dense, slot, c0):
        self.e, self.r, self.dense, self.slot, self.c0 = experts, rank, dense, slot, c0
        self.er = experts * rank
        self.cols = self.er + experts


def build(nc, a):
    L1 = Attention(4, 96, 2, None, False, 1, START, 4)
    L2 = Attention(8, 128, 1, 1e-5, True, 0, L1.end, L1.c0 + CHUNKS * 4 + 4)
    L3 = Attention(8, 128, 2, 1e-6, False, 1, L2.end, L2.c0 + CHUNKS * 8 + 4)
    F0 = Experts(8, 16, False, 0, 0)
    F1 = Experts(4, 16, False, 1, L1.c0 + CHUNKS * 4)
    F2 = Experts(8, 16, True, 0, L2.c0 + CHUNKS * 8)
    SMALL = 16 * 10
    SUMS = 6
    SUM_AT = (7, 9, 13, 15, 16 + 1, 16 + 5)
    NORM0 = L1.steps

    with ExitStack() as ctx:
        used = nc.sbuf_usable_end - nc.sbuf_bytes_remaining

        def at(name, shape, dt, offset):
            n = int(np.prod(shape[1:])) * 4
            return nc.alloc_sbuf_tensor_at(name, shape, dt, offset=offset), offset + (n + 31) // 32 * 32

        base = (used + 31) // 32 * 32
        X, o = at("x", [P, T, D], F32, base)
        HT_at = o
        HTh, o_e = at("hT_hi", [P, KD, B, S, 2], F32R, o)
        HTl, o = at("hT_lo", [P, KD, B, S, 2], F32R, o_e)
        w_at = o
        WQh = [None, None]; WQl = [None, None]; WOh = [None, None]; WOl = [None, None]
        for s in range(2):
            WQh[s], o = at(f"wqkv_hi{s}", [P, KD, QC], F32R, o)
            WQl[s], o = at(f"wqkv_lo{s}", [P, KD, QC], F32R, o)
            if s == 0:
                wo0_at = o
            wo_at = o
            WOh[s], o = at(f"wo_hi{s}", [P, HG, D], F32R, o)
            WOl[s], o = at(f"wo_lo{s}", [P, HG, D], F32R, o)
        w_end = o
        stage = [None, None]
        for s in range(2):
            stage[s], o = at(f"stage{s}", [P, STG], F32, o)
        ident, o = at("ident", [P, P], F32, o)
        ident_r, o = at("ident_r", [P, P], F32R, o)
        mask, o = at("mask", [P, S], F32, o)
        knorm, o = at("knorm", [P, 4], F32, o)
        kw, o = at("kw", [P, 2], F32, o)
        mhalf, o = at("mhalf", [P, 8], F32, o)
        st, o = at("ln_stats", [P, T, 6], F32, o)
        mv, o = at("ln_mean_var", [P, T, 2], F32, o)
        ve, o = at("ln_var_eps", [P, T], F32, o)
        rstd, o = at("ln_rstd", [P, T], F32, o)
        mneg, o = at("ln_minus_mean", [P, T], F32, o)
        shift, o = at("ln_shift", [P, T], F32, o)
        rb = [None, None]
        for s in range(2):
            rb[s], o = at(f"router_bias{s}", [P, 8], F32, o)
        tri, o = at("tri", [P, 16], F32, o)
        xn = [None, None]
        for s in range(2):
            xn[s], o = at(f"xn{s}", [P, D], F32, o)
        bias, o = at("bias_rows", [P, D], F32, o)
        bias_at = o
        o += 256
        work = o
        qkh = [None, None]; vh = [None] * 4; vl = [None] * 4
        sq, o = at("squares", [P, QC], F32, work)
        ss, o = at("sumsq", [P, 8], F32, o)
        ms, o = at("meansq", [P, 8], F32, o)
        rs, o = at("rnorm", [P, 8], F32, o)
        for s in range(2):
            qkh[s], o = at(f"qk_hat{s}", [P, QC], F32, o)
        qT, o = at("qT", [P, HG * P], F32, o)
        kT, o = at("kT", [P, 2 * P], F32, o)
        for s in range(4):
            vh[s], o = at(f"v_hi{s}", [P, 2 * P], F32R, o)
            vl[s], o = at(f"v_lo{s}", [P, 2 * P], F32R, o)
        sc, o = at("scores", [P, 4 * P], F32, o)
        smx, o = at("score_max", [P, 4], F32, o)
        ssum, o = at("score_sum", [P, 4], F32, o)
        srec, o = at("score_rec", [P, 4], F32, o)
        pTh, o = at("pT_hi", [P, 4 * P], F32R, o)
        pTl, o = at("pT_lo", [P, 4 * P], F32R, o)
        oTh, o = at("oT_hi", [P, 4 * P], F32R, o)
        oTl, o = at("oT_lo", [P, 4 * P], F32R, o)
        assert o <= nc.sbuf_usable_end, o - nc.sbuf_usable_end
        lr, o = at("low_logits", [P, T, 136], F32, work)
        gated, o = at("gated", [P, T, P], F32, o)
        gT, o = at("gatedT", [P, T, P], F32, o)
        Bf, o = at("expert_out", [P, D], F32, o)
        z, o = at("z", [P, T, 8], F32, o)
        z2, o = at("z2", [P, T, 8], F32, o)
        z3, o = at("z3", [P, T, 8], F32, o)
        zr, o = at("zr", [P, T], F32, o)
        zs, o = at("zs", [P, T], F32, o)
        zt, o = at("zt", [P, T], F32, o)
        pair, o = at("pairs", [P, T, 8, 8], F32, o)
        pair2, o = at("pairs2", [P, T, 4, 4], F32, o)
        gates, o = at("gates", [P, T, 8], F32, o)
        assert o <= nc.sbuf_usable_end
        packed, o = at("packed", [P, 4, 256], I32, wo_at)
        low4, o = at("low4", [P, 4, 256], I32, o)
        wdq, o = at("w_dequant", [P, 4, 8, 32, 2], F32, o)
        assert o <= w_end
        wsc, o = at("w_scales", [P, 4, 8], F32, bias_at)
        wze, o = at("w_zeros", [P, 4, 8], F32, o)
        dots, o = at("dots", [P, W0 + 1, D], F32, w_at)
        ctxn, _ = at("ctxn", [P, T, D], F32, w_at)
        K0, o = at("k_padded", [P, T, KW], F32, o)
        V0, o = at("v_padded", [P, T, KW], F32, o)
        E0, o = at("head_sum", [P, T, P], F32, o)
        ETr, o = at("head_spread", [P, T, P], F32R, o)
        w0, o = at("w_l0", [P, 4, P], F32, o)
        b0, o = at("b_l0", [P, 4], F32, o)
        assert o <= w_end
        q0, o = at("q_l0", [P, T, D], F32, work)
        mx0, o = at("max_l0", [P, D], F32, o)
        rspread = [None, None]
        spread_of = [None, None]
        for s in range(2):
            spread_of[s], o = at(f"head_spread_of{s}", [P, P], F32R, o)
            rspread[s], o = at(f"rec_spread{s}", [P, D], F32, o)
        pair_of = [None] * 4
        for s in range(2):
            pair_of[s], o = at(f"prods{s}", [P, 2, D], F32, o)
        assert o <= nc.sbuf_usable_end
        E0r, o = at("head_sum_r", [P, T, P], F32R, HT_at)
        ETs, o = at("head_spread_in", [P, T, P], F32, o)
        proh = [None] * 4; prol = [None] * 4
        for s in range(4):
            proh[s], o = at(f"prod_hi{s}", [P, D], F32R, o)
            prol[s], o = at(f"prod_lo{s}", [P, D], F32R, o)
        for s in range(2, 4):
            pair_of[s], o = at(f"prods{s}", [P, 2, D], F32, o)
        assert o <= w_at
        qk_prod = [pair_of[t // 2][:, t % 2, :] for t in range(T)]
        o = work
        psumd = [None] * 4
        for s in range(4):
            psumd[s], o = at(f"prod_pair{s}", [P, D], F32, o)
        rec, o = at("rec_l0", [P, D], F32, o)
        rech, o = at("rec_hi", [P, D], F32R, o)
        recl, o = at("rec_lo", [P, D], F32R, o)
        ctxT, o = at("ctxT", [P, KD, B * S], F32, wo0_at)
        assert o == wo0_at + 4 * KD * B * S and o >= w_at + 4 * (W0 + 1) * D
        pv_prod = qk_prod[0:4] + [None] * 4
        for s in range(4, 8):
            pv_prod[s], o = at(f"pv_prod{s}", [P, D], F32, o)
        o0, o = at("o_l0", [P, D], F32, o)
        assert o <= w_at + 4 * (W0 + 1) * D + 4 * T * KW
        eh = HTh.ap().rearrange("p k b j s -> p (k b j s)").rearrange("p (w t) -> p w t", w=W0)
        el = HTl.ap().rearrange("p k b j s -> p (k b j s)").rearrange("p (w t) -> p w t", w=W0)

        ps = {}
        for name in ("q", "kv", "qT", "kT", "s", "pT", "oT", "y"):
            ps[name] = ctx.enter_context(nc.psum_tensor("ps_" + name, [P, 512], F32))

        sems = {}

        def sem(name):
            if name not in sems:
                sems[name] = ctx.enter_context(nc.semaphore(name))
            return sems[name]

        STEP = {
            "pe": ["kv_mm", "q_mm", "qkT_mm", "s_mm", "pT_mm", "av_mm", "y_mm"],
            "act": ["v_hi", "qT_ev", "exp", "pT_hi", "oT_hi", "squared"],
            "dve": ["v_lo", "hat", "hat_k", "kT_ev", "smax", "ssub", "ssum", "srec", "prob", "pT_lo", "oT_lo", "x_add", "sumsq", "meansq"],
            "pool": ["rnorm"],
        }
        block = ctx.enter_context(nc.Block())

        def prime(eng, who):
            for name in STEP[who]:
                eng.sem_inc(sem(name), START)

        def tile_of(H, k, t, s):
            return H[:, k, 2 * t:2 * t + 2, :, s].rearrange("p b j -> p (b j)")

        def row(t3, i):
            return t3[:, bass.ds(i, 1), :].rearrange("p a b -> p (a b)")

        def lr_bank(t, cols):
            return ps["kT"][:, 256 * t:256 * t + cols] if t < 2 else ps[("s", "pT")[t % 2]][:, 0:cols]

        def dense_bank(t):
            return ps["qT"] if t == 0 else ps[("y", "oT", "kT")[(t - 1) % 3]]

        def norm_bank(phase, t):
            if phase % 2:
                return ps[("q", "kv")[t % 2]]
            return ps[("s", "pT", "qT", "kT", "s", "pT", "s", "pT")[t]]

        @block.sync
        def _(sp):
            sp.dma_start(w0[:, :, :], a["w0"]).then_inc(sem("w0_in"), 16)
            sp.dma_start(b0[:, :], a["b0"]).then_inc(sem("b0_in"), 16)
            for h in range(T // 2):
                sp.dma_start(ctxn[:, 2 * h:2 * h + 2, :], a["ctx"][2 * h * P:2 * (h + 1) * P, :].rearrange("(t p) d -> p t d", p=P))\
                    .then_inc(sem(f"ctx_in{h}"), 16)
            sp.dma_start(E0[:, :, :], a["head_sum"]).then_inc(sem("e_in"), 16)
            sp.dma_start(ETs[:, :, :], a["head_spread"]).then_inc(sem("e_in"), 16)
            sp.dma_start(ident[:, :], a["ident"]).then_inc(sem("small_in"), 16)
            sp.dma_start(mask[0:S, :], a["mask"]).then_inc(sem("small_in"), 16)
            sp.dma_start(mask[S:P, :], a["mask"]).then_inc(sem("small_in"), 16)
            sp.dma_start(knorm[:, :], a["knorm"]).then_inc(sem("small_in"), 16)
            sp.dma_start(rb[0][:, :], a["f0_rb"].partition_broadcast(P)).then_inc(sem("small_in"), 16)
            sp.dma_start(rb[1][:, :], a["f2_rb"].partition_broadcast(P)).then_inc(sem("small_in"), 16)
            sp.dma_start(tri[:, :], a["tri"].partition_broadcast(P)).then_inc(sem("small_in"), 16)
            sp.dma_start(bias[:, :], a["f2_bias"].partition_broadcast(P)).then_inc(sem("small_in"), 16)
            sp.dma_start(wsc[:, :, :], a["scales"].rearrange("(t p) g -> p t g", p=P)).then_inc(sem("small_in"), 16)
            sp.dma_start(wze[:, :, :], a["zeros"].rearrange("(t p) g -> p t g", p=P)).then_inc(sem("small_in"), 16)

            def load(c, k, src):
                if not isinstance(k, int) or k >= 2:
                    sp.wait_ge(sem("w_lo"), k - 1)
                rows, n = src.shape[0], src.shape[1]
                sp.dma_start(stage[c % 2][0:rows, 0:n], src).then_inc(sem(f"stage{c % 2}"), 16)

            def load_experts(f, src):
                for c in range(KD):
                    load(c, f.c0 + c, src[c])

            def load_group(l, g, name):
                for c in range(KD):
                    load(c, l.c0 + g * CHUNKS + c, a[name + "_qkv"][bass.ds(g, 1), c].rearrange("o p n -> (o p) n"))
                for c in range(2):
                    load(c, l.c0 + g * CHUNKS + KD + c,
                         a[name + "_o"][bass.ds(g, 1), c].rearrange("o p n -> (o p) n"))

            for c in range(2):
                load(c, F0.c0 + c, a["f0_ar"][c])
            sp.wait_ge(sem("e_lo"), W0 // 2)
            sp.wait_ge(sem("e_lo_odd"), W0 // 2)
            sp.dma_start(ctxT[:, :, :], a["ctxT"].rearrange("k p t -> p k t")).then_inc(sem("ctxT_in"), 16)
            for c in range(2, KD):
                load(c, F0.c0 + c, a["f0_ar"][c])
            sp.wait_ge(sem("x_l0"), T + 1)
            sp.dma_start(Bf[:, :], a["f0_b"]).then_inc(sem("ff_in"), 16)
            with sp.Fori(0, L1.groups) as g:
                load_group(L1, g, "l1")
            load_experts(F1, a["f1_ar"])
            sp.wait_ge(sem("x_add"), L1.end)
            sp.dma_start(Bf[0:F1.er, :], a["f1_b"]).then_inc(sem("ff_in"), 16)
            with sp.Fori(0, L2.groups) as g:
                load_group(L2, g, "l2")
            load_experts(F2, a["f2_ar"])
            sp.wait_ge(sem("x_add"), L2.end)
            sp.dma_start(Bf[:, :], a["f2_b"]).then_inc(sem("ff_in"), 16)
            with sp.Fori(0, L3.groups) as g:
                load_group(L3, g, "l3")
            sp.wait_ge(sem("bias_add"), T)
            sp.dma_start(bias[:, :], a["f3_bias"].partition_broadcast(P)).then_inc(sem("bias_in"), 16)
            sp.wait_ge(sem("y_mm"), L3.end - T)
            sp.dma_start(packed[:, :, :], a["packed"].rearrange("(t p) c -> p t c", p=P)).then_inc(sem("pk_in"), 16)
            for t in range(T):
                sp.wait_ge(sem("dense_add"), T + t + 1)
                sp.dma_start(a["out"][t * P:(t + 1) * P, :], X[:, t, :]).then_inc(sem("out"), 16)
            sp.wait_ge(sem("out"), 16 * T)

        @block.tensor
        def _(pe):
            prime(pe, "pe")
            pe.sem_inc(sem("even_mm"), 4)
            pe.sem_inc(sem("odd_mm"), 4)
            pe.sem_inc(sem("spread_mm"), 2 * W0)
            pe.sem_inc(sem("windowsum_mm"), 3)
            pe.sem_inc(sem("y_l0"), 1)

            def passes(out, groups):
                n = len(groups)
                for k, (sh, sl, mh, ml) in enumerate(groups):
                    pe.matmul(out, sh, mh, start=(k == 0), stop=False)
                    pe.matmul(out, sh, ml, start=False, stop=False)
                    last = pe.matmul(out, sl, mh, start=False, stop=(k == n - 1))
                return last

            def norm_T(phase, t):
                pe.wait_ge(sem("ln_xn"), phase * T + t + 1)
                last_user = t - 2 if phase % 2 or t >= 6 else t - 4
                if last_user >= 0:
                    pe.wait_ge(sem("ln_lo"), (phase - 1) * T + last_user + 1)
                bank = norm_bank(phase, t)
                for k in range(KD):
                    last = pe.transpose(bank[:, k * P:(k + 1) * P], xn[t % 2][:, k * P:(k + 1) * P], ident[:, :])
                last.then_inc(sem("ln_T"), 1)

            def windowed_attention():
                banks = ("q", "kv", "s", "qT", "kT", "pT")
                pe.wait_ge(sem("w0_in"), 16)
                for m in range(3 * T):
                    t = m // 2 if m < 2 * T else m - 2 * T
                    if m >= 6:
                        if m % 2 == 0 or m - 6 >= 2 * T:
                            pe.wait_ge(sem("l0_ev"), (m - 6) // 2 + 1 if m - 6 < 2 * T else m - 5 - T)
                        else:
                            pe.wait_ge(sem("v_ev"), (m - 6) // 2 + 1)
                    if m < 2 * T:
                        if m % 4 == 0:
                            pe.wait_ge(sem(f"ctx_in{t // 2}"), 16)
                        j, moving = 1 + m % 2, ctxn[:, t, :]
                    else:
                        pe.wait_ge(sem("ln_xn"), t + 1)
                        j, moving = 0, xn[t % 2][:, :]
                    pe.matmul(ps[banks[m % 6]][:, :], w0[:, j, :], moving, start=True, stop=True).then_inc(sem("l0_mm"), 1)

                def even(w, h, m):
                    pe.wait_ge(sem("prod"), w * (T // 2) + (m + 1))
                    if m == 0:
                        pe.wait_ge(sem("dots_ev"), w + 1)
                    pe.matmul(ps[("y", "oT")[h]][:, :], E0[:, 2 * m, :], qk_prod[2 * m],
                              start=(m == 0), stop=False, skip_group_check=True).then_inc(sem("even_mm"), 1)

                def odd(w, h, m):
                    bank = ps[("y", "oT")[h]]
                    pe.wait_ge(sem("prod_lo"), w * (T // 2) + (m + 1) + 4)
                    pe.matmul(bank[:, :], E0r[:, 2 * m + 1, :], proh[m][:, :], start=False, stop=False, skip_group_check=True)
                    pe.matmul(bank[:, :], E0r[:, 2 * m + 1, :], prol[m][:, :], start=False,
                              stop=(m == T // 2 - 1), skip_group_check=True).then_inc(sem("odd_mm"), 1)

                pe.wait_ge(sem("e_in"), 32)
                pe.wait_ge(sem("e_cast"), 1)
                with pe.Fori(0, W0 // 2) as i:
                    for h in range(2):
                        w = i * 2 + h
                        for m in range(T // 2):
                            even(w, h, m)
                            if m >= 2:
                                odd(w, h, m - 2)
                            elif h == 1:
                                odd(w - 1, 0, m + 2)
                            else:
                                with pe.If(i > 0):
                                    odd(w - 1, 1, m + 2)
                for m in range(2, T // 2):
                    odd(W0 - 1, 1, m)
                pe.wait_ge(sem("dots_ev"), W0 + 2)
                banks = ("q", "kv", "qT", "kT")

                def spread(t, h, u):
                    j = t * W0 + u
                    pe.wait_ge(sem("pv"), j + 1)
                    pe.matmul(ps[banks[u % 4]][:, :], spread_of[h][:, :], eh[:, u, :], start=True, stop=False)
                    pe.matmul(ps[banks[u % 4]][:, :], spread_of[h][:, :], el[:, u, :], start=False,
                              stop=True).then_inc(sem("spread_mm"), 1)

                def windowsum(t, h, k):
                    if k == 0:
                        pe.wait_ge(sem("o_l0"), t + 1)
                    if k % 3 == 2:
                        pe.wait_ge(sem("quad"), t * 2 + (k // 3 + 1))
                    else:
                        pe.wait_ge(sem("pair"), t * (W0 // 2) + (k // 3 * 4 + k % 3 + 5))
                    pe.matmul(ps[("s", "pT")[h]][:, :], ident[:, :], psumd[k % 3][:, :], start=(k == 0),
                              stop=(k == SUMS - 1), skip_group_check=True).then_inc(sem("windowsum_mm"), 1)

                def weight_sum():
                    for w in range(W0):
                        pe.wait_ge(sem(("e_lo", "e_lo_odd")[w % 2]), w // 2 + 1)
                        for part, last in ((eh, False), (el, w == W0 - 1)):
                            ins = pe.matmul(ps["oT"][:, :], ident_r[:, :], part[:, w, :],
                                            start=(w == 0 and part is eh), stop=last)
                    ins.then_inc(sem("e_sum"), 1)

                def rec_spread(t, h):
                    pe.wait_ge(sem("rec_lo"), 1)
                    pe.wait_ge(sem("rspread_ev"), t + 1)
                    pe.matmul(ps["y"][:, :], spread_of[h][:, :], rech[:, :], start=True, stop=False)
                    pe.matmul(ps["y"][:, :], spread_of[h][:, :], recl[:, :], start=False, stop=True)\
                        .then_inc(sem("rspread_mm"), 1)

                def out(t):
                    pe.wait_ge(sem("o_l0"), t + 3)
                    pe.wait_ge(sem("x_l0"), t + 1)
                    pe.matmul(ps["oT"][:, :], w0[:, 3, :], o0[:, :], start=True, stop=True).then_inc(sem("y_l0"), 1)

                pe.wait_ge(sem("e_cast"), 3)
                weight_sum()
                with pe.Fori(0, T // 2) as i:
                    for h in range(2):
                        t = i * 2 + h
                        pe.wait_ge(sem("spread_of"), t + 1)
                        for u in range(W0):
                            spread(t, h, u)
                            if u in SUM_AT:
                                windowsum(t, h, SUM_AT.index(u))
                            elif u + W0 in SUM_AT and h == 1:
                                windowsum(t - 1, 0, SUM_AT.index(u + W0))
                            elif u + W0 in SUM_AT:
                                with pe.If(i > 0):
                                    windowsum(t - 1, 1, SUM_AT.index(u + W0))
                            if u == W0 - 2:
                                rec_spread(t, h)
                            if u == 11 and h == 1:
                                out(t - 1)
                            elif u == 11:
                                with pe.If(i > 0):
                                    out(t - 1)
                windowsum(T - 1, 1, SUMS - 2)
                pe.wait_ge(sem("pair"), T * (W0 // 2) + 3)
                pe.matmul(ps["pT"][:, :], ident[:, :], psumd[2][:, :], start=False, stop=False, skip_group_check=True)
                pe.wait_ge(sem("last_pair"), 1)
                pe.matmul(ps["pT"][:, :], ident[:, :], psumd[3][:, :], start=False, stop=True, skip_group_check=True)\
                    .then_inc(sem("windowsum_mm"), 1)
                pe.wait_ge(sem("pv"), T * W0 + 2)
                norm_T(1, 0)
                norm_T(1, 1)
                out(T - 1)

            def dequantised_T(k):
                pe.wait_ge(sem("wdq"), 2)
                bank = ps[("qT", "kT", "s", "pT")[k]]
                wk = wdq[:, :, :, :, :].rearrange("p t g j e -> p t (g j e)")
                for o_ in range(4):
                    last = pe.transpose(bank[:, o_ * P:(o_ + 1) * P], wk[:, o_, k * P:(k + 1) * P], ident[:, :])
                last.then_inc(sem("wdq_T"), 1)

            def experts(f, phase, index, x_done, part=None):
                xf = index * T
                if f is None:
                    wh, wl, cols, n_dense = WQh[1], WQl[1], 0, T
                else:
                    wh, wl, cols, n_dense = WQh[f.slot], WQl[f.slot], f.cols, 0
                off = D if f is None or f.dense else 0
                products = lambda t, c: [(tile_of(HTh, k, t, 1), tile_of(HTl, k, t, 1), wh[:, k, c], wl[:, k, c])
                                         for k in range(KD)]

                def low_rank(t):
                    if cols:
                        pe.wait_ge(sem("ln_lo"), (phase - 1) * T + t + 1)
                        if t >= 4:
                            pe.wait_ge(sem("lr_ev"), index * T + t - 1)
                        passes(lr_bank(t, cols), products(t, slice(off, off + cols)))\
                            .then_inc(sem("lr_mm"), 1)

                def dense(t):
                    if off:
                        pe.wait_ge(sem("ln_lo"), (phase - 1) * T + t + 1)
                        if t >= 4:
                            pe.wait_ge(sem("dense_add"), n_dense + t - 2)
                        elif t == 1:
                            pe.wait_ge(sem("x_add"), x_done)
                        elif t == 3 and f is not None:
                            pe.wait_ge(sem("lr_ev"), index * T + 2)
                        passes(dense_bank(t)[:, :], products(t, slice(0, D))).then_inc(sem("dense_mm"), 1)

                def gates_T(h):
                    pe.wait_ge(sem("gated"), 2 * index + h + 1)
                    for j in range(4):
                        last = pe.transpose(ps[("qT", "kT")[h]][0:f.er, j * P:j * P + P],
                                            gated[:, 4 * h + j, 0:f.er], ident[:, :])
                    last.then_inc(sem("gT_mm"), 1)

                def expand(t):
                    pe.wait_ge(sem("gT_ev"), 2 * index + 1 + t // 4)
                    if t >= 4:
                        pe.wait_ge(sem("x_ff"), xf + t - 3)
                    pe.matmul(ps[("oT", "y", "q", "kv")[t % 4]][:, :], gT[0:f.er, t, :], Bf[0:f.er, :],
                              start=True, stop=True).then_inc(sem("ff_mm"), 1)

                if part is not None:
                    if f is not None:
                        if part == 0:
                            pe.wait_ge(sem("w_lo"), f.c0 + KD)
                        low_rank(part)
                    else:
                        dequantised_T(2 * part)
                        dequantised_T(2 * part + 1)
                    return
                if f is None:
                    pe.wait_ge(sem("wdq_lo"), KD)
                elif index == 0:
                    pe.wait_ge(sem("w_lo"), f.c0 + KD)
                    low_rank(0)
                    low_rank(1)
                dense(0)
                low_rank(2)
                low_rank(3)
                if f is None:
                    dense(1)
                norm_T(phase, 4)
                norm_T(phase, 5)
                for t in range(2 if f is None else 1, 4):
                    dense(t)
                for t in range(4, 6):
                    low_rank(t)
                    norm_T(phase, t + 2)
                dense(4)
                dense(5)
                if f is not None:
                    gates_T(0)
                low_rank(6)
                low_rank(7)
                dense(6)
                dense(7)
                if f is None:
                    return
                pe.wait_ge(sem("ff_in"), 16 * (index + 1))
                if f.dense:
                    pe.wait_ge(sem("dense_add"), T)
                for t in range(4):
                    expand(t)
                gates_T(1)
                for t in range(4, T):
                    expand(t)

            def attention(l, phase, fill):
                d, cols = l.d, l.cols

                def project(n, t, slot, g):
                    if t == 0:
                        pe.wait_ge(sem("w_lo"), g * CHUNKS + (l.c0 + KD))
                    pe.wait_ge(sem("ln_lo"), (phase - 1) * T + t + 1)
                    pe.wait_ge(sem("v_lo"), n)
                    pe.wait_ge(sem("hat_k"), n)
                    for j in range(l.tiles):
                        if l.tiles == 2:
                            st_ = lambda H, k: H[:, k, 2 * t + j, :, :].rearrange("p j s -> p (j s)")
                        else:
                            st_ = lambda H, k: tile_of(H, k, t, 0)
                        last = passes(ps["kv"][:, j * 2 * d:(j + 1) * 2 * d],
                                      [(st_(HTh, k), st_(HTl, k), WQh[slot][:, k, HG * d:cols],
                                        WQl[slot][:, k, HG * d:cols]) for k in range(KD)])
                    last.then_inc(sem("kv_mm"), 1)
                    pe.wait_ge(sem("hat"), n)
                    passes(ps["q"][:, 0:HG * d],
                           [(tile_of(HTh, k, t, 1), tile_of(HTl, k, t, 1),
                             WQh[slot][:, k, 0:HG * d], WQl[slot][:, k, 0:HG * d])
                            for k in range(KD)]).then_inc(sem("q_mm"), 1)

                def transpose_qk(n):
                    pe.wait_ge(sem("hat"), n + 1)
                    pe.wait_ge(sem("qT_ev"), n)
                    pe.wait_ge(sem("kT_ev"), n)
                    hat = qkh_of(n)
                    for h in range(HG):
                        pe.transpose(ps["qT"][0:d, h * P:(h + 1) * P], hat[:, h * d:(h + 1) * d], ident[:, :])
                    for j in range(l.tiles):
                        last = pe.transpose(ps["kT"][0:d, j * P:(j + 1) * P],
                                            hat[:, (HG + j) * d:(HG + j + 1) * d], ident[:, :])
                    last.then_inc(sem("qkT_mm"), 1)

                def scores(n):
                    pe.wait_ge(sem("qT_ev"), n + 1)
                    pe.wait_ge(sem("kT_ev"), n + 1)
                    pe.wait_ge(sem("ssub"), n)
                    
                    for hp in range(2):
                        for b in range(NB):
                            c = (hp * NB + b) * l.keys
                            last = pe.matmul(ps["s"][:, c:c + l.keys], qT[0:d, (b * 2 + hp) * P:(b * 2 + hp + 1) * P],
                                             kT[0:d, b * l.keys:(b + 1) * l.keys], start=True, stop=True)
                    last.then_inc(sem("s_mm"), 1)

                def transpose_p(n):
                    pe.wait_ge(sem("prob"), n + 1)
                    pe.wait_ge(sem("pT_lo"), n)
                    if l.tiles == 2:
                        for b in range(NB):
                            for hp in range(2):
                                c = (hp * NB + b) * P
                                last = pe.transpose(ps["pT"][:, (b * 2 + hp) * P:(b * 2 + hp + 1) * P],
                                                    sc[:, c:c + P], ident[:, :])
                    else:
                        for hp in range(2):
                            last = pe.transpose(ps["pT"][:, hp * P:(hp + 1) * P], sc[:, hp * P:(hp + 1) * P],
                                                ident[:, :])
                    last.then_inc(sem("pT_mm"), 1)

                def values(n, v):
                    pe.wait_ge(sem("pT_lo"), n + 1)
                    pe.wait_ge(sem("v_lo"), n + 1)
                    pe.wait_ge(sem("oT_lo"), n)
                    if l.tiles == 2:
                        for b in range(NB):
                            c = slice(b * 2 * P, (b + 1) * 2 * P)
                            last = passes(ps["oT"][0:d, c], [(vh[v][:, b * d:(b + 1) * d], vl[v][:, b * d:(b + 1) * d],
                                                              pTh[:, c], pTl[:, c])])
                    else:
                        last = passes(ps["oT"][0:d, :], [(vh[v][:, 0:d], vl[v][:, 0:d], pTh[:, :], pTl[:, :])])
                    last.then_inc(sem("av_mm"), 1)

                def project_out(n, t, slot, g):
                    if t == 0:
                        pe.wait_ge(sem("w_lo"), g * CHUNKS + (l.c0 + CHUNKS))
                    pe.wait_ge(sem("oT_lo"), n + 1)
                    pe.wait_ge(sem("x_add"), n)
                    passes(ps["y"][:, :], [(oTh[0:d, h * P:(h + 1) * P], oTl[0:d, h * P:(h + 1) * P], WOh[slot][0:d, h, :], WOl[slot][0:d, h, :])
                                           for h in range(HG)]).then_inc(sem("y_mm"), 1)

                slots = [(l.slot0 + h) % 2 for h in range(2)]
                n0 = l.n0
                qkh_of = lambda n: qkh[parity[0]]
                parity = [0]
                for t in range(4):
                    norm_T(phase, t)
                pe.wait_ge(sem("ctx_lo"), KD)
                project(n0, 0, slots[0], 0)
                for t in range(4, T):
                    norm_T(phase, t)
                transpose_qk(n0)
                project(n0 + 1, 1, slots[0], 0)
                pe.wait_ge(sem("ln_lo"), phase * T)
                scores(n0)
                last_i = l.groups // 2 - 1
                with pe.Fori(0, l.groups // 2) as i:
                    for s in range(2 * T):
                        n = i * (2 * T) + (n0 + s)

                        def full_step():
                            u = (s + 2) % (2 * T)
                            project(n + 2, u % T, slots[u // T], i * 2 + (s + 2) // T)
                            transpose_qk(n + 1)
                            transpose_p(n)
                            if s == 0:
                                with pe.If(i > 0):
                                    project_out(n - 1, T - 1, slots[1], 0)
                            else:
                                project_out(n - 1, (s - 1) % T, slots[(s - 1) // T], i * 2 + (s - 1) // T)
                            scores(n + 1)
                            values(n, s % 4)

                        parity[0] = (s + 1) % 2
                        if s < 2 * T - 2:
                            full_step()
                            continue
                        with pe.If(i < last_i):
                            full_step()
                        with pe.If(i > last_i - 1):
                            if s == 2 * T - 2:
                                pe.wait_ge(sem("v_lo"), l.end)
                                pe.wait_ge(sem("hat"), l.end)
                                norm_T(phase + 1, 0)
                                norm_T(phase + 1, 1)
                                transpose_qk(n + 1)
                            project_out(n - 1, s - 1 - T, slots[1], i * 2 + 1)
                            transpose_p(n)
                            if s == 2 * T - 2:
                                scores(n + 1)
                            else:
                                norm_T(phase + 1, 2)
                                norm_T(phase + 1, 3)
                                fill[0]()
                            values(n, s % 4)
                            if s == 2 * T - 1:
                                fill[1]()
                project_out(l.end - 1, T - 1, slots[1], 0)

            windowed_attention()
            for t in range(2, 4):
                norm_T(1, t)
            experts(F0, 1, 0, 0)
            def ahead(*of):
                return [(lambda k=k: experts(*of, part=k)) for k in range(2)]

            attention(L1, 2, ahead(F1, 3, 1, L1.end))
            experts(F1, 3, 1, L1.end)
            attention(L2, 4, ahead(F2, 5, 2, L2.end))
            experts(F2, 5, 2, L2.end)
            attention(L3, 6, ahead(None, 7, 3, L3.end))
            experts(None, 7, 3, L3.end)

        @block.scalar
        def _(act):
            prime(act, "act")
            act.sem_inc(sem("dots_ev"), 2)
            act.sem_inc(sem("rspread_ev"), 1)
            for h in range(T // 2):
                act.dma_start(X[:, 2 * h:2 * h + 2, :], a["x"][2 * h * P:2 * (h + 1) * P, :].rearrange("(t p) d -> p t d", p=P))\
                    .then_inc(sem(f"x_in{h}"), 16)

            def copy(out, in_):
                return act.activation(out, in_, ACT.Copy)

            def cut_hi(c, k, out, rows, n, src_view=None):
                if isinstance(k, int):
                    act.wait_ge(sem(f"stage{c % 2}"), 16 * (k // 2 + 1))
                else:
                    act.wait_ge(sem(f"stage{c % 2}"), k)
                src = stage[c % 2][0:rows, 0:n]
                if src_view:
                    src = src_view(src)
                copy(out, src).then_inc(sem("w_hi"), 1)

            def cut_experts(f, only=None):
                n = f.cols + (D if f.dense else 0)
                for c in range(KD) if only is None else (only,):
                    cut_hi(c, f.c0 + c, WQh[f.slot][:, c, 0:n], P, n)

            def cut_chunk(l, c, slot, g=None):
                if g is None:
                    k = l.c0 + c
                else:
                    k = g * (8 * CHUNKS) + 16 * ((l.c0 + c) // 2 + 1)
                if c < KD:
                    cut_hi(c, k, WQh[slot][:, c, 0:l.cols], P, l.cols)
                else:
                    cut_hi(c, k, WOh[slot][0:l.d, 2 * (c - KD):2 * (c - KD) + 2, :].rearrange("p h n -> p (h n)"),
                           l.d, STG)

            def norm_x(phase, t):
                act.wait_ge(sem("ln_shift"), 2 * phase + t // 4 + 1)
                if t >= 2:
                    act.wait_ge(sem("ln_T"), (phase - 1) * T + t - 1)
                act.activation(xn[t % 2][:, :], X[:, t, :], ACT.Identity, bias=shift[:, t:t + 1],
                               scale=rstd[:, t:t + 1]).then_inc(sem("ln_xn"), 1)

            def norm_hi(phase, t):
                act.wait_ge(sem("ln_T"), (phase - 1) * T + t + 1)
                copy(HTh[:, :, 2 * t:2 * t + 2, :, 1], norm_bank(phase, t)[:, :].rearrange("p (k b j) -> p k b j", k=KD, b=NB))\
                    .then_inc(sem("ln_hi"), 1)

            def windowed_attention():
                act.wait_ge(sem("b0_in"), 16)
                for m in range(3 * T):
                    t = m // 2 if m < 2 * T else m - 2 * T
                    j = 1 + m % 2 if m < 2 * T else 0
                    if j == 2:
                        continue
                    dst = (q0[:, t, :], K0[:, t, PAD0:PAD0 + D])[j]
                    act.wait_ge(sem("l0_mm"), m + 1)
                    act.activation(dst, ps[("q", "kv", "s", "qT", "kT", "pT")[m % 6]][:, :], ACT.Identity, bias=b0[:, j:j + 1])\
                        .then_inc(sem("l0_ev"), 1)

                act.wait_ge(sem("e_in"), 32)
                copy(E0r[:, :, :], E0[:, :, :]).then_inc(sem("e_cast"), 1)

                def dots_out(w, h):
                    act.wait_ge(sem("odd_mm"), w * (T // 2) + (T // 2 + 4))
                    copy(row(dots, w + 1), ps[("y", "oT")[h]][:, :]).then_inc(sem("dots_ev"), 1)

                with act.Fori(0, W0 // 2) as i:
                    for h in range(2):
                        w = i * 2 + h
                        for m in range(T // 2):
                            act.wait_ge(sem("prod"), w * (T // 2) + (m + 1))
                            act.wait_ge(sem("odd_mm"), w * (T // 2) + (m + 1))
                            copy(proh[m][:, :], qk_prod[2 * m + 1]).then_inc(sem("prod_hi"), 1)
                            if m == 2 and h == 1:
                                dots_out(w - 1, 0)
                            elif m == 2:
                                with act.If(i > 0):
                                    dots_out(w - 1, 1)
                dots_out(W0 - 1, 1)
                copy(ETr[:, :, :], ETs[:, :, :]).then_inc(sem("e_cast"), 1)
                act.wait_ge(sem("small_in"), SMALL)
                copy(ident_r[:, :], ident[:, :]).then_inc(sem("e_cast"), 1)
                act.wait_ge(sem("e_cast"), 2)
                with act.Fori(0, W0 // 2) as i:
                    for h in range(2):
                        w = i * 2 + h
                        act.wait_ge(sem("e_sub"), w + 1)
                        act.activation(row(dots, w + 1), row(dots, w + 1), ACT.Exp, scale=float(S // H0) ** -0.5)\
                            .then_inc(sem("e_exp"), 1)
                    for h in range(2):
                        w = i * 2 + h
                        act.wait_ge(sem("e_exp"), w + 1)
                        copy(row(eh, w), row(dots, w + 1)).then_inc(sem("e_hi"), 1)
                with act.Fori(0, T // 2) as i:
                    for h in range(2):
                        t = i * 2 + h
                        act.wait_ge(sem("spread_mm"), t * W0 + W0)
                        copy(spread_of[h][:, :], row(ETr, t)).then_inc(sem("spread_of"), 1)
                        if h == 0:
                            act.wait_ge(sem("rec"), 1)
                            with act.If(i > T // 2 - 2):
                                cut_experts(F0)
                            with act.If(i < 1):
                                copy(rech[:, :], rec[:, :]).then_inc(sem("rec_hi"), 1)
                        act.wait_ge(sem("rspread_mm"), t + 1)
                        act.wait_ge(sem("o_l0"), t + 1)
                        copy(rspread[h][:, :], ps["y"][:, :]).then_inc(sem("rspread_ev"), 1)

            def experts(f, phase, cuts):
                index = (phase - 1) // 2

                def low_rank(t):
                    act.wait_ge(sem("lr_mm"), index * T + max(t, 1) + 1)
                    copy(lr[:, t, 0:f.cols], lr_bank(t, f.cols)).then_inc(sem("lr_ev"), 1)

                def gate_exp(h):
                    if index < 2:
                        act.wait_ge(sem("gate_in"), 2 * index + h + 1)
                        act.activation(z2[:, 4 * h:4 * h + 4, 0:f.e], z[:, 4 * h:4 * h + 4, 0:f.e], ACT.Exp)\
                            .then_inc(sem("gate_exp"), 1)

                def gates_T(h):
                    act.wait_ge(sem("gT_mm"), 2 * index + h + 1)
                    copy(gT[0:f.er, 4 * h:4 * h + 4, :].rearrange("p t n -> p (t n)"),
                         ps[("qT", "kT")[h]][0:f.er, :]).then_inc(sem("gT_ev"), 1)

                def cut_some(place):
                    for cut_one in cuts[place]:
                        cut_one()

                cut_some(0)
                for t in range(3):
                    low_rank(t)
                norm_x(phase, 4)
                norm_x(phase, 5)
                low_rank(3)
                gate_exp(0)
                norm_hi(phase, 4)
                norm_hi(phase, 5)
                norm_x(phase, 6)
                norm_x(phase, 7)
                cut_some(1)
                for t in range(4, 6):
                    low_rank(t)
                    norm_hi(phase, t + 2)
                gates_T(0)
                cut_some(2)
                low_rank(6)
                low_rank(7)
                gate_exp(1)
                cut_some(3)
                gates_T(1)
                cut_some(4)
                norm_x(phase + 1, 0)
                norm_x(phase + 1, 1)
                for t in range(4):
                    norm_hi(phase + 1, t)
                    norm_x(phase + 1, t + 2)

            def dequantised_hi(k):
                act.wait_ge(sem("wdq_T"), k + 1)
                copy(WQh[1][:, k, 0:D], ps[("qT", "kT", "s", "pT")[k]][:, :]).then_inc(sem("wdq_hi"), 1)

            def attention(l, f, phase):
                d = l.d

                def v_and_squares(n, v):
                    act.wait_ge(sem("kv_mm"), n + 1)
                    act.wait_ge(sem("av_mm"), n - 3)
                    kv = ps["kv"][:, 0:l.tiles * 2 * d].rearrange("p (j c) -> p j c", j=l.tiles)
                    if l.norm_eps is not None:
                        act.wait_ge(sem("sumsq"), n - NORM0)
                        act.activation(sq[:, HG * d:(HG + l.tiles) * d].rearrange("p (j c) -> p j c", j=l.tiles),
                                       kv[:, :, 0:d], ACT.Square)
                    copy(vh[v][:, 0:l.tiles * d].rearrange("p (j c) -> p j c", j=l.tiles), kv[:, :, d:2 * d])\
                        .then_inc(sem("v_hi"), 1)
                    if l.norm_eps is not None:
                        act.wait_ge(sem("q_mm"), n + 1)
                        act.activation(sq[:, 0:HG * d], ps["q"][:, 0:HG * d], ACT.Square).then_inc(sem("squared"), 1)

                def qT_out(n):
                    act.wait_ge(sem("qkT_mm"), n + 1)
                    act.wait_ge(sem("s_mm"), n)
                    copy(qT[0:d, :].rearrange("p (b h q) -> p h b q", b=NB, h=HG),
                         ps["qT"][0:d, :].rearrange("p (h b q) -> p h b q", h=HG, b=NB)).then_inc(sem("qT_ev"), 1)

                def exps(n):
                    act.wait_ge(sem("ssub"), n + 1)
                    act.activation(sc[:, 0:4 * l.keys], sc[:, 0:4 * l.keys], ACT.Exp,
                                   scale=1.0 if l.masked else l.scale).then_inc(sem("exp"), 1)

                def pT_out(n):
                    act.wait_ge(sem("pT_mm"), n + 1)
                    act.wait_ge(sem("av_mm"), n)
                    if l.tiles == 2:
                        copy(pTh[:, :], ps["pT"][:, :]).then_inc(sem("pT_hi"), 1)
                    else:
                        for b in range(NB):
                            last = copy(pTh[b * S:(b + 1) * S, b * 2 * P:(b + 1) * 2 * P],
                                        block_of(b))
                        last.then_inc(sem("pT_hi"), 1)

                def block_of(b):
                    return ps["pT"][b * S:(b + 1) * S, 0:2 * P]

                by_head = lambda v: v[0:d, :].rearrange("p (h b q) -> p b h q", h=HG, b=NB)
                from_batch = lambda v: v[0:d, :].rearrange("p (b h q) -> p b h q", b=NB, h=HG)

                def oT_out(n):
                    act.wait_ge(sem("av_mm"), n + 1)
                    act.wait_ge(sem("y_mm"), n)
                    copy(by_head(oTh), from_batch(ps["oT"])).then_inc(sem("oT_hi"), 1)

                slots = [(l.slot0 + h) % 2 for h in range(2)]
                n0 = l.n0
                v_and_squares(n0, 0)
                norm_hi(phase, 4)
                norm_x(phase, 6)
                norm_hi(phase, 5)
                norm_x(phase, 7)
                norm_hi(phase, 6)
                norm_hi(phase, 7)
                qT_out(n0)
                v_and_squares(n0 + 1, 1)
                last_i = l.groups // 2 - 1
                with act.Fori(0, l.groups // 2) as i:
                    for s in range(2 * T):
                        n = i * (2 * T) + (n0 + s)
                        if s == 0:
                            with act.If(i > 0):
                                oT_out(n - 1)
                        else:
                            oT_out(n - 1)
                        exps(n)
                        if s >= 2 * T - 2:
                            with act.If(i < last_i):
                                v_and_squares(n + 2, (s + 2) % 4)
                            if s == 2 * T - 2:
                                with act.If(i > last_i - 1):
                                    norm_hi(phase + 1, 0)
                                    norm_hi(phase + 1, 1)
                        else:
                            v_and_squares(n + 2, (s + 2) % 4)
                        if s == 2 * T - 1:
                            with act.If(i < last_i):
                                qT_out(n + 1)
                        else:
                            qT_out(n + 1)
                        pT_out(n)
                        c = s % T - 1
                        if 0 <= c < CHUNKS:
                            slot = slots[(s // T + 1) % 2]
                            if s < T:
                                act.wait_ge(sem("y_mm"), n - 1)
                                cut_chunk(l, c, slot, i * 2 + 1)
                            else:
                                with act.If(i < last_i):
                                    act.wait_ge(sem("y_mm"), n - 1)
                                    cut_chunk(l, c, slot, i * 2 + 2)
                                if c < KD and f is not None:
                                    with act.If(i > last_i - 1):
                                        act.wait_ge(sem("y_mm"), n - 1)
                                        cut_experts(f, c)
                        if s in (2 * T - 3, 2 * T - 2):
                            with act.If(i > last_i - 1):
                                for t in range(2):
                                    norm_x(phase + 1, 2 * (s - 2 * T + 3) + t)
                        if s == 2 * T - 1:
                            with act.If(i > last_i - 1):
                                norm_hi(phase + 1, 2)
                                norm_hi(phase + 1, 3)
                                if f is None:
                                    dequantised_hi(0)
                                    dequantised_hi(1)
                oT_out(l.end - 1)

            def cuts_of(l, places):
                c, out = 0, []
                for n in places:
                    out.append([(lambda k=k: cut_chunk(l, k, l.slot0)) for k in range(c, c + n)])
                    c += n
                return out

            def cut_ctx(c):
                act.wait_ge(sem("ctxT_in"), 16)
                copy(HTh[:, c, :, :, 0], ctxT[:, c, :].rearrange("p (b j) -> p b j", b=B)).then_inc(sem("ctx_hi"), 1)

            windowed_attention()
            norm_x(1, 0)
            norm_x(1, 1)
            for t in range(4):
                norm_hi(1, t)
                if t < 2:
                    norm_x(1, t + 2)
            act.wait_ge(sem("x_l0"), T + 1)
            cuts = cuts_of(L1, (0, 0, 2, 2, 2))
            cuts[0] = [lambda: cut_ctx(0), lambda: cut_ctx(1)]
            cuts[1] = [lambda: cut_ctx(2), lambda: cut_ctx(3)]
            experts(F0, 1, cuts)
            attention(L1, F1, 2)
            experts(F1, 3, cuts_of(L2, (0, 2, 0, 2, 2)))
            attention(L2, F2, 4)
            experts(F2, 5, cuts_of(L3, (0, 2, 0, 2, 2)))
            attention(L3, None, 6)
            dequantised_hi(2)
            dequantised_hi(3)
            norm_x(7, 4)
            norm_x(7, 5)
            for t in range(4, T):
                norm_hi(7, t)
                if t + 2 < T:
                    norm_x(7, t + 2)

        @block.gpsimd
        def _(pool):
            prime(pool, "pool")
            pool.sem_inc(sem("pair"), 4)
            pool.sem_inc(sem("prod_lo"), 4)
            pool.memset(mhalf[:, :], -0.5).then_inc(sem("mhalf"), 1)
            pool.wait_ge(sem("mhalf"), 1)

            def sub(out, in0, in1):
                return pool.tensor_tensor(out, in0, in1, ALU.subtract)

            def cut_lo(c, k, out, hi, rows, n, src_view=None):
                pool.wait_ge(sem("w_hi"), k + 1)
                src = stage[c % 2][0:rows, 0:n]
                if src_view:
                    src = src_view(src)
                sub(out, src, hi.bitcast(F32)).then_inc(sem("w_lo"), 1)

            def cut_experts(f, chunks=range(KD)):
                n = f.cols + (D if f.dense else 0)
                for c in chunks:
                    cut_lo(c, f.c0 + c, WQl[f.slot][:, c, 0:n], WQh[f.slot][:, c, 0:n], P, n)

            def cut_chunk(l, c, slot, g=0):
                k = g * CHUNKS + (l.c0 + c)
                if c < KD:
                    cut_lo(c, k, WQl[slot][:, c, 0:l.cols], WQh[slot][:, c, 0:l.cols], P, l.cols)
                else:
                    v = [w[slot][0:l.d, 2 * (c - KD):2 * (c - KD) + 2, :].rearrange("p h n -> p (h n)")
                         for w in (WOl, WOh)]
                    cut_lo(c, k, v[0], v[1], l.d, STG)

            def norm_rstd(phase, h):
                tt = slice(4 * h, 4 * h + 4)
                pool.wait_ge(sem("ln_mv"), phase * T + 4 * h + 4)
                if phase:
                    pool.wait_ge(sem("ln_xn"), (phase - 1) * T + 4 * h + 4)
                pool.tensor_scalar(ve[:, tt], mv[:, tt, 1], LNEPS, None, ALU.add).then_inc(sem("ln_ve"), 1)
                pool.tensor_scalar(mneg[:, tt], mv[:, tt, 0], -1.0, None, ALU.mult).then_inc(sem("ln_ve"), 1)
                pool.wait_ge(sem("ln_ve"), 4 * phase + 2 * h + 2)
                pool.tensor_tensor(rstd[:, tt], ve[:, tt], mhalf[:, 0:4], ALU.pow).then_inc(sem("ln_rstd"), 1)
                pool.wait_ge(sem("ln_rstd"), 2 * phase + h + 1)
                pool.tensor_tensor(shift[:, tt], mneg[:, tt], rstd[:, tt], ALU.mult).then_inc(sem("ln_shift"), 1)

            def attention(l, f, phase):
                def norms(n):
                    k = HG + l.tiles
                    m = n - NORM0
                    pool.wait_ge(sem("meansq"), m + 1)
                    pool.wait_ge(sem("hat"), n)
                    pool.tensor_tensor(rs[:, 0:k], ms[:, 0:k], mhalf[:, 0:k], ALU.pow).then_inc(sem("rnorm"), 1)

                slots = [(l.slot0 + h) % 2 for h in range(2)]
                if l.norm_eps is not None:
                    norms(l.n0)
                    norms(l.n0 + 1)
                last_i = l.groups // 2 - 1
                with pool.Fori(0, l.groups // 2) as i:
                    for s in range(2 * T):
                        n = i * (2 * T) + (l.n0 + s)
                        if l.norm_eps is not None:
                            if s >= 2 * T - 2:
                                with pool.If(i < last_i):
                                    norms(n + 2)
                            else:
                                norms(n + 2)
                        c = s % T - 1
                        if 0 <= c < CHUNKS:
                            slot = slots[(s // T + 1) % 2]
                            if s < T:
                                cut_chunk(l, c, slot, i * 2 + 1)
                            else:
                                with pool.If(i < last_i):
                                    cut_chunk(l, c, slot, i * 2 + 2)
                                if c < KD and f is not None:
                                    with pool.If(i > last_i - 1):
                                        cut_experts(f, (c,))
                        if s == 2 * T - 4:
                            with pool.If(i > last_i - 1):
                                norm_rstd(phase + 1, 0)
                norm_rstd(phase + 1, 1)

            def add_bias(phase, tiles):
                for t in tiles:
                    pool.wait_ge(sem("ln_xn"), phase * T + t + 1)
                    pool.tensor_tensor(X[:, t, :], X[:, t, :], bias[:, :], ALU.add).then_inc(sem("bias_add"), 1)

            norm_rstd(0, 0)
            norm_rstd(0, 1)
            with pool.Fori(0, W0) as w:
                for m in range(T // 2):
                    pool.wait_ge(sem("prod_hi"), w * (T // 2) + (m + 1))
                    sub(prol[m][:, :], qk_prod[2 * m + 1], proh[m][:, :].bitcast(F32)).then_inc(sem("prod_lo"), 1)
            with pool.Fori(0, W0 // 2) as i:
                pool.wait_ge(sem("e_hi"), i * 2 + 1)
                sub(row(el, i * 2), row(dots, i * 2 + 1), row(eh, i * 2).bitcast(F32)).then_inc(sem("e_lo"), 1)
            def pair_sum(i, h):
                pool.wait_ge(sem("pv"), (i * 4 + h) * 2 + 6)
                pool.wait_ge(sem("windowsum_mm"), i * 3 + min(h + 1, 3))
                pool.tensor_tensor(psumd[h][:, :], pv_prod[2 * h][:, :], pv_prod[2 * h + 1][:, :], ALU.add)\
                    .then_inc(sem("pair"), 1)

            def pairs(first, end):
                with pool.Fori(first, end) as i:
                    for h in range(4):
                        pair_sum(i, h)
                    pool.wait_ge(sem("pair"), i * 4 + 8)
                    pool.tensor_tensor(psumd[2][:, :], psumd[2][:, :], psumd[3][:, :], ALU.add).then_inc(sem("quad"), 1)

            pairs(0, 12)
            cut_experts(F0, (0, 1))
            pairs(12, 14)
            cut_experts(F0, (2, 3))
            norm_rstd(1, 0)
            pairs(14, 2 * T - 1)
            for h in range(3):
                pair_sum(2 * T - 1, h)
            norm_rstd(1, 1)

            def cut_ctx(c):
                pool.wait_ge(sem("ctx_hi"), c + 1)
                sub(HTl[:, c, :, :, 0], ctxT[:, c, :].rearrange("p (b j) -> p b j", b=B),
                    HTh[:, c, :, :, 0].bitcast(F32)).then_inc(sem("ctx_lo"), 1)

            def cut_first(l, chunks):
                for c in chunks:
                    cut_chunk(l, c, l.slot0)

            for c in range(KD):
                cut_ctx(c)
            cut_first(L1, (0, 1, 2, 3))
            norm_rstd(2, 0)
            cut_first(L1, (4,))
            norm_rstd(2, 1)
            cut_first(L1, (5,))
            attention(L1, F1, 2)
            cut_first(L2, (0, 1, 2, 3))
            norm_rstd(4, 0)
            cut_first(L2, (4,))
            norm_rstd(4, 1)
            cut_first(L2, (5,))
            attention(L2, F2, 4)
            add_bias(5, range(4))
            cut_first(L3, (0, 1))
            add_bias(5, range(4, T))
            cut_first(L3, (2, 3))
            norm_rstd(6, 0)
            cut_first(L3, (4,))
            norm_rstd(6, 1)
            cut_first(L3, (5,))
            attention(L3, None, 6)
            pool.wait_ge(sem("bias_in"), 16)
            add_bias(7, range(T))

        @block.vector
        def _(dve):
            prime(dve, "dve")
            dve.sem_inc(sem("pv"), 4)
            dve.sem_inc(sem("o_l0"), 2)
            dve.sem_inc(sem("x_l0"), 1)
            links = [0]

            def link(ins):
                links[0] += 1
                ins.then_inc(sem("dve_link"), 1)
                dve.wait_ge(sem("dve_link"), links[0])

            def sub(out, in0, in1):
                return dve.tensor_tensor(out, in0, in1, ALU.subtract)

            def stats(t):
                dve.bn_stats(st[:, t, :], X[:, t, :]).then_inc(sem("ln_st"), 1)

            def mean_var(phase, h):
                for t in range(4 * h, 4 * h + 4):
                    dve.wait_ge(sem("ln_st"), phase * T + t + 1)
                    dve.bn_aggr(mv[:, t, :], st[:, t, :]).then_inc(sem("ln_mv"), 1)

            def norm_lo(phase, t):
                dve.wait_ge(sem("ln_hi"), (phase - 1) * T + t + 1)
                sub(HTl[:, :, 2 * t:2 * t + 2, :, 1], norm_bank(phase, t)[:, :].rearrange("p (k b j) -> p k b j", k=KD, b=NB),
                    HTh[:, :, 2 * t:2 * t + 2, :, 1].bitcast(F32)).then_inc(sem("ln_lo"), 1)

            def windowed_attention():
                for pad in (K0, V0):
                    dve.memset(pad[:, :, 0:PAD0], 0.0)
                    dve.memset(pad[:, :, PAD0 + D:KW], 0.0).then_inc(sem("pads"), 1)
                dve.memset(mx0[:, :], -3.0e38).then_inc(sem("max_l0"), 1)
                dve.wait_ge(sem("b0_in"), 16)

                def v_out(t):
                    dve.wait_ge(sem("l0_mm"), 2 * t + 2)
                    dve.tensor_scalar(V0[:, t, PAD0:PAD0 + D], ps[("q", "kv", "s", "qT", "kT", "pT")[(2 * t + 1) % 6]][:, :],
                                      b0[:, 2:3], None, ALU.add).then_inc(sem("v_ev"), 1)

                def norm_x(t):
                    dve.wait_ge(sem("ln_shift"), t // 4 + 1)
                    if t >= 2:
                        dve.wait_ge(sem("l0_mm"), 2 * T + t - 1)
                    dve.tensor_scalar(xn[t % 2][:, :], X[:, t, :], mv[:, t, 0:1], rstd[:, t:t + 1],
                                      ALU.subtract, ALU.mult).then_inc(sem("ln_xn"), 1)

                for t in range(T):
                    if t < 4:
                        v_out(t)
                    dve.wait_ge(sem(f"x_in{t // 2}"), 16)
                    stats(t)
                    if t == 3:
                        mean_var(0, 0)
                    elif t == 5:
                        v_out(4)
                        v_out(5)
                        norm_x(0)
                        norm_x(1)
                    elif t == 7:
                        mean_var(0, 1)
                        v_out(6)
                        v_out(7)
                for t in range(2, T):
                    norm_x(t)
                dve.wait_ge(sem("pads"), 2)
                dve.wait_ge(sem("l0_ev"), 2 * T)

                def running_max(w):
                    dve.wait_ge(sem("dots_ev"), w + 3)
                    dve.wait_ge(sem("max_l0"), w + 1)
                    dve.tensor_tensor(mx0[:, :], mx0[:, :], row(dots, w + 1), ALU.max).then_inc(sem("max_l0"), 1)

                def products(w, m):
                    dve.wait_ge(sem("even_mm"), w * (T // 2) + (m + 1))
                    dve.wait_ge(sem("prod_lo"), w * (T // 2) + (m + 1))
                    tt = slice(2 * m, 2 * m + 2)
                    dve.tensor_tensor(pair_of[m][:, :, :], q0[:, tt, :], K0[:, tt, bass.ds(w, D)],
                                      ALU.mult).then_inc(sem("prod"), 1)

                for w in range(2):
                    for m in range(T // 2):
                        products(w, m)
                with dve.Fori(1, W0 // 2) as i:
                    for h in range(2):
                        for m in range(T // 2):
                            products(i * 2 + h, m)
                            if m == 0:
                                running_max(i * 2 + (h - 2))
                running_max(W0 - 2)
                dve.wait_ge(sem("dots_ev"), W0 + 2)
                dve.wait_ge(sem("max_l0"), W0)
                dve.tensor_tensor(mx0[:, :], mx0[:, :], dots[:, W0, :], ALU.max).then_inc(sem("max_l0"), 1)
                dve.wait_ge(sem("max_l0"), W0 + 1)
                for w in range(0, W0, 2):
                    sub(dots[:, w + 1:w + 3, :], dots[:, w + 1:w + 3, :],
                        mx0[:, :].unsqueeze(1).to_broadcast([P, 2, D])).then_inc(sem("e_sub"), 2)
                for w in range(1, W0, 2):
                    dve.wait_ge(sem("e_hi"), w + 1)
                    sub(el[:, w, :], dots[:, w + 1, :], eh[:, w, :].bitcast(F32)).then_inc(sem("e_lo_odd"), 1)
                banks = ("q", "kv", "qT", "kT")

                def weighted(t, u):
                    j = t * W0 + u
                    dve.wait_ge(sem("spread_mm"), j + (1 + 2 * W0))
                    dve.wait_ge(sem("pair"), t * (W0 // 2) + (u // 2 + 1))
                    dve.tensor_tensor(pv_prod[u % 8][:, :], ps[banks[u % 4]][:, :],
                                      V0[:, bass.ds(t, 1), u:u + D].rearrange("p a b -> p (a b)"), ALU.mult)\
                        .then_inc(sem("pv"), 1)

                def over_sum(t, h):
                    dve.wait_ge(sem("windowsum_mm"), t * SUMS + (SUMS + 3))
                    dve.wait_ge(sem("rspread_ev"), t + 2)
                    dve.wait_ge(sem("y_l0"), t + 1)
                    dve.tensor_tensor(o0[:, :], ps[("s", "pT")[h]][:, :], rspread[h][:, :], ALU.mult)\
                        .then_inc(sem("o_l0"), 1)

                def x_update(t):
                    dve.wait_ge(sem("y_l0"), t + 2)
                    dve.scalar_tensor_tensor(row(X, t), ps["oT"][:, :], b0[:, 3:4], row(X, t), ALU.add, ALU.add)\
                        .then_inc(sem("x_l0"), 1)

                def stats_l0(t):
                    dve.wait_ge(sem("x_l0"), t + 2)
                    dve.bn_stats(row(st, t), row(X, t)).then_inc(sem("ln_st"), 1)

                def tile(t, h, first=False):
                    for u in range(W0):
                        weighted(t, u)
                        if u == 7 and not first:
                            over_sum(t - 1, 1 - h)
                        elif u == 12 and not first:
                            x_update(t - 1)
                        elif u == 14 and not first:
                            stats_l0(t - 1)
                        elif u == 6 and first:
                            dve.wait_ge(sem("e_sum"), 1)
                            dve.reciprocal(rec[:, :], ps["oT"][:, :]).then_inc(sem("rec"), 1)
                            dve.wait_ge(sem("rec_hi"), 1)
                            sub(recl[:, :], rec[:, :], rech[:, :].bitcast(F32)).then_inc(sem("rec_lo"), 1)

                tile(0, 0, first=True)
                tile(1, 1)
                with dve.Fori(1, T // 4 + 1) as i:
                    for h in range(2):
                        tile(i * 2 + h, h)
                mean_var(1, 0)
                with dve.Fori(T // 4 + 1, T // 2) as i:
                    for h in range(2):
                        tile(i * 2 + h, h)
                dve.wait_ge(sem("pv"), T * W0 + 4)
                dve.wait_ge(sem("quad"), 2 * T - 1)
                dve.tensor_tensor(psumd[3][:, :], pv_prod[6][:, :], pv_prod[7][:, :], ALU.add).then_inc(sem("last_pair"), 1)
                over_sum(T - 1, 1)
                norm_lo(1, 0)
                norm_lo(1, 1)
                x_update(T - 1)
                stats_l0(T - 1)
                mean_var(1, 1)

            def gating(f, index, h, meanwhile=lambda: None):
                e = f.e
                tt = slice(4 * h, 4 * h + 4)
                dve.wait_ge(sem("lr_ev"), index * T + 4 * h + 4)
                if index == 0:
                    dve.wait_ge(sem("small_in"), SMALL)
                logits = lr[:, tt, f.er:f.er + e]
                over_e = lambda v: v[:, tt].unsqueeze(2).to_broadcast([P, 4, e])
                zv, ev, wv, gv = z[:, tt, 0:e], z2[:, tt, 0:e], z3[:, tt, 0:e], gates[:, tt, 0:e]
                pv, qv = pair[:, tt, 0:e, 0:e], pair2[:, tt, :, :]
                r1, s1, t1 = zr[:, tt], zs[:, tt], zt[:, tt]
                as_j = lambda v: v.unsqueeze(2).to_broadcast([P, 4, e, e])
                as_e = lambda v: v.unsqueeze(3).to_broadcast([P, 4, e, e])
                if index != 1:
                    link(dve.tensor_tensor(zv, logits, rb[index // 2][:, 0:e].unsqueeze(1).to_broadcast([P, 4, e]), ALU.add))
                if index == 0:
                    link(dve.tensor_reduce(r1, zv, AX.X, ALU.max))
                    sub(zv, zv, over_e(zr)).then_inc(sem("gate_in"), 1)
                    meanwhile()
                    dve.wait_ge(sem("gate_exp"), h + 1)
                    link(dve.tensor_reduce(s1, ev, AX.X, ALU.add))
                    link(dve.reciprocal(t1, s1))
                    link(dve.scalar_tensor_tensor(gv, ev, e * 32.0 / 16.0, over_e(zt), ALU.mult, ALU.mult))
                elif index == 1:
                    link(dve.tensor_reduce(r1, logits, AX.X, ALU.max))
                    sub(zv, logits, over_e(zr)).then_inc(sem("gate_in"), 1)
                    dve.tensor_tensor(pv, as_j(logits), as_e(logits), ALU.is_gt)
                    link(dve.tensor_tensor(qv, as_j(logits), as_e(logits), ALU.is_equal))
                    link(dve.tensor_tensor(qv, qv,
                                           tri[:, :].rearrange("p (a b) -> p a b", a=e).unsqueeze(1).to_broadcast([P, 4, e, e]),
                                           ALU.mult))
                    link(dve.tensor_tensor(pv, pv, qv, ALU.add))
                    link(dve.tensor_reduce(wv, pv, AX.X, ALU.add))
                    meanwhile()
                    dve.wait_ge(sem("gate_exp"), 2 + h + 1)
                    link(dve.scalar_tensor_tensor(ev, wv, 1.5, ev, ALU.is_lt, ALU.mult))
                    link(dve.tensor_reduce(s1, ev, AX.X, ALU.add))
                    link(dve.reciprocal(t1, s1))
                    link(dve.scalar_tensor_tensor(gv, ev, 4.0, over_e(zt), ALU.mult, ALU.mult))
                else:
                    link(dve.tensor_tensor(pv, as_j(zv), as_e(zv), ALU.subtract))
                    link(dve.tensor_scalar(pv, pv, 0.0, None, ALU.max))
                    meanwhile()
                    link(dve.tensor_reduce(wv, pv, AX.X, ALU.add))
                    link(dve.tensor_scalar(wv, wv, 1.0, None, ALU.is_lt))
                    dve.tensor_reduce(r1, wv, AX.X, ALU.add)
                    link(dve.tensor_tensor(ev, wv, zv, ALU.mult))
                    link(dve.tensor_reduce(s1, ev, AX.X, ALU.add))
                    link(dve.reciprocal(t1, r1))
                    link(dve.scalar_tensor_tensor(s1, s1, -1.0, t1, ALU.add, ALU.mult))
                    link(dve.tensor_tensor(ev, zv, over_e(zs), ALU.subtract))
                    link(dve.tensor_scalar(gv, ev, 0.0, None, ALU.max))
                dve.tensor_tensor(gated[:, tt, 0:f.er].rearrange("p t (e r) -> p t e r", e=e),
                                  lr[:, tt, 0:f.er].rearrange("p t (e r) -> p t e r", e=e),
                                  gv.unsqueeze(3).to_broadcast([P, 4, e, f.r]), ALU.mult).then_inc(sem("gated"), 1)

            def dense_add(n_dense, tiles):
                for t in tiles:
                    dve.wait_ge(sem("dense_mm"), n_dense + t + 1)
                    dve.wait_ge(sem("bias_add"), n_dense + t + 1)
                    dve.tensor_tensor(X[:, t, :], X[:, t, :], dense_bank(t)[:, :], ALU.add)\
                        .then_inc(sem("dense_add"), 1)

            def experts(f, phase):
                index = (phase - 1) // 2
                dense = (lambda *tiles: dense_add(0, tiles)) if f.dense else (lambda *tiles: None)

                def x_update(t):
                    dve.wait_ge(sem("ff_mm"), index * T + t + 1)
                    dve.tensor_tensor(X[:, t, :], X[:, t, :], ps[("oT", "y", "q", "kv")[t % 4]][:, :], ALU.add)\
                        .then_inc(sem("x_ff"), 1)

                def x_stats(t):
                    dve.wait_ge(sem("x_ff"), index * T + t + 1)
                    stats(t)

                def first_two():
                    x_update(0)
                    x_update(1)

                def lo_4_and_5():
                    norm_lo(phase, 4)
                    norm_lo(phase, 5)

                gating(f, index, 0, lo_4_and_5)
                dense(0, 1, 2, 3)
                norm_lo(phase, 6)
                norm_lo(phase, 7)
                dense(4, 5)
                if f.dense:
                    gating(f, index, 1)
                    dense(6, 7)
                    dve.wait_ge(sem("dense_add"), T)
                    first_two()
                else:
                    gating(f, index, 1, first_two)
                x_update(2)
                x_stats(0)
                x_update(3)
                x_stats(1)
                x_stats(2)
                x_stats(3)
                mean_var(phase + 1, 0)
                x_update(4)
                x_update(5)
                x_stats(4)
                x_update(6)
                x_stats(5)
                x_update(7)
                x_stats(6)
                x_stats(7)
                mean_var(phase + 1, 1)
                for t in range(4):
                    norm_lo(phase + 1, t)

            def attention(l, norm_w, phase, dequantise=None):
                d, keys = l.d, l.keys
                nq = HG + l.tiles

                def v_rest(n, v):
                    dve.wait_ge(sem("v_hi"), n + 1)
                    kv = ps["kv"][:, 0:l.tiles * 2 * d].rearrange("p (j c) -> p j c", j=l.tiles)
                    sub(vl[v][:, 0:l.tiles * d].rearrange("p (j c) -> p j c", j=l.tiles), kv[:, :, d:2 * d],
                        vh[v][:, 0:l.tiles * d].rearrange("p (j c) -> p j c", j=l.tiles).bitcast(F32))\
                        .then_inc(sem("v_lo"), 1)

                def sum_squares(n):
                    if l.norm_eps is None:
                        return
                    m = n - NORM0
                    dve.wait_ge(sem("squared"), m + 1)
                    dve.tensor_reduce(ss[:, 0:nq], sq[:, 0:nq * d].rearrange("p (h c) -> p h c", h=nq), AX.X, ALU.add)\
                        .then_inc(sem("sumsq"), 1)
                    dve.wait_ge(sem("sumsq"), m + 1)
                    dve.wait_ge(sem("rnorm"), m)
                    dve.tensor_scalar(ms[:, 0:nq], ss[:, 0:nq], 1.0 / d, l.norm_eps, ALU.mult, ALU.add)\
                        .then_inc(sem("meansq"), 1)

                def hats(n, p):
                    dve.wait_ge(sem("kv_mm"), n + 1)
                    dve.wait_ge(sem("q_mm"), n + 1)
                    dve.wait_ge(sem("qkT_mm"), n - 1)
                    kv = ps["kv"][:, 0:l.tiles * 2 * d].rearrange("p (j c) -> p j c", j=l.tiles)[:, :, 0:d]
                    k_out = qkh[p][:, HG * d:nq * d].rearrange("p (j c) -> p j c", j=l.tiles)
                    if l.norm_eps is None:
                        dve.tensor_copy(k_out, kv).then_inc(sem("hat_k"), 1)
                        dve.tensor_copy(qkh[p][:, 0:HG * d], ps["q"][:, 0:HG * d]).then_inc(sem("hat"), 1)
                    else:
                        dve.wait_ge(sem("rnorm"), n - NORM0 + 1)
                        dve.tensor_tensor(k_out, kv, rs[:, HG:nq].unsqueeze(2).to_broadcast([P, l.tiles, d]), ALU.mult)\
                            .then_inc(sem("hat_k"), 1)
                        dve.tensor_tensor(qkh[p][:, 0:HG * d].rearrange("p (h c) -> p h c", h=HG),
                                          ps["q"][:, 0:HG * d].rearrange("p (h c) -> p h c", h=HG),
                                          rs[:, 0:HG].unsqueeze(2).to_broadcast([P, HG, d]), ALU.mult)\
                            .then_inc(sem("hat"), 1)

                def kT_out(n):
                    dve.wait_ge(sem("qkT_mm"), n + 1)
                    dve.wait_ge(sem("s_mm"), n)
                    src = ps["kT"][0:d, 0:l.tiles * P]
                    if norm_w is None:
                        dve.tensor_copy(kT[0:d, 0:l.tiles * P], src).then_inc(sem("kT_ev"), 1)
                    else:
                        dve.tensor_scalar(kT[0:d, 0:l.tiles * P], src, norm_w, None, ALU.mult).then_inc(sem("kT_ev"), 1)

                s3 = sc[:, 0:4 * keys].rearrange("p (g k) -> p g k", g=4)
                p3 = ps["s"][:, 0:4 * keys].rearrange("p (g k) -> p g k", g=4)
                over_k = lambda v: v[:, :].unsqueeze(2).to_broadcast([P, 4, keys])

                def score_rest(n):
                    dve.wait_ge(sem("s_mm"), n + 1)
                    dve.wait_ge(sem("pT_mm"), n)
                    if l.masked:
                        dve.scalar_tensor_tensor(s3, p3, l.scale, mask[:, :].unsqueeze(1).to_broadcast([P, 4, keys]),
                                                 ALU.mult, ALU.add).then_inc(sem("masked"), 1)
                        dve.wait_ge(sem("masked"), n - l.n0 + 1)
                        src = s3
                    else:
                        src = p3
                    dve.tensor_reduce(smx[:, :], src, AX.X, ALU.max).then_inc(sem("smax"), 1)
                    dve.wait_ge(sem("smax"), n + 1)
                    sub(s3, src, over_k(smx)).then_inc(sem("ssub"), 1)

                def probs(n):
                    dve.wait_ge(sem("exp"), n + 1)
                    dve.tensor_reduce(ssum[:, :], s3, AX.X, ALU.add).then_inc(sem("ssum"), 1)
                    dve.wait_ge(sem("ssum"), n + 1)
                    dve.reciprocal(srec[:, :], ssum[:, :]).then_inc(sem("srec"), 1)
                    dve.wait_ge(sem("srec"), n + 1)
                    dve.tensor_tensor(s3, s3, over_k(srec), ALU.mult).then_inc(sem("prob"), 1)

                def pT_rest(n):
                    dve.wait_ge(sem("pT_hi"), n + 1)
                    if l.tiles == 2:
                        sub(pTl[:, :], ps["pT"][:, :], pTh[:, :].bitcast(F32)).then_inc(sem("pT_lo"), 1)
                    else:
                        for b in range(NB):
                            c = slice(b * 2 * P, (b + 1) * 2 * P)
                            r = slice(b * S, (b + 1) * S)
                            last = sub(pTl[r, c], ps["pT"][r, 0:2 * P], pTh[r, c].bitcast(F32))
                        last.then_inc(sem("pT_lo"), 1)

                by_head = lambda v: v[0:d, :].rearrange("p (h b q) -> p b h q", h=HG, b=NB)
                from_batch = lambda v: v[0:d, :].rearrange("p (b h q) -> p b h q", b=NB, h=HG)

                def oT_rest(n):
                    dve.wait_ge(sem("oT_hi"), n + 1)
                    sub(by_head(oTl), from_batch(ps["oT"]), by_head(oTh).bitcast(F32)).then_inc(sem("oT_lo"), 1)

                def x_update(n, t):
                    dve.wait_ge(sem("y_mm"), n + 1)
                    dve.tensor_tensor(X[:, t, :], X[:, t, :], ps["y"][:, :], ALU.add).then_inc(sem("x_add"), 1)

                n0 = l.n0
                if l.tiles == 1:
                    for v in (pTh, pTl):
                        for b in range(NB):
                            dve.memset(v[b * S:(b + 1) * S, (1 - b) * 2 * P:(2 - b) * 2 * P].bitcast(F32), 0.0)
                for k in range(2):
                    v_rest(n0 + k, k)
                    sum_squares(n0 + k)
                    if k == 0:
                        norm_lo(phase, 4)
                        norm_lo(phase, 5)
                    hats(n0 + k, k)
                    if k == 0:
                        norm_lo(phase, 6)
                        norm_lo(phase, 7)
                        kT_out(n0)
                last_i = l.groups // 2 - 1
                with dve.Fori(0, l.groups // 2) as i:
                    for s in range(2 * T):
                        n = i * (2 * T) + (n0 + s)
                        score_rest(n)
                        if s == 0:
                            with dve.If(i > 0):
                                oT_rest(n - 1)
                        else:
                            oT_rest(n - 1)
                        probs(n)

                        def full_step():
                            v_rest(n + 2, (s + 2) % 4)
                            sum_squares(n + 2)
                            kT_out(n + 1)
                            pT_rest(n)
                            hats(n + 2, s % 2)
                            if s == 0:
                                with dve.If(i > 0):
                                    x_update(n - 1, T - 1)
                            else:
                                x_update(n - 1, (s - 1) % T)

                        def x_stats():
                            dve.wait_ge(sem("x_add"), n0 + (l.groups - 2) * T + s)
                            stats(s - 1 - T)

                        if s < 2 * T - 2:
                            full_step()
                            if s > T:
                                with dve.If(i > last_i - 1):
                                    x_stats()
                                    if s == 2 * T - 4:
                                        mean_var(phase + 1, 0)
                                    if dequantise and T + 2 <= s < T + 5:
                                        dequantise(2 * (s - T - 2))
                                        dequantise(2 * (s - T - 2) + 1)
                            continue
                        with dve.If(i < last_i):
                            full_step()
                        with dve.If(i > last_i - 1):
                            if s == 2 * T - 2:
                                kT_out(n + 1)
                            else:
                                norm_lo(phase + 1, 0)
                                norm_lo(phase + 1, 1)
                            x_update(n - 1, s - 1 - T)
                            x_stats()
                            pT_rest(n)
                            if s == 2 * T - 1:
                                norm_lo(phase + 1, 2)
                                norm_lo(phase + 1, 3)
                oT_rest(l.end - 1)
                if dequantise:
                    for k in range(KD):
                        dequantised_lo(k)
                x_update(l.end - 1, T - 1)
                dve.wait_ge(sem("x_add"), l.end)
                stats(T - 1)
                mean_var(phase + 1, 1)

            def dequantised_lo(k):
                dve.wait_ge(sem("wdq_hi"), k + 1)
                sub(WQl[1][:, k, 0:D], ps[("qT", "kT", "s", "pT")[k]][:, :], WQh[1][:, k, 0:D].bitcast(F32))\
                    .then_inc(sem("wdq_lo"), 1)

            def dequantise(step):
                shape = [P, 4, 8, 32]
                if step == 0:
                    dve.wait_ge(sem("pk_in"), 16)
                    dve.tensor_scalar(low4[:, :, :], packed[:, :, :], 15, None, ALU.bitwise_and).then_inc(sem("nibbles"), 1)
                elif step == 1:
                    dve.tensor_scalar(packed[:, :, :], packed[:, :, :], 4, 15, ALU.logical_shift_right, ALU.bitwise_and)\
                        .then_inc(sem("nibbles"), 1)
                elif step < 4:
                    nib = (low4, packed)[step - 2]
                    dve.wait_ge(sem("nibbles"), step - 1)
                    dve.tensor_tensor(wdq[:, :, :, :, step - 2], nib[:, :, :].rearrange("p t (g c) -> p t g c", g=8),
                                      wsc[:, :, :].unsqueeze(3).to_broadcast(shape), ALU.mult).then_inc(sem("wdq_mul"), 1)
                else:
                    dve.wait_ge(sem("wdq_mul"), step - 3)
                    w = wdq[:, :, :, :, step - 4]
                    dve.tensor_tensor(w, w, wze[:, :, :].unsqueeze(3).to_broadcast(shape), ALU.add).then_inc(sem("wdq"), 1)

            windowed_attention()
            for t in range(2, 4):
                norm_lo(1, t)
            experts(F0, 1)
            attention(L1, None, 2)
            experts(F1, 3)
            for j in range(2):
                dve.tensor_tensor(kw[:, j:j + 1], knorm[:, 2 * j:2 * j + 1], knorm[:, 2 * j + 1:2 * j + 2], ALU.mult)\
                    .then_inc(sem("kw"), 1)
            dve.wait_ge(sem("kw"), 2)
            attention(L2, kw[:, 0:1], 4)
            experts(F2, 5)
            attention(L3, kw[:, 1:2], 6, dequantise)
            dense_add(T, (0, 1))
            norm_lo(7, 4)
            norm_lo(7, 5)
            dense_add(T, (2, 3))
            norm_lo(7, 6)
            norm_lo(7, 7)
            dense_add(T, range(4, T))


def kernel(**inputs):
    import concourse.bacc as bacc
    from concourse.bass_utils import run_bass_kernel_spmd

    v = {k: np.asarray(x) for k, x in inputs.items()}
    f32 = np.float32

    def pair_rows(w):
        out = np.zeros((P, P), w.dtype)
        out[:S, :S] = w.T
        out[S:, S:] = w.T
        return out

    def group_qkv(wq, wk, wv, groups, d):
        q = wq.reshape(KD, P, groups, HG * d).transpose(2, 0, 1, 3)
        k = wk.reshape(KD, P, groups, d).transpose(2, 0, 1, 3)
        w = wv.reshape(KD, P, groups, d).transpose(2, 0, 1, 3)
        return np.ascontiguousarray(np.concatenate([q, k, w], -1))

    def group_out(wo, groups, d):
        return np.ascontiguousarray(wo.reshape(groups, 2, 2, d, D).transpose(0, 1, 3, 2, 4).reshape(groups, 2, d, 2 * D))

    def rows(w):
        return np.ascontiguousarray(w.T.reshape(KD, P, -1))

    ranks = lambda w: w.reshape(-1, D)
    c = np.arange(P)
    head = np.zeros((P, T, P), f32)
    for t in range(T):
        head[c, t, t * 16 + c // 8] = 1.0
    arrays = {
        "x": v["x"].reshape(B * S, D),
        "ctx": v["ctx_4096"].reshape(B * S, D),
        "ctxT": np.ascontiguousarray(v["ctx_4096"].reshape(B * S, D).T.reshape(KD, P, B * S)),
        "mask": v["mask_1x1xSxS2_ff0"].reshape(S, S),
        "ident": np.eye(P, dtype=f32),
        "tri": np.tril(np.ones((4, 4), f32), -1).reshape(16),
        "head_sum": head,
        "head_spread": np.ascontiguousarray(head.transpose(2, 1, 0)),
        "w0": np.ascontiguousarray(np.stack([pair_rows(v["L0_xattn_W" + n]) for n in "qkvo"], 1)),
        "b0": np.ascontiguousarray(np.stack([np.tile(v["L0_xattn_b" + n], 2) for n in "qkvo"], 1)),
        "knorm": np.ascontiguousarray(np.stack([v["L2_xattn_q_norm_w"], v["L2_xattn_k_norm_w"],
                                                v["L3_xattn_q_norm_w"], v["L3_xattn_k_norm_w"]], 1)),
        "f0_ar": rows(np.concatenate([ranks(v["L0_ffn_A"]), v["L0_ffn_Wr"]], 0)),
        "f0_b": np.ascontiguousarray(v["L0_ffn_B"].transpose(0, 2, 1).reshape(P, D)),
        "f0_rb": v["L0_ffn_br"],
        "f1_ar": rows(np.concatenate([ranks(v["L1_ffn_A"]), v["L1_ffn_Wr"]], 0)),
        "f1_b": np.ascontiguousarray(v["L1_ffn_B"].transpose(0, 2, 1).reshape(64, D)),
        "f2_ar": rows(np.concatenate([v["L2_ffn_W_base"], ranks(v["L2_ffn_lora_A"].transpose(0, 2, 1)),
                                      v["L2_ffn_W_router"]], 0)),
        "f2_b": v["L2_ffn_lora_B"].reshape(P, D),
        "f2_rb": v["L2_ffn_b_router"],
        "f2_bias": v["L2_ffn_b_base"],
        "l1_qkv": group_qkv(v["L1_xattn_Wq"].T, v["L1_xattn_Wk"].T, v["L1_xattn_Wv"].T, 4, 96),
        "l1_o": group_out(v["L1_xattn_Wo"].T, 4, 96),
        "l2_qkv": group_qkv(v["L2_xattn_q_proj_w"].T, v["L2_xattn_k_proj_w"].T, v["L2_xattn_v_proj_w"].T, 8, 128),
        "l2_o": group_out(v["L2_xattn_o_proj_w"].T, 8, 128),
        "l3_qkv": group_qkv(v["L3_xattn_Wq"], v["L3_xattn_Wk"], v["L3_xattn_Wv"], 8, 128),
        "l3_o": group_out(v["L3_xattn_Wo"], 8, 128),
        "packed": v["L3_ffn_weight_packed"].reshape(D, 256),
        "scales": v["L3_ffn_weight_scales"].reshape(D, 8),
        "zeros": v["L3_ffn_weight_zeros"].reshape(D, 8),
        "f3_bias": v["L3_ffn_bias"],
    }
    nc = bacc.Bacc("TRN2", target_bir_lowering=False, num_devices=1)
    feeds, aps = {}, {}
    for name, x in arrays.items():
        x = np.ascontiguousarray(x)
        feeds["in_" + name] = x
        aps[name] = nc.dram_tensor("in_" + name, x.shape, mybir.dt.from_np(x.dtype), kind="ExternalInput").ap()
    aps["out"] = nc.dram_tensor("out_x", (B * S, D), F32, kind="ExternalOutput").ap()
    build(nc, aps)
    r = run_bass_kernel_spmd(nc, [feeds], core_ids=[0])
    return r.results[0]["out_x"].reshape(B, S, D)
```
